# Optimizing a Trainium2 kernel written in Bass

```python
import numpy as np
import jax
import jax.numpy as jnp

def _softmax(x, axis=-1):
    return jax.nn.softmax(x, axis=axis)

def _gelu(x):
    return jax.nn.gelu(x, approximate=True)

def _silu(x):
    return jax.nn.silu(x)

def _sigmoid(x):
    return jax.nn.sigmoid(x)

def _layernorm(x, axis=-1, eps=1e-05):
    m = jnp.mean(x, axis=axis, keepdims=True)
    v = jnp.var(x, axis=axis, keepdims=True)
    return (x - m) / jnp.sqrt(v + eps)

def _scatter_add(tgt, idx, src, axis=0):
    return tgt.at[idx].add(src)

def _segment_sum(src, seg, n):
    return jax.ops.segment_sum(src, seg, n)
kernel_name = 'mk_conv_preact_d4_conv_nchw512_r2_edd2a7'

def setup_inputs(seed: int=0):
    np.random.seed(seed)
    _w = jnp.asarray

    def _rec_inputs():
        import jax
        import jax.numpy as jnp
        _gk = jax.random.key(seed)
        x = -0.0002928 + 1 * jax.random.normal(jax.random.fold_in(_gk, 1), (8, 256, 32, 32), jnp.float32)
        return x
    x = _rec_inputs()

    def _L0_conv_setup():
        import jax, jax.numpy as jnp
        from jax import lax
        import numpy as np
        D_IN = 256
        HID = 64
        D_INNER = 2 * HID
        D_PROJ = 2 * D_INNER
        N_STATE = 16
        R_DT = 8
        B, H, W = (8, 32, 32)

        def _layernorm(y, g, b):
            mu = y.mean(-1, keepdims=True)
            var = ((y - mu) ** 2).mean(-1, keepdims=True)
            return (y - mu) / jnp.sqrt(var + 1e-05) * g + b

        def _ssm(x, xw, dtw, dtb, Al, Dv, g, be):
            Bb, D, L = x.shape
            n = Al.shape[1]
            xd = jnp.einsum('bdl,kd->blk', x, xw)
            dts = xd[..., :R_DT]
            Bs = xd[..., R_DT:R_DT + n]
            Cs = xd[..., R_DT + n:]
            delta = jax.nn.softplus(jnp.einsum('blr,dr->bld', dts, dtw) + dtb)
            A = -jnp.exp(Al)
            xt = x.transpose(0, 2, 1)
            dA = jnp.exp(delta[..., None] * A)
            dBx = delta[..., None] * Bs[:, :, None, :] * xt[..., None]

            def step(h, inp):
                da, dbx, c = inp
                h = h * da + dbx
                return (h, jnp.einsum('bdn,bn->bd', h, c))
            h0 = jnp.zeros((Bb, D, n), x.dtype)
            _, ys = lax.scan(step, h0, (dA.transpose(1, 0, 2, 3), dBx.transpose(1, 0, 2, 3), Cs.transpose(1, 0, 2)))
            y = ys.transpose(1, 0, 2) + xt * Dv
            return _layernorm(y, g, be)

        def _up2(y, h, w):
            Bb, L, C = y.shape
            img = y.transpose(0, 2, 1).reshape(Bb, C, h, w)
            img = jnp.repeat(jnp.repeat(img, 2, axis=2), 2, axis=3)
            return img.reshape(Bb, C, 4 * L).transpose(0, 2, 1)

        def _conv1x1(x, w, b):
            return jnp.einsum('bchw,oc->bohw', x, w) + b[None, :, None, None]

        def _conv2s2(x, w, b):
            out = lax.conv_general_dilated(x, w, (2, 2), 'VALID', dimension_numbers=('NCHW', 'OIHW', 'NCHW'))
            return out + b[None, :, None, None]

        def _forward(input_f, in_w, in_b, c1_w, c1_b, c2_w, c2_b, c3_w, c3_b, out_w, out_b, xw1, dtw1, dtb1, Al1, Dv1, g1, be1, xw2, dtw2, dtb2, Al2, Dv2, g2, be2, xw3, dtw3, dtb3, Al3, Dv3, g3, be3):
            xz = _conv1x1(input_f, in_w, in_b)
            x, z = jnp.split(xz, 2, axis=1)
            f1 = _conv1x1(x, c1_w, c1_b)
            f2 = _conv2s2(f1, c2_w, c2_b)
            f3 = _conv2s2(f2, c3_w, c3_b)
            Bb, C, h3, w3 = f3.shape
            fx3 = f3.reshape(Bb, C, h3 * w3)
            y3 = _ssm(fx3, xw3, dtw3, dtb3, Al3, Dv3, g3, be3) + jnp.flip(_ssm(jnp.flip(fx3, -1), xw3, dtw3, dtb3, Al3, Dv3, g3, be3), 1)
            y2_ = _up2(y3, h3, w3)
            _, _, h2, w2 = f2.shape
            fx2 = f2.reshape(Bb, C, h2 * w2)
            y2 = _ssm(fx2, xw2, dtw2, dtb2, Al2, Dv2, g2, be2) + jnp.flip(_ssm(jnp.flip(fx2, -1), xw2, dtw2, dtb2, Al2, Dv2, g2, be2), 1) + y2_
            y1_ = _up2(y2, h2, w2)
            _, _, h1, w1 = f1.shape
            fx1 = f1.reshape(Bb, C, h1 * w1)
            y1 = _ssm(fx1, xw1, dtw1, dtb1, Al1, Dv1, g1, be1) + jnp.flip(_ssm(jnp.flip(fx1, -1), xw2, dtw2, dtb2, Al2, Dv2, g2, be2), 1) + y1_
            out1 = y1.transpose(0, 2, 1).reshape(Bb, C, h1, w1)
            out = out1 * jax.nn.silu(z)
            return _conv1x1(out, out_w, out_b)
        key = jax.random.key(seed)
        ks = iter(jax.random.split(key, 32))

        def nrm(shape, s=0.05):
            return jax.random.normal(next(ks), shape, dtype=jnp.float32) * s
        inp = {'input_f': jax.random.normal(next(ks), (B, D_IN, H, W), dtype=jnp.float32), 'in_w': nrm((D_PROJ, D_IN)), 'in_b': nrm((D_PROJ,)), 'c1_w': nrm((D_INNER, D_INNER)), 'c1_b': nrm((D_INNER,)), 'c2_w': nrm((D_INNER, D_INNER, 2, 2)), 'c2_b': nrm((D_INNER,)), 'c3_w': nrm((D_INNER, D_INNER, 2, 2)), 'c3_b': nrm((D_INNER,)), 'out_w': nrm((D_IN, D_INNER)), 'out_b': nrm((D_IN,))}
        Al = jnp.log(jnp.tile(jnp.arange(1, N_STATE + 1, dtype=jnp.float32), (D_INNER, 1)))
        for i in (1, 2, 3):
            inp[f'xw{i}'] = nrm((R_DT + 2 * N_STATE, D_INNER))
            inp[f'dtw{i}'] = nrm((D_INNER, R_DT), s=R_DT ** (-0.5))
            inp[f'dtb{i}'] = nrm((D_INNER,)) - 4.0
            inp[f'Al{i}'] = Al
            inp[f'Dv{i}'] = jnp.ones((D_INNER,), jnp.float32)
            inp[f'g{i}'] = jnp.ones((D_INNER,), jnp.float32)
            inp[f'be{i}'] = jnp.zeros((D_INNER,), jnp.float32)
        return inp
    _L0_conv_all = _L0_conv_setup()
    _L0_conv_in = {k: v for k, v in _L0_conv_all.items() if k in ('in_w', 'in_b', 'c1_w', 'c1_b', 'c2_w', 'c2_b', 'c3_w', 'c3_b', 'out_w', 'out_b', 'xw1', 'dtw1', 'dtb1', 'Al1', 'Dv1', 'g1', 'be1', 'xw2', 'dtw2', 'dtb2', 'Al2', 'Dv2', 'g2', 'be2', 'xw3', 'dtw3', 'dtb3', 'Al3', 'Dv3', 'g3', 'be3')}
    del _L0_conv_all

    def _L1_conv_setup():
        import jax, jax.numpy as jnp
        import numpy as np
        N_HEADS = 8
        EMB = 32
        key = jax.random.key(seed)
        k1, k2, k3, k4, k5 = jax.random.split(key, 5)
        b, c, h, w = (8, 256, 32, 32)
        scale_qkv = 1.0 / np.sqrt(c)
        scale_proj = 1.0 / np.sqrt(c)
        return {'x': jax.random.normal(k1, (b, c, h, w), dtype=jnp.float32), 'qkv_w': jax.random.normal(k2, (3 * c, c), dtype=jnp.float32) * scale_qkv, 'qkv_b': jax.random.normal(k3, (3 * c,), dtype=jnp.float32) * 0.01, 'proj_w': jax.random.normal(k4, (c, c), dtype=jnp.float32) * scale_proj, 'proj_b': jax.random.normal(k5, (c,), dtype=jnp.float32) * 0.01}
    _L1_conv_all = _L1_conv_setup()
    _L1_conv_in = {k: v for k, v in _L1_conv_all.items() if k in ('qkv_w', 'qkv_b', 'proj_w', 'proj_b')}
    del _L1_conv_all

    def _L2_conv_setup():
        import jax, jax.numpy as jnp
        import numpy as np
        EPS = 1e-05
        RATES = (1, 6, 12, 18)

        def _bn(x, g, b, m, v):
            inv = g / jnp.sqrt(v + EPS)
            return x * inv[None, :, None, None] + (b - m * inv)[None, :, None, None]
        key = jax.random.key(seed)
        ks = jax.random.split(key, 20)
        B, C, H, W = (8, 256, 48, 48)
        Cq = C // 4
        f32 = jnp.float32
        inp = {}
        inp['x'] = jax.random.normal(ks[0], (B, C, H, W), f32)
        inp['wdw'] = jax.random.normal(ks[1], (4, Cq, 1, 3, 3), f32) * 0.1
        inp['bdw'] = jax.random.normal(ks[2], (4, Cq), f32) * 0.01
        inp['gdw'] = jnp.ones((4, Cq), f32) + 0.1 * jax.random.normal(ks[3], (4, Cq), f32)
        inp['bedw'] = jax.random.normal(ks[4], (4, Cq), f32) * 0.01
        inp['mdw'] = jax.random.normal(ks[5], (4, Cq), f32) * 0.01
        inp['vdw'] = jax.random.uniform(ks[6], (4, Cq), f32, 0.5, 1.5)
        inp['ws'] = jax.random.normal(ks[7], (4, 4, 1, 1), f32) * 0.5
        inp['bs'] = jax.random.normal(ks[8], (4,), f32) * 0.01
        inp['gs'] = jnp.ones((4,), f32) + 0.1 * jax.random.normal(ks[9], (4,), f32)
        inp['bes'] = jax.random.normal(ks[10], (4,), f32) * 0.01
        inp['ms'] = jax.random.normal(ks[11], (4,), f32) * 0.01
        inp['vs'] = jax.random.uniform(ks[12], (4,), f32, 0.5, 1.5)
        inp['wo'] = jax.random.normal(ks[13], (C, C, 1, 1), f32) * (1.0 / np.sqrt(C))
        inp['bo'] = jax.random.normal(ks[14], (C,), f32) * 0.01
        inp['go'] = jnp.ones((C,), f32) + 0.1 * jax.random.normal(ks[15], (C,), f32)
        inp['beo'] = jax.random.normal(ks[16], (C,), f32) * 0.01
        inp['mo'] = jax.random.normal(ks[17], (C,), f32) * 0.01
        inp['vo'] = jax.random.uniform(ks[18], (C,), f32, 0.5, 1.5)
        return inp
    _L2_conv_all = _L2_conv_setup()
    _L2_conv_in = {k: v for k, v in _L2_conv_all.items() if k in ('wdw', 'bdw', 'gdw', 'bedw', 'mdw', 'vdw', 'ws', 'bs', 'gs', 'bes', 'ms', 'vs', 'wo', 'bo', 'go', 'beo', 'mo', 'vo')}
    del _L2_conv_all

    def _L3_conv_setup():
        import jax, jax.numpy as jnp
        import numpy as np
        HEADS = 8
        EPS = 1e-05

        def _layernorm(x, gamma, beta):
            mu = jnp.mean(x, axis=-1, keepdims=True)
            var = jnp.var(x, axis=-1, keepdims=True)
            return (x - mu) * jax.lax.rsqrt(var + EPS) * gamma + beta
        key = jax.random.key(seed)
        ks = jax.random.split(key, 4)
        dim = 256
        x = jax.random.normal(ks[0], (4, dim, 32, 32), dtype=jnp.float32)
        w_qkv = jax.random.normal(ks[1], (dim, 3 * dim), dtype=jnp.float32) * dim ** (-0.5)
        b_qkv = jnp.zeros((3 * dim,), jnp.float32)
        w_out = jax.random.normal(ks[2], (dim, dim), dtype=jnp.float32) * dim ** (-0.5)
        b_out = jnp.zeros((dim,), jnp.float32)
        gamma1 = jnp.ones((dim,), jnp.float32)
        beta1 = jnp.zeros((dim,), jnp.float32)
        gamma2 = jnp.ones((dim,), jnp.float32)
        beta2 = jnp.zeros((dim,), jnp.float32)
        return {'x': x, 'w_qkv': w_qkv, 'b_qkv': b_qkv, 'w_out': w_out, 'b_out': b_out, 'gamma1': gamma1, 'beta1': beta1, 'gamma2': gamma2, 'beta2': beta2}
    _L3_conv_all = _L3_conv_setup()
    _L3_conv_in = {k: v for k, v in _L3_conv_all.items() if k in ('w_qkv', 'b_qkv', 'w_out', 'b_out', 'gamma1', 'beta1', 'gamma2', 'beta2')}
    del _L3_conv_all
    return {'x': x, 'L0_conv_in_w': _L0_conv_in['in_w'], 'L0_conv_in_b': _L0_conv_in['in_b'], 'L0_conv_c1_w': _L0_conv_in['c1_w'], 'L0_conv_c1_b': _L0_conv_in['c1_b'], 'L0_conv_c2_w': _L0_conv_in['c2_w'], 'L0_conv_c2_b': _L0_conv_in['c2_b'], 'L0_conv_c3_w': _L0_conv_in['c3_w'], 'L0_conv_c3_b': _L0_conv_in['c3_b'], 'L0_conv_out_w': _L0_conv_in['out_w'], 'L0_conv_out_b': _L0_conv_in['out_b'], 'L0_conv_xw1': _L0_conv_in['xw1'], 'L0_conv_dtw1': _L0_conv_in['dtw1'], 'L0_conv_dtb1': _L0_conv_in['dtb1'], 'L0_conv_Al1': _L0_conv_in['Al1'], 'L0_conv_Dv1': _L0_conv_in['Dv1'], 'L0_conv_g1': _L0_conv_in['g1'], 'L0_conv_be1': _L0_conv_in['be1'], 'L0_conv_xw2': _L0_conv_in['xw2'], 'L0_conv_dtw2': _L0_conv_in['dtw2'], 'L0_conv_dtb2': _L0_conv_in['dtb2'], 'L0_conv_Al2': _L0_conv_in['Al2'], 'L0_conv_Dv2': _L0_conv_in['Dv2'], 'L0_conv_g2': _L0_conv_in['g2'], 'L0_conv_be2': _L0_conv_in['be2'], 'L0_conv_xw3': _L0_conv_in['xw3'], 'L0_conv_dtw3': _L0_conv_in['dtw3'], 'L0_conv_dtb3': _L0_conv_in['dtb3'], 'L0_conv_Al3': _L0_conv_in['Al3'], 'L0_conv_Dv3': _L0_conv_in['Dv3'], 'L0_conv_g3': _L0_conv_in['g3'], 'L0_conv_be3': _L0_conv_in['be3'], 'L1_conv_qkv_w': _L1_conv_in['qkv_w'], 'L1_conv_qkv_b': _L1_conv_in['qkv_b'], 'L1_conv_proj_w': _L1_conv_in['proj_w'], 'L1_conv_proj_b': _L1_conv_in['proj_b'], 'L2_conv_wdw': _L2_conv_in['wdw'], 'L2_conv_bdw': _L2_conv_in['bdw'], 'L2_conv_gdw': _L2_conv_in['gdw'], 'L2_conv_bedw': _L2_conv_in['bedw'], 'L2_conv_mdw': _L2_conv_in['mdw'], 'L2_conv_vdw': _L2_conv_in['vdw'], 'L2_conv_ws': _L2_conv_in['ws'], 'L2_conv_bs': _L2_conv_in['bs'], 'L2_conv_gs': _L2_conv_in['gs'], 'L2_conv_bes': _L2_conv_in['bes'], 'L2_conv_ms': _L2_conv_in['ms'], 'L2_conv_vs': _L2_conv_in['vs'], 'L2_conv_wo': _L2_conv_in['wo'], 'L2_conv_bo': _L2_conv_in['bo'], 'L2_conv_go': _L2_conv_in['go'], 'L2_conv_beo': _L2_conv_in['beo'], 'L2_conv_mo': _L2_conv_in['mo'], 'L2_conv_vo': _L2_conv_in['vo'], 'L3_conv_w_qkv': _L3_conv_in['w_qkv'], 'L3_conv_b_qkv': _L3_conv_in['b_qkv'], 'L3_conv_w_out': _L3_conv_in['w_out'], 'L3_conv_b_out': _L3_conv_in['b_out'], 'L3_conv_gamma1': _L3_conv_in['gamma1'], 'L3_conv_beta1': _L3_conv_in['beta1'], 'L3_conv_gamma2': _L3_conv_in['gamma2'], 'L3_conv_beta2': _L3_conv_in['beta2']}

def reference(x, L0_conv_in_w, L0_conv_in_b, L0_conv_c1_w, L0_conv_c1_b, L0_conv_c2_w, L0_conv_c2_b, L0_conv_c3_w, L0_conv_c3_b, L0_conv_out_w, L0_conv_out_b, L0_conv_xw1, L0_conv_dtw1, L0_conv_dtb1, L0_conv_Al1, L0_conv_Dv1, L0_conv_g1, L0_conv_be1, L0_conv_xw2, L0_conv_dtw2, L0_conv_dtb2, L0_conv_Al2, L0_conv_Dv2, L0_conv_g2, L0_conv_be2, L0_conv_xw3, L0_conv_dtw3, L0_conv_dtb3, L0_conv_Al3, L0_conv_Dv3, L0_conv_g3, L0_conv_be3, L1_conv_qkv_w, L1_conv_qkv_b, L1_conv_proj_w, L1_conv_proj_b, L2_conv_wdw, L2_conv_bdw, L2_conv_gdw, L2_conv_bedw, L2_conv_mdw, L2_conv_vdw, L2_conv_ws, L2_conv_bs, L2_conv_gs, L2_conv_bes, L2_conv_ms, L2_conv_vs, L2_conv_wo, L2_conv_bo, L2_conv_go, L2_conv_beo, L2_conv_mo, L2_conv_vo, L3_conv_w_qkv, L3_conv_b_qkv, L3_conv_w_out, L3_conv_b_out, L3_conv_gamma1, L3_conv_beta1, L3_conv_gamma2, L3_conv_beta2):
    import jax
    import jax.numpy as jnp

    def _L0_conv_ref(input_f, in_w, in_b, c1_w, c1_b, c2_w, c2_b, c3_w, c3_b, out_w, out_b, xw1, dtw1, dtb1, Al1, Dv1, g1, be1, xw2, dtw2, dtb2, Al2, Dv2, g2, be2, xw3, dtw3, dtb3, Al3, Dv3, g3, be3):
        import jax, jax.numpy as jnp
        from jax import lax
        import numpy as np
        D_IN = 256
        HID = 64
        D_INNER = 2 * HID
        D_PROJ = 2 * D_INNER
        N_STATE = 16
        R_DT = 8
        B, H, W = (8, 32, 32)

        def _layernorm(y, g, b):
            mu = y.mean(-1, keepdims=True)
            var = ((y - mu) ** 2).mean(-1, keepdims=True)
            return (y - mu) / jnp.sqrt(var + 1e-05) * g + b

        def _ssm(x, xw, dtw, dtb, Al, Dv, g, be):
            Bb, D, L = x.shape
            n = Al.shape[1]
            xd = jnp.einsum('bdl,kd->blk', x, xw)
            dts = xd[..., :R_DT]
            Bs = xd[..., R_DT:R_DT + n]
            Cs = xd[..., R_DT + n:]
            delta = jax.nn.softplus(jnp.einsum('blr,dr->bld', dts, dtw) + dtb)
            A = -jnp.exp(Al)
            xt = x.transpose(0, 2, 1)
            dA = jnp.exp(delta[..., None] * A)
            dBx = delta[..., None] * Bs[:, :, None, :] * xt[..., None]

            def step(h, inp):
                da, dbx, c = inp
                h = h * da + dbx
                return (h, jnp.einsum('bdn,bn->bd', h, c))
            h0 = jnp.zeros((Bb, D, n), x.dtype)
            _, ys = lax.scan(step, h0, (dA.transpose(1, 0, 2, 3), dBx.transpose(1, 0, 2, 3), Cs.transpose(1, 0, 2)))
            y = ys.transpose(1, 0, 2) + xt * Dv
            return _layernorm(y, g, be)

        def _up2(y, h, w):
            Bb, L, C = y.shape
            img = y.transpose(0, 2, 1).reshape(Bb, C, h, w)
            img = jnp.repeat(jnp.repeat(img, 2, axis=2), 2, axis=3)
            return img.reshape(Bb, C, 4 * L).transpose(0, 2, 1)

        def _conv1x1(x, w, b):
            return jnp.einsum('bchw,oc->bohw', x, w) + b[None, :, None, None]

        def _conv2s2(x, w, b):
            out = lax.conv_general_dilated(x, w, (2, 2), 'VALID', dimension_numbers=('NCHW', 'OIHW', 'NCHW'))
            return out + b[None, :, None, None]

        def _forward(input_f, in_w, in_b, c1_w, c1_b, c2_w, c2_b, c3_w, c3_b, out_w, out_b, xw1, dtw1, dtb1, Al1, Dv1, g1, be1, xw2, dtw2, dtb2, Al2, Dv2, g2, be2, xw3, dtw3, dtb3, Al3, Dv3, g3, be3):
            xz = _conv1x1(input_f, in_w, in_b)
            x, z = jnp.split(xz, 2, axis=1)
            f1 = _conv1x1(x, c1_w, c1_b)
            f2 = _conv2s2(f1, c2_w, c2_b)
            f3 = _conv2s2(f2, c3_w, c3_b)
            Bb, C, h3, w3 = f3.shape
            fx3 = f3.reshape(Bb, C, h3 * w3)
            y3 = _ssm(fx3, xw3, dtw3, dtb3, Al3, Dv3, g3, be3) + jnp.flip(_ssm(jnp.flip(fx3, -1), xw3, dtw3, dtb3, Al3, Dv3, g3, be3), 1)
            y2_ = _up2(y3, h3, w3)
            _, _, h2, w2 = f2.shape
            fx2 = f2.reshape(Bb, C, h2 * w2)
            y2 = _ssm(fx2, xw2, dtw2, dtb2, Al2, Dv2, g2, be2) + jnp.flip(_ssm(jnp.flip(fx2, -1), xw2, dtw2, dtb2, Al2, Dv2, g2, be2), 1) + y2_
            y1_ = _up2(y2, h2, w2)
            _, _, h1, w1 = f1.shape
            fx1 = f1.reshape(Bb, C, h1 * w1)
            y1 = _ssm(fx1, xw1, dtw1, dtb1, Al1, Dv1, g1, be1) + jnp.flip(_ssm(jnp.flip(fx1, -1), xw2, dtw2, dtb2, Al2, Dv2, g2, be2), 1) + y1_
            out1 = y1.transpose(0, 2, 1).reshape(Bb, C, h1, w1)
            out = out1 * jax.nn.silu(z)
            return _conv1x1(out, out_w, out_b)
        return _forward(input_f, in_w, in_b, c1_w, c1_b, c2_w, c2_b, c3_w, c3_b, out_w, out_b, xw1, dtw1, dtb1, Al1, Dv1, g1, be1, xw2, dtw2, dtb2, Al2, Dv2, g2, be2, xw3, dtw3, dtb3, Al3, Dv3, g3, be3)

    def _L1_conv_ref(x, qkv_w, qkv_b, proj_w, proj_b):
        import jax, jax.numpy as jnp
        import numpy as np
        N_HEADS = 8
        EMB = 32
        b, c, h, w = x.shape
        t = h * w
        xf = x.reshape(b, c, t)
        qkv = jnp.einsum('oc,bct->bot', qkv_w, xf) + qkv_b[None, :, None]
        qkv = qkv.transpose(0, 2, 1).reshape(b, t, 3, N_HEADS, EMB)
        q, k, v = (qkv[:, :, 0], qkv[:, :, 1], qkv[:, :, 2])
        scores = jnp.einsum('bthe,bThe->bhtT', q, k) / jnp.sqrt(jnp.float32(EMB))
        attn = jax.nn.softmax(scores, axis=-1)
        out = jnp.einsum('bhtT,bThe->bthe', attn, v)
        out = out.reshape(b, t, c).transpose(0, 2, 1)
        out = jnp.einsum('oc,bct->bot', proj_w, out) + proj_b[None, :, None]
        return out.reshape(b, c, h, w)

    def _L2_conv_ref(x, wdw, bdw, gdw, bedw, mdw, vdw, ws, bs, gs, bes, ms, vs, wo, bo, go, beo, mo, vo):
        import jax, jax.numpy as jnp
        import numpy as np
        EPS = 1e-05
        RATES = (1, 6, 12, 18)

        def _bn(x, g, b, m, v):
            inv = g / jnp.sqrt(v + EPS)
            return x * inv[None, :, None, None] + (b - m * inv)[None, :, None, None]
        B = x.shape[0]
        Cq = wdw.shape[1]
        xs = jnp.split(x, 4, axis=1)
        branches = []
        for i, r in enumerate(RATES):
            y = jax.lax.conv_general_dilated(xs[i], wdw[i], window_strides=(1, 1), padding=[(r, r), (r, r)], rhs_dilation=(r, r), dimension_numbers=('NCHW', 'OIHW', 'NCHW'), feature_group_count=Cq)
            y = y + bdw[i][None, :, None, None]
            y = jax.nn.relu(_bn(y, gdw[i], bedw[i], mdw[i], vdw[i]))
            branches.append(y)
        z = jnp.stack(branches, axis=2)
        W4 = ws[:, :, 0, 0]
        z = jnp.einsum('oi,bcihw->bcohw', W4, z) + bs[None, None, :, None, None]
        inv_s = gs / jnp.sqrt(vs + EPS)
        z = jax.nn.relu(z * inv_s[None, None, :, None, None] + (bes - ms * inv_s)[None, None, :, None, None])
        z = z.reshape(B, Cq * 4, z.shape[3], z.shape[4])
        Wo = wo[:, :, 0, 0]
        out = jnp.einsum('oi,bihw->bohw', Wo, z) + bo[None, :, None, None]
        out = jax.nn.relu(_bn(out, go, beo, mo, vo))
        return out

    def _L3_conv_ref(x, w_qkv, b_qkv, w_out, b_out, gamma1, beta1, gamma2, beta2):
        import jax, jax.numpy as jnp
        import numpy as np
        HEADS = 8
        EPS = 1e-05

        def _layernorm(x, gamma, beta):
            mu = jnp.mean(x, axis=-1, keepdims=True)
            var = jnp.var(x, axis=-1, keepdims=True)
            return (x - mu) * jax.lax.rsqrt(var + EPS) * gamma + beta
        b, c, f, t = x.shape
        h = HEADS
        dh = c // h
        scale = dh ** (-0.5)
        xp = jnp.transpose(x, (0, 2, 3, 1))
        xn = _layernorm(xp, gamma1, beta1)
        qkv = xn @ w_qkv + b_qkv
        q, k, v = jnp.split(qkv, 3, axis=-1)

        def to_heads(u):
            return jnp.transpose(u.reshape(b, f * t, h, dh), (0, 2, 1, 3))
        q, k, v = (to_heads(q), to_heads(k), to_heads(v))
        scores = jnp.einsum('bhqd,bhkd->bhqk', q, k) * scale
        attn = jax.nn.softmax(scores, axis=-1)
        o = jnp.einsum('bhqk,bhkd->bhqd', attn, v)
        o = jnp.transpose(o, (0, 2, 1, 3)).reshape(b, f, t, c)
        o = _layernorm(o, gamma2, beta2)
        o = o @ w_out + b_out
        o = o + xn
        return jnp.transpose(o, (0, 3, 1, 2))

    def _gn(v, G=32, eps=1e-05):
        B_, C_, H_, W_ = v.shape
        g = v.reshape(B_, G, C_ // G, H_, W_)
        m = jnp.mean(g, axis=(2, 3, 4), keepdims=True)
        s = jnp.var(g, axis=(2, 3, 4), keepdims=True)
        return ((g - m) / jnp.sqrt(s + eps)).reshape(v.shape)

    def _ln_c(v, eps=1e-06):
        m = jnp.mean(v, axis=1, keepdims=True)
        s = jnp.var(v, axis=1, keepdims=True)
        return (v - m) / jnp.sqrt(s + eps)

    def _ln_t(v, eps=1e-05):
        m = jnp.mean(v, axis=-1, keepdims=True)
        s = jnp.var(v, axis=-1, keepdims=True)
        return (v - m) / jnp.sqrt(s + eps)

    def _to_tokens(v):
        B_, C_, H_, W_ = v.shape
        return v.reshape(B_, C_, H_ * W_).transpose(0, 2, 1)

    def _from_tokens(t, like):
        B_, C_, H_, W_ = like.shape
        return t.transpose(0, 2, 1).reshape(B_, C_, H_, W_)
    x = x + _L0_conv_ref(_gn(x), L0_conv_in_w, L0_conv_in_b, L0_conv_c1_w, L0_conv_c1_b, L0_conv_c2_w, L0_conv_c2_b, L0_conv_c3_w, L0_conv_c3_b, L0_conv_out_w, L0_conv_out_b, L0_conv_xw1, L0_conv_dtw1, L0_conv_dtb1, L0_conv_Al1, L0_conv_Dv1, L0_conv_g1, L0_conv_be1, L0_conv_xw2, L0_conv_dtw2, L0_conv_dtb2, L0_conv_Al2, L0_conv_Dv2, L0_conv_g2, L0_conv_be2, L0_conv_xw3, L0_conv_dtw3, L0_conv_dtb3, L0_conv_Al3, L0_conv_Dv3, L0_conv_g3, L0_conv_be3)
    x = x + _L1_conv_ref(_gn(x), L1_conv_qkv_w, L1_conv_qkv_b, L1_conv_proj_w, L1_conv_proj_b)
    x = x + _L2_conv_ref(_gn(x), L2_conv_wdw, L2_conv_bdw, L2_conv_gdw, L2_conv_bedw, L2_conv_mdw, L2_conv_vdw, L2_conv_ws, L2_conv_bs, L2_conv_gs, L2_conv_bes, L2_conv_ms, L2_conv_vs, L2_conv_wo, L2_conv_bo, L2_conv_go, L2_conv_beo, L2_conv_mo, L2_conv_vo)
    x = x + _L3_conv_ref(_gn(x), L3_conv_w_qkv, L3_conv_b_qkv, L3_conv_w_out, L3_conv_b_out, L3_conv_gamma1, L3_conv_beta1, L3_conv_gamma2, L3_conv_beta2)
    return x

_drawn_inputs = setup_inputs


def setup_inputs(seed=0):
    import zlib

    import numpy as np

    out = dict(_drawn_inputs(seed))
    spreads = {'L0_conv_Dv1': (1.0, 0.6),
     'L0_conv_g1': (1.0, 0.2),
     'L0_conv_be1': (0.0, 0.35),
     'L0_conv_Dv2': (1.0, 0.6),
     'L0_conv_g2': (1.0, 0.2),
     'L0_conv_be2': (0.0, 0.1),
     'L0_conv_Dv3': (1.0, 0.6),
     'L0_conv_g3': (1.0, 0.2),
     'L0_conv_be3': (0.0, 0.1),
     'L3_conv_b_qkv': (0.0, 0.1),
     'L3_conv_b_out': (0.0, 0.1),
     'L3_conv_gamma1': (1.0, 0.2),
     'L3_conv_beta1': (0.0, 0.1),
     'L3_conv_gamma2': (1.0, 0.2),
     'L3_conv_beta2': (0.0, 0.1)}
    factors = {'L0_conv_xw1': 8.0,
     'L0_conv_dtw1': 8.0,
     'L0_conv_dtb1': 23.141,
     'L0_conv_Al1': 8.0,
     'L0_conv_xw2': 7.77,
     'L0_conv_dtw2': 8.0,
     'L0_conv_dtb2': 8.0,
     'L0_conv_Al2': 8.0,
     'L0_conv_xw3': 8.0,
     'L0_conv_dtw3': 8.0,
     'L0_conv_dtb3': 100.953,
     'L0_conv_Al3': 8.0,
     'L1_conv_qkv_b': 3.219,
     'L1_conv_proj_b': 3.737,
     'L2_conv_bdw': 8.0,
     'L2_conv_gdw': 8.0,
     'L2_conv_bedw': 8.0,
     'L2_conv_mdw': 8.0,
     'L2_conv_vdw': 6.965,
     'L2_conv_bs': 8.0,
     'L2_conv_gs': 8.0,
     'L2_conv_bes': 8.0,
     'L2_conv_ms': 8.0,
     'L2_conv_vs': 7.087,
     'L2_conv_bo': 6.395,
     'L2_conv_go': 8.0,
     'L2_conv_beo': 5.816,
     'L2_conv_mo': 5.865,
     'L2_conv_vo': 5.389}
    for name, (base, spread) in spreads.items():
        noise = np.random.default_rng([zlib.crc32(name.encode()), seed]).standard_normal(out[name].shape)
        drawn = base * np.exp(spread * noise) if base else spread * noise
        out[name] = jnp.asarray(drawn.astype(out[name].dtype))
    for name, factor in factors.items():
        out[name] = (out[name] * factor).astype(out[name].dtype)
    return out
```

```python
from contextlib import ExitStack

import concourse.bass as bass
from concourse import mybir

F32 = mybir.dt.float32
F32R = mybir.dt.float32r
ACT = mybir.ActivationFunctionType
ALU = mybir.AluOpType
AX = mybir.AxisListType

P = 128
B, C, HH, WW = 8, 256, 32, 32
L = HH * WW
CT = C // P
N = 512
NC = L // N
HEADS, DH = 8, 32
GH = 4
GROUPS = HEADS // GH
KT = L // P
D_IN, NST, R_DT = 128, 16, 8
DPG = P // NST
SG = D_IN // DPG
L2, L3 = L // 4, L // 16
W3 = L2 + L3
COLS = 2 * L + W3
PASS_AT = (0, L, 2 * L)
PASS_W = (L, L, W3)
RATES = (1, 6, 12, 18)
TAPS = [(1, 1)] + [(y, x) for y in range(3) for x in range(3) if (y, x) != (1, 1)]
SCALE = float(DH) ** -0.5
GN_EPS = 1e-5
LN_EPS = 1e-5
BN_EPS = 1e-5
SMALL_U = 1.0 / 128

WSEC = [("in_w", 2 * 256), ("c1", 128), ("c2", 4 * 128), ("c3", 4 * 128),
        ("xb", 3 * 128), ("xc", 3 * 128), ("out", 256),
        ("qkv1", 2 * 768), ("proj1", 2 * 256), ("wo", 2 * 256), ("qkv3", 2 * 768), ("out3", 2 * 256)]
WOFF, WTOT = {}, 0
for _n, _w in WSEC:
    WOFF[_n] = WTOT
    WTOT += _w

VSEC = [("in_b", 2), ("c1_b", 1), ("c2_b", 1), ("c3_b", 1), ("out_b", 2), ("dtb", 3), ("Dv", 3),
        ("g", 3), ("be", 3), ("Al", 3 * SG), ("qkv_b1", 6), ("proj_b", 2),
        ("bn_b", 6), ("bn_g", 6), ("bn_be", 6), ("bn_m", 6), ("bn_v", 6), ("wdw", 18), ("ws", 8),
        ("qkv_b3", 6), ("out3_b", 2), ("gamma1", 2), ("beta1", 2), ("gamma2", 2), ("beta2", 2)]
VOFF, VTOT = {}, 0
for _n, _w in VSEC:
    VOFF[_n] = VTOT
    VTOT += _w


class Signal:

    def __init__(self, sem, per):
        self.sem, self.per = sem, per

    def __call__(self, b, k):
        return self.sem, b * self.per + k


def build(nc, x, wpack, vpack, w8, out):
    with ExitStack() as ctx:
        sb = lambda name, shape, dt=F32: ctx.enter_context(nc.sbuf_tensor(name, shape, dt))
        per_name = {}

        def sig(name, per):
            per_name[name] = per
            return Signal(ctx.enter_context(nc.semaphore(name)), per)

        sem = lambda name: ctx.enter_context(nc.semaphore(name))

        xin = sb("xin", [P, CT, L])
        xr = sb("xr", [P, CT, L])
        xg = sb("xg", [P, CT, L])
        W = sb("W", [P, WTOT])
        V = sb("V", [P, VTOT])
        W8 = sb("W8", [R_DT, 3, 2, P])
        Wd = sb("Wd", [P, 3, P])
        ident = sb("ident", [P, P])
        id2 = sb("id2", [P, 64])
        g8 = sb("g8", [P, P])
        mean128 = sb("mean128", [P, P])
        mean256 = sb("mean256", [P, P])
        ones32 = sb("ones32", [P, 32])
        e8 = sb("e8", [P, DPG])
        ysel = sb("ysel", [P, 4, 32])
        sel = sb("sel", [P, 8, P], F32R)
        DW = sb("DW", [P, 2, 9, P])
        MX = sb("MX", [P, 2, 256])
        Aneg = sb("Aneg", [P, 3 * SG])
        binv = sb("binv", [P, 6])
        bbias = sb("bbias", [P, 6])
        bes = sb("bes", [P, 3])
        eps = sb("eps", [P, 1])
        mhalf = sb("mhalf", [P, 1])
        small = sb("small", [P, 64])
        st = small[:, 0:24].rearrange("p (t c s) -> p t c s", t=2, c=2)
        msum = small[:, 24:26]
        dev = small[:, 46:54].rearrange("p (t q) -> p t q", t=2)
        dd = small[:, 54:62].rearrange("p (t q) -> p t q", t=2)
        m2 = small[:, 30:32]
        lnv = small[:, 32:34]
        rs = small[:, 34:36]
        sh = small[:, 36:38]
        tmp6 = small[:, 40:46]
        PS = ctx.enter_context(nc.psum_tensor("PS", [P, 8, N], F32))

        with ExitStack() as over:
            so = lambda name, shape, dt=F32: over.enter_context(nc.sbuf_tensor(name, shape, dt))
            Brep = so("Brep", [P, COLS])
            Crep = so("Crep", [P, COLS])
            work = so("work", [P, 12, L])
            yv = so("yv", [P, 3, L])
            f1 = so("f1", [P, L])
            f23 = so("f23", [P, W3])
            dstk = so("dstk", [P, 2, COLS], F32R)
            ustk = so("ustk", [P, 2, COLS], F32R)
        with ExitStack() as over:
            so = lambda name, shape, dt=F32: over.enter_context(nc.sbuf_tensor(name, shape, dt))
            QS = so("QS", [98, HEADS, L], F32R)
            KS = so("KS", [98, HEADS, L], F32R)
            piece = so("piece", [P, 2, 2, L], F32R)
            Vt = so("Vt", [P, KT, C])
            PT = so("PT", [P, 3, GH, N])
            oT = so("oT", [P, CT, L])
            lr = so("lr", [P, 2, N])
            mx = so("mx", [P, GH * KT])
            nm = so("nm", [GH * KT, 2, P], F32R)
        with ExitStack() as over:
            so = lambda name, shape, dt=F32: over.enter_context(nc.sbuf_tensor(name, shape, dt))
            br = so("br", [P, 2, L])
            zm = so("zm", [P, 2, L])
            rl = so("rl", [P, 4, N])
        sel32 = work[:, 0, :].rearrange("p (g m) -> p g m", g=8)
        sq = PT[:, 0, :, :]
        rstd = PT[:, 1, :, :]

        w_in = W[:, WOFF["in_w"]:WOFF["in_w"] + 512].rearrange("p (k m) -> p k m", k=2)
        w_c1 = W[:, WOFF["c1"]:WOFF["c1"] + 128]
        w_c2 = W[:, WOFF["c2"]:WOFF["c2"] + 512].rearrange("p (k m) -> p k m", k=4)
        w_c3 = W[:, WOFF["c3"]:WOFF["c3"] + 512].rearrange("p (k m) -> p k m", k=4)
        w_xb = W[:, WOFF["xb"]:WOFF["xb"] + 384].rearrange("p (s m) -> p s m", s=3)
        w_xc = W[:, WOFF["xc"]:WOFF["xc"] + 384].rearrange("p (s m) -> p s m", s=3)
        w_out = W[:, WOFF["out"]:WOFF["out"] + 256]
        w_qkv = [W[:, WOFF[n]:WOFF[n] + 1536].rearrange("p (k m) -> p k m", k=2) for n in ("qkv1", "qkv3")]
        w_proj = [W[:, WOFF[n]:WOFF[n] + 512].rearrange("p (k m) -> p k m", k=2) for n in ("proj1", "out3")]
        w_o = W[:, WOFF["wo"]:WOFF["wo"] + 512].rearrange("p (k m) -> p k m", k=2)
        v = lambda name, i=0, n=1: V[:, VOFF[name] + i:VOFF[name] + i + n]

        loaded = sem("loaded")
        built = sem("built")
        folded = sem("folded")
        prepared = sem("prepared")
        logged = sem("logged")

        xin_here = sig("xin_here", 16)
        stored = sig("stored", 16)
        gn_st, gn_sum, gn_dev, gn_dd, gn_q = sig("gn_st", 16), sig("gn_sum", 4), sig("gn_dev", 4), sig("gn_dd", 4), sig("gn_q", 4)
        gn_gm, gn_m2, gn_gv = sig("gn_gm", 4), sig("gn_m2", 4), sig("gn_gv", 4)
        gn_ln, gn_rs, gn_sh = sig("gn_ln", 4), sig("gn_rs", 4), sig("gn_sh", 4)
        gn_xa, gn_xb = sig("gn_xa", 4), sig("gn_xb", 4)
        xp_ps, xp_sb = sig("xp_ps", 2), sig("xp_sb", 2)
        f1_ps, f1_sb = sig("f1_ps", 2), sig("f1_sb", 2)
        f2_ps, f2_sb = sig("f2_ps", 1), sig("f2_sb", 1)
        f3_ps, f3_sb = sig("f3_ps", 1), sig("f3_sb", 1)
        pre_ps, brep_ps, crep_ps = sig("pre_ps", 3), sig("brep_ps", 3), sig("crep_ps", 3)
        brep_sb, crep_sb = sig("brep_sb", 3), sig("crep_sb", 3)
        sp_abs, sp_pos, sp_exp, sp_one = sig("sp_abs", 4), sig("sp_pos", 4), sig("sp_exp", 3), sig("sp_one", 3)
        sp_ln, sp_cut, sp_sum = sig("sp_ln", 3), sig("sp_cut", 3), sig("sp_sum", 3)
        sp_q, sp_qu, sp_poly, sp_big, sp_one_of = (sig(n, 3) for n in ("sp_q", "sp_qu", "sp_poly", "sp_big", "sp_one_of"))
        step, stepx = sig("step", 3), sig("stepx", 3)
        heads_in, rests_in = sig("heads_in", 12), sig("rests_in", 12)
        d_ps, u_ps = sig("d_ps", 48), sig("u_ps", 48)
        dA_sb, dBx_sb = sig("dA_sb", 64), sig("dBx_sb", 48)
        scanned, hC_sb, y_ps = sig("scanned", 96), sig("hC_sb", 48), sig("y_ps", 12)
        y_sb = sig("y_sb", 6)
        lm_ps, lm_d, lm_sq, lv_ps = sig("lm_ps", 4), sig("lm_d", 4), sig("lm_sq", 4), sig("lv_ps", 4)
        lv_ln, lv_rs, ln_n = sig("lv_ln", 4), sig("lv_rs", 4), sig("ln_n", 4)
        levels = sig("levels", 14)
        z_ps, z_sb, gated = sig("z_ps", 2), sig("z_sb", 2), sig("gated", 1)
        o_ps, x_new = sig("o_ps", 16), sig("x_new", 16)
        qk_ps, qk_head, qk_rest = sig("qk_ps", 8), sig("qk_head", 8), sig("qk_rest", 8)
        stackedq = [sig(f"stackedq{g}", 2 * 12 * 16) for g in range(GROUPS)]
        stackedk = [sig(f"stackedk{g}", 2 * 12 * 16) for g in range(GROUPS)]
        ones_in = sig("ones_in", 1)
        v_ps, v_sb = sig("v_ps", 4), sig("v_sb", 4)
        r_ps, r_max = sig("r_ps", 2 * HEADS * KT), sig("r_max", 2 * HEADS * KT)
        mt_ps, nm_head, nm_rest = sig("mt_ps", 4), sig("nm_head", 4), sig("nm_rest", 4)
        nm_in = [sig(f"nm_in{g}", 2 * 2 * 16) for g in range(GROUPS)]
        s_ps, p_sb = sig("s_ps", 128), sig("p_sb", 128)
        pv_ps, den_ln, den_rc = sig("pv_ps", 64), sig("den_ln", 8), sig("den_rc", 8)
        o_raw, o_sb = sig("o_raw", 8), sig("o_sb", 8)
        cm_ps, cm_d, cm_sq, cv_ps = sig("cm_ps", 4), sig("cm_d", 8), sig("cm_sq", 8), sig("cv_ps", 4)
        cv_ln, cv_rs, cn_n, cn_x = sig("cv_ln", 4), sig("cv_rs", 4), sig("cn_n", 8), sig("cn_x", 8)
        x3n = sig("x3n", 2)
        dw_ps, dw_sb, mix_ps, mix_sb = sig("dw_ps", 4), sig("dw_sb", 4), sig("mix_ps", 4), sig("mix_sb", 4)
        wo_sb = sig("wo_sb", 4)

        NLOAD = 16 * 8
        NBUILT = 21
        NPREP = 38

        def norm_job(k):
            return [(L, yv[:, 0, :], 2, 0), (L, yv[:, 1, :], 4, 2),
                    (W3, yv[:, 2, 0:W3], 6, 4), (W3, yv[:, 2, N:N + W3], 7, 5)][k]

        out_v = out.rearrange("b (t p) n -> b p t n", p=P)
        x_v = x.rearrange("b (t p) n -> b p t n", p=P)

        block = ctx.enter_context(nc.Block())

        @block.sync
        def _(sp):
            sp.dma_start(xin[:, :, :], x_v[0]).then_inc(xin_here.sem, 16)
            sp.dma_start(V[:, :], vpack).then_inc(loaded, 16)
            sp.dma_start(W8[:, :, :, :], w8).then_inc(loaded, 16)
            cuts = [0, WOFF["c1"], WOFF["xb"], WOFF["qkv1"], WOFF["wo"], WOFF["qkv3"], WTOT]
            for a, e in zip(cuts, cuts[1:]):
                sp.dma_start(W[:, a:e], wpack[:, a:e]).then_inc(loaded, 16)

            def attention(b, a):
                for g in range(GROUPS):
                    for kind, (stack, done) in enumerate(((QS, stackedq[g]), (KS, stackedk[g]))):
                        n = 4 * a + 2 * g + kind
                        sp.wait_ge(*qk_head(b, n + 1))
                        sp.wait_ge(*qk_rest(b, n + 1))
                        if kind == 1:
                            sp.wait_ge(*ones_in(b, 1))
                        parts = (0, 1, 0) if kind == 0 else (0, 0, 1)
                        for j in range(GH):
                            for blk, part in enumerate(parts):
                                sp.dma_start(stack[32 * blk:32 * blk + 32, GH * g + j, :].bitcast(F32),
                                             piece[32 * j:32 * j + 32, kind, part, :].bitcast(F32)).then_inc(done.sem, 16)
                for g in range(GROUPS):
                    sp.wait_ge(*nm_rest(b, 2 * a + g + 1))
                    for part in range(2):
                        sp.dma_start(QS[96 + part:97 + part, GH * g:GH * g + GH, :].bitcast(F32),
                                     nm[:, part, :].bitcast(F32)).then_inc(nm_in[g].sem, 16)

            def sample(b, last):
                sp.wait_ge(*x_new(b, 4))
                if not last:
                    sp.dma_start(xin[:, :, :], x_v[b + 1]).then_inc(xin_here.sem, 16)
                attention(b, 0)
                attention(b, 1)
                sp.wait_ge(*x_new(b, 16))
                sp.dma_start(out_v[b], xr[:, :, :]).then_inc(stored.sem, 16)

            with sp.Fori(0, B - 1) as b:
                sample(b, False)
            sample(B - 1, True)
            sp.wait_ge(*stored(B - 1, 16))

        @block.gpsimd
        def _(pool):
            nb = [0]

            def step_(ins):
                nb[0] += 1
                ins.then_inc(built, 1)
                pool.wait_ge(built, nb[0])

            step_(pool.memset(ident[:, :], 0.0))
            step_(pool.affine_select(out=ident[:, :], in_=ident[:, :], compare_op=ALU.not_equal, fill=1.0,
                                     base=0, pattern=[[-1, P]], channel_multiplier=1))
            step_(pool.memset(g8[:, :], 1.0 / 32))
            gv = g8[:, :].rearrange("p (k r) -> p k r", r=8)
            step_(pool.affine_select(out=gv, in_=gv, compare_op=ALU.is_ge, fill=0.0, base=0,
                                     pattern=[[-8, 16], [0, 8]], channel_multiplier=1))
            step_(pool.affine_select(out=gv, in_=gv, compare_op=ALU.is_ge, fill=0.0, base=7,
                                     pattern=[[8, 16], [0, 8]], channel_multiplier=-1))
            step_(pool.memset(e8[:, :], 1.0))
            step_(pool.affine_select(out=e8[:, :], in_=e8[:, :], compare_op=ALU.is_ge, fill=0.0, base=0,
                                     pattern=[[-NST, DPG]], channel_multiplier=1))
            step_(pool.affine_select(out=e8[:, :], in_=e8[:, :], compare_op=ALU.is_ge, fill=0.0, base=NST - 1,
                                     pattern=[[NST, DPG]], channel_multiplier=-1))
            step_(pool.memset(ysel[:, :, :], 0.0))
            for i in range(4):
                step_(pool.tensor_copy(ysel[:, i, 8 * i:8 * i + 8], e8[:, :]))
            step_(pool.memset(sel32[:, :, :], 0.0))
            for base in (0, -64):
                s4 = sel32[:, :, :].rearrange("p g (d n) -> p g d n", n=NST)
                step_(pool.affine_select(out=s4, in_=s4, compare_op=ALU.not_equal, fill=1.0, base=base,
                                         pattern=[[-8, 8], [-1, 8], [0, NST]], channel_multiplier=1))
            step_(pool.memset(mean128[:, :], 1.0 / 128))
            step_(pool.memset(mean256[:, :], 1.0 / 256))
            step_(pool.memset(ones32[:, :], 1.0))
            step_(pool.memset(eps[:, :], 1e-5))
            step_(pool.memset(mhalf[:, :], -0.5))

            def sample(b):
                for n in range(3 * SG):
                    ps, at = n // SG, PASS_AT[n // SG]
                    if n >= 6:
                        pool.wait_ge(*y_ps(b, (n - 6) // 4 + 1))
                    if n == 0:
                        pool.wait_ge(*crep_sb(b, 3))
                    slot = work[:, 6 + n % 6, :]
                    h = work[:, 4 + n % 2, :]
                    if ps < 2:
                        pool.wait_ge(*scanned(b, n + 1))
                        pool.tensor_tensor(slot, h, Crep[:, at:at + L], ALU.mult).then_inc(hC_sb.sem, 1)
                    else:
                        pool.wait_ge(*scanned(b, 32 + 4 * (n - 32) + 4))
                        two = lambda t: t.rearrange("p (d w) -> p d w", d=2)[:, :, 0:W3]
                        pool.tensor_tensor(two(slot), two(h), Crep[:, None, at:at + W3].broadcast_to((P, 2, W3)),
                                           ALU.mult).then_inc(hC_sb.sem, 1)
                pool.wait_ge(*x_new(b, 4))
                one = ones32[96:98, 0:1].broadcast_to((2, HEADS * L))
                pool.tensor_tensor(KS[96:98, :, :].rearrange("p h n -> p (h n)"), one, one,
                                   ALU.mult).then_inc(ones_in.sem, 1)
                pool.wait_ge(*x_new(b, 16))

            with pool.Fori(0, B) as b:
                sample(b)

        @block.scalar
        def _(act):
            act.preload_act_table_set("natural_log_exp_and_others")
            act.wait_ge(loaded, NLOAD)
            act.wait_ge(built, NBUILT)
            act.activation(Aneg[:, :], v("Al", 0, 3 * SG), ACT.Exp).then_inc(logged, 1)
            act.activation(tmp6, v("bn_v", 0, 6), ACT.Ln, bias=eps[:, :]).then_inc(logged, 1)
            act.wait_ge(logged, 2)
            act.activation(tmp6, tmp6, ACT.Exp, scale=-0.5).then_inc(logged, 1)

            def group_norm(b, s, X):
                act.wait_ge(*gn_gv(b, s + 1))
                act.activation(lnv, PS[:, 6, 0:2], ACT.Ln, scale=4.0 / L, bias=eps[:, :]).then_inc(gn_ln.sem, 1)
                act.wait_ge(*gn_ln(b, s + 1))
                act.activation(rs, lnv, ACT.Exp, scale=-0.5).then_inc(gn_rs.sem, 1)
                act.wait_ge(*gn_rs(b, s + 1))
                act.wait_ge(*gn_sh(b, s + 1))
                act.activation(xg[:, 1, :], X[:, 1, :], ACT.Identity, scale=rs[:, 1:2],
                               bias=sh[:, 1:2]).then_inc(gn_xb.sem, 1)

            def block0(b):
                for c in range(NC):
                    act.wait_ge(*xp_ps(b, c + 1))
                    act.activation(yv[:, 0, c * N:c * N + N], PS[:, c, :], ACT.Identity,
                                   bias=v("in_b", 0)).then_inc(xp_sb.sem, 1)
                act.wait_ge(*f2_ps(b, 1))
                act.activation(f23[:, 0:L2], PS[:, 4, 0:L2], ACT.Identity, bias=v("c2_b")).then_inc(f2_sb.sem, 1)
                act.wait_ge(*f3_ps(b, 1))
                act.activation(f23[:, L2:W3], PS[:, 5, 0:L3], ACT.Identity, bias=v("c3_b")).then_inc(f3_sb.sem, 1)
                for ps in range(3):
                    at, w = PASS_AT[ps], PASS_W[ps]
                    tu, tl = work[:, ps % 2, 0:w], work[:, 2 + ps % 2, 0:w]
                    act.wait_ge(*pre_ps(b, ps + 1))
                    if ps == 2:
                        act.wait_ge(*step(b, 1))
                    if ps < 2:
                        src = PS[:, (0, 6)[ps]:(0, 6)[ps] + 2, :].rearrange("p a n -> p (a n)")
                        act.activation(tu, src, ACT.Abs, bias=v("dtb", ps)).then_inc(sp_abs.sem, 1)
                    else:
                        act.activation(tu[:, 0:L2], PS[:, 4, 0:L2], ACT.Abs, bias=v("dtb", 1)).then_inc(sp_abs.sem, 1)
                        act.activation(tu[:, L2:W3], PS[:, 4, L2:W3], ACT.Abs, bias=v("dtb", 2)).then_inc(sp_abs.sem, 1)
                    for a_, e_, bias in (((0, w, v("dtb", ps)),) if ps < 2 else ((0, L2, v("dtb", 1)), (L2, W3, v("dtb", 2)))):
                        if ps < 2:
                            act.activation(work[:, 4 + ps, :], src, ACT.Relu, bias=bias).then_inc(sp_pos.sem, 1)
                        else:
                            act.activation(work[:, 4, a_:e_], PS[:, 4, a_:e_], ACT.Relu, bias=bias).then_inc(sp_pos.sem, 1)
                    act.wait_ge(*sp_abs(b, (1, 2, 4)[ps]))
                    act.activation(tu, tu, ACT.Exp, scale=-1.0).then_inc(sp_exp.sem, 1)
                    act.wait_ge(*sp_exp(b, ps + 1))
                    if ps == 2:
                        act.wait_ge(*sp_sum(b, 1))
                    act.activation(tl, tu, ACT.Ln, bias=1.0).then_inc(sp_ln.sem, 1)
                    if ps >= 1:
                        act.wait_ge(*sp_cut(b, ps))
                        act.wait_ge(*sp_poly(b, ps))
                    act.activation(work[:, 9, 0:w], tu, ACT.Identity, bias=1.0).then_inc(sp_one.sem, 1)
                    act.activation(work[:, 10, 0:w], tu, ACT.Identity, scale=1.0 / 3, bias=mhalf[:, :]).then_inc(sp_q.sem, 1)
                    for dst, src_ps, done, bank in ((Brep, brep_ps, brep_sb, (2, 0, 6)), (Crep, crep_ps, crep_sb, (4, 2, 0))):
                        act.wait_ge(*src_ps(b, ps + 1))
                        src = PS[:, bank[ps]:bank[ps] + 2, :].rearrange("p a n -> p (a n)")[:, 0:w]
                        act.activation(dst[:, at:at + w], src, ACT.Copy).then_inc(done.sem, 1)
                act.wait_ge(*rests_in(b, 12))
                for n in range(3 * SG):
                    ps = n // SG
                    g = scan_group(n)
                    slot = 2 + 2 * ((2 * n) % 3)
                    if n >= 2:
                        act.wait_ge(*scanned(b, scans(n - 2)))
                    act.wait_ge(*d_ps(b, n + 1))
                    dst = work[:, n % 2, :]
                    src = PS[:, slot:slot + 2, :].rearrange("p a n -> p (a n)")
                    if ps < 2:
                        act.activation(dst, src, ACT.Exp, scale=Aneg[:, ps * SG + g:ps * SG + g + 1]).then_inc(dA_sb.sem, 1)
                    else:
                        act.activation(dst[:, 0:L2], src[:, 0:L2], ACT.Exp,
                                       scale=Aneg[:, SG + g:SG + g + 1]).then_inc(dA_sb.sem, 1)
                        act.activation(dst[:, L2:W3], src[:, L2:W3], ACT.Exp,
                                       scale=Aneg[:, 2 * SG + g:2 * SG + g + 1]).then_inc(dA_sb.sem, 1)
                for k in range(4):
                    w, ybuf, mb, vb = norm_job(k)
                    act.wait_ge(*lm_d(b, k + 1))
                    t = work[:, k, 0:w]
                    act.activation(t, ybuf, ACT.Square).then_inc(lm_sq.sem, 1)
                    act.wait_ge(*lv_ps(b, k + 1))
                    src = PS[:, vb:vb + 2, :].rearrange("p a n -> p (a n)")[:, 0:w]
                    t2 = work[:, 4 + k, 0:w]
                    act.activation(t2, src, ACT.Ln, bias=eps[:, :]).then_inc(lv_ln.sem, 1)
                    act.wait_ge(*lv_ln(b, k + 1))
                    act.activation(t2, t2, ACT.Exp, scale=-0.5).then_inc(lv_rs.sem, 1)
                for c in range(NC):
                    act.wait_ge(*z_ps(b, c + 1))
                    act.activation(work[:, 8, c * N:c * N + N], PS[:, 6 + c, :], ACT.Silu,
                                   bias=v("in_b", 1)).then_inc(z_sb.sem, 1)
                act.preload_act_table_set("natural_log_exp_and_others")

            def chan_norm(b, s, X, gamma, beta):
                for c in range(NC):
                    n = NC * s + c
                    for t in range(CT):
                        act.wait_ge(*cm_d(b, 2 * n + t + 1))
                        act.activation(sq[:, 2 * c + t, :], X[:, t, c * N:c * N + N], ACT.Square).then_inc(cm_sq.sem, 1)
                for c in range(NC):
                    n = NC * s + c
                    act.wait_ge(*cv_ps(b, n + 1))
                    act.activation(rstd[:, c, :], PS[:, 2 + c, :], ACT.Ln, bias=eps[:, :]).then_inc(cv_ln.sem, 1)
                    act.wait_ge(*cv_ln(b, n + 1))
                    act.activation(rstd[:, c, :], rstd[:, c, :], ACT.Exp, scale=-0.5).then_inc(cv_rs.sem, 1)
                for c in range(NC):
                    n = NC * s + c
                    for t in range(CT):
                        act.wait_ge(*cn_n(b, 2 * n + t + 1))
                        act.activation(X[:, t, c * N:c * N + N], X[:, t, c * N:c * N + N], ACT.Identity,
                                       scale=v(gamma, t), bias=v(beta, t)).then_inc(cn_x.sem, 1)

            def attention(b, a):
                bq = ("qkv_b1", "qkv_b3")[a]
                for g in range(GROUPS):
                    for kind in range(2):
                        n = 2 * g + kind
                        act.wait_ge(*qk_ps(b, 4 * a + n + 1))
                        if g == 1:
                            done = (stackedq, stackedk)[kind][0]
                            act.wait_ge(*done(b, (a + 1) * 192))
                        src = PS[:, 2 * n:2 * n + 2, :].rearrange("p a n -> p (a n)")
                        act.activation(piece[:, kind, 0, :], src, ACT.Identity,
                                       bias=v(bq, 2 * kind + g)).then_inc(qk_head.sem, 1)
                for q in range(2):
                    act.wait_ge(*v_ps(b, 2 * a + q + 1))
                    act.activation(Vt[:, 4 * q:4 * q + 4, :].rearrange("p k c -> p (k c)"),
                                   PS[:, 2 * q:2 * q + 2, :].rearrange("p a n -> p (a n)"), ACT.Copy).then_inc(v_sb.sem, 1)
                def neg_max(g):
                    act.wait_ge(*mt_ps(b, 2 * a + g + 1))
                    if g == 1:
                        act.wait_ge(*nm_in[0](b, (a + 1) * 32))
                    act.activation(nm[:, 0, :], PS[0:GH * KT, 6, 0:P], ACT.Copy, scale=-1.0).then_inc(nm_head.sem, 1)
                neg_max(0)
                for g in range(GROUPS):
                    for c in range(NC):
                        for kt in range(KT):
                            i = (a * GROUPS + g) * NC * KT + c * KT + kt
                            if i % (2 * NC * KT) >= 3:
                                act.wait_ge(*pv_ps(b, i - 2))
                            for pr in range(2):
                                act.wait_ge(*s_ps(b, 2 * i + pr + 1))
                                act.activation(PT[:, i % 3, 2 * pr:2 * pr + 2, :], PS[:, 2 + 2 * pr:4 + 2 * pr, :],
                                               ACT.Exp, scale=SCALE).then_inc(p_sb.sem, 1)
                        if g == 0 and c == NC - 1:
                            neg_max(1)
                        j = (a * GROUPS + g) * NC + c
                        act.wait_ge(*pv_ps(b, (j + 1) * KT))
                        act.activation(lr[:, 0, :], PS[:, 1, :], ACT.Ln).then_inc(den_ln.sem, 1)
                        act.wait_ge(*den_ln(b, j + 1))
                        if j % 4 >= 1:
                            act.wait_ge(*o_raw(b, j))
                        act.activation(lr[:, 1, :], lr[:, 0, :], ACT.Exp, scale=-1.0).then_inc(den_rc.sem, 1)

            def block2(b):
                for t in range(2):
                    for c in range(NC):
                        n = 2 * t + c
                        act.wait_ge(*dw_ps(b, n + 1))
                        act.activation(br[:, t, c * N:c * N + N], PS[:, n, :], ACT.Relu, scale=binv[:, t:t + 1],
                                       bias=bbias[:, t:t + 1]).then_inc(dw_sb.sem, 1)
                for m in range(2):
                    for c in range(NC):
                        n = 2 * m + c
                        act.wait_ge(*mix_ps(b, n + 1))
                        act.activation(zm[:, m, c * N:c * N + N], PS[:, 4 + n, :], ACT.Relu, scale=binv[:, 2 + m:3 + m],
                                       bias=bbias[:, 2 + m:3 + m]).then_inc(mix_sb.sem, 1)
                for m in range(2):
                    for c in range(NC):
                        n = 2 * m + c
                        act.wait_ge(*o_ps(b, 8 + n + 1))
                        act.activation(rl[:, n, :], PS[:, n, :], ACT.Relu, scale=binv[:, 4 + m:5 + m],
                                       bias=bbias[:, 4 + m:5 + m]).then_inc(wo_sb.sem, 1)

            with act.Fori(0, B) as b:
                act.wait_ge(*xin_here(b, 16))
                group_norm(b, 0, xin)
                block0(b)
                act.wait_ge(*x_new(b, 4))
                group_norm(b, 1, xr)
                attention(b, 0)
                act.wait_ge(*x_new(b, 8))
                group_norm(b, 2, xr)
                block2(b)
                act.wait_ge(*x_new(b, 12))
                group_norm(b, 3, xr)
                chan_norm(b, 0, xg, "gamma1", "beta1")
                attention(b, 1)
                chan_norm(b, 1, oT, "gamma2", "beta2")
                act.wait_ge(*x_new(b, 16))

        @block.vector
        def _(dve):
            dve.wait_ge(loaded, NLOAD)
            dve.wait_ge(built, NBUILT)
            dve.wait_ge(logged, 3)
            nprep = [0]

            def prep(ins):
                nprep[0] += 1
                ins.then_inc(prepared, 1)
                dve.wait_ge(prepared, nprep[0])

            prep(dve.tensor_copy(sel[:, :, :], sel32[:, :, :]))
            prep(dve.tensor_scalar(Aneg[:, :], Aneg[:, :], -1.0, None, ALU.mult))
            prep(dve.tensor_tensor(binv[:, :], tmp6, v("bn_g", 0, 6), ALU.mult))
            prep(dve.tensor_tensor(bbias[:, :], v("bn_b", 0, 6), v("bn_m", 0, 6), ALU.subtract))
            prep(dve.tensor_tensor(bbias[:, :], bbias[:, :], binv[:, :], ALU.mult))
            prep(dve.tensor_tensor(bbias[:, :], bbias[:, :], v("bn_be", 0, 6), ALU.add))
            prep(dve.tensor_tensor(bes[:, 0:1], v("be", 0), v("be", 1), ALU.add))
            prep(dve.tensor_tensor(bes[:, 1:3], v("be", 1, 2), v("be", 1, 2), ALU.add))
            prep(dve.tensor_tensor(id2[:, :], ident[:, 0:64], ident[:, 64:128], ALU.add))
            for t in range(2):
                for tap in range(9):
                    prep(dve.tensor_scalar(DW[:, t, tap, :], ident[:, :], v("wdw", 9 * t + tap), None, ALU.mult))
                for o in range(4):
                    prep(dve.tensor_scalar(MX[:, t, 64 * o:64 * o + 64], id2[:, :], v("ws", 4 * t + o), None, ALU.mult))
            for s in range(3):
                dve.wait_ge(folded, s + 1)
                prep(dve.tensor_copy(Wd[:, s, :], PS[:, s, 0:P]))

            def group_norm(b, s, X):
                for t in range(CT):
                    for c in range(NC):
                        dve.bn_stats(st[:, t, c, :], X[:, t, c * N:c * N + N]).then_inc(gn_st.sem, 1)
                quarter = st.rearrange("p t c (e k) -> p t (c e) k", e=2)
                dve.wait_ge(*gn_st(b, 4 * s + 4))
                dve.tensor_reduce(msum, quarter[:, :, :, 1], AX.X, ALU.add).then_inc(gn_sum.sem, 1)
                dve.wait_ge(*gn_gm(b, s + 1))
                dve.tensor_tensor(dev, quarter[:, :, :, 1], PS[:, 7, 0:2, None].broadcast_to((P, CT, 4)),
                                  ALU.subtract).then_inc(gn_dev.sem, 1)
                dve.wait_ge(*gn_dev(b, s + 1))
                dve.tensor_tensor(dd, dev, dev, ALU.mult).then_inc(gn_dd.sem, 1)
                dve.wait_ge(*gn_dd(b, s + 1))
                dve.scalar_tensor_tensor(out=dd, in0=dd, scalar=float(L // 4), in1=quarter[:, :, :, 2],
                                         op0=ALU.mult, op1=ALU.add).then_inc(gn_q.sem, 1)
                dve.wait_ge(*gn_q(b, s + 1))
                dve.tensor_reduce(m2, dd, AX.X, ALU.add).then_inc(gn_m2.sem, 1)
                dve.wait_ge(*gn_rs(b, s + 1))
                dve.scalar_tensor_tensor(out=sh, in0=PS[:, 7, 0:2], scalar=-1.0, in1=rs, op0=ALU.mult,
                                         op1=ALU.mult).then_inc(gn_sh.sem, 1)
                dve.wait_ge(*gn_sh(b, s + 1))
                dve.tensor_scalar(xg[:, 0, :], X[:, 0, :], rs[:, 0:1], sh[:, 0:1], ALU.mult, ALU.add).then_inc(gn_xa.sem, 1)

            def block0(b):
                for c in range(NC):
                    dve.wait_ge(*f1_ps(b, c + 1))
                    dve.tensor_scalar(f1[:, c * N:c * N + N], PS[:, 2 + c, :], v("c1_b"), None, ALU.add).then_inc(f1_sb.sem, 1)
                for ps in range(3):
                    at, w = PASS_AT[ps], PASS_W[ps]
                    tu, tl = work[:, ps % 2, 0:w], work[:, 2 + ps % 2, 0:w]
                    pos, cut = work[:, 4 + ps % 2, 0:w], work[:, 6, 0:w]
                    dl, ux = work[:, 7, 0:w], work[:, 8, 0:w]
                    one, qu, big = work[:, 9, 0:w], work[:, 10, 0:w], work[:, 11, 0:w]
                    dve.wait_ge(*sp_exp(b, ps + 1))
                    dve.tensor_scalar(big, tu, SMALL_U, None, ALU.is_ge).then_inc(sp_big.sem, 1)
                    dve.wait_ge(*sp_one(b, ps + 1))
                    dve.scalar_tensor_tensor(out=cut, in0=one, scalar=-1.0, in1=tu, op0=ALU.add,
                                             op1=ALU.subtract).then_inc(sp_cut.sem, 1)
                    dve.wait_ge(*sp_q(b, ps + 1))
                    dve.tensor_tensor(qu, qu, tu, ALU.mult).then_inc(sp_qu.sem, 1)
                    dve.wait_ge(*sp_cut(b, ps + 1))
                    dve.tensor_tensor(cut, tl, cut, ALU.subtract).then_inc(sp_sum.sem, 1)
                    dve.wait_ge(*sp_qu(b, ps + 1))
                    dve.scalar_tensor_tensor(out=dl, in0=qu, scalar=1.0, in1=tu, op0=ALU.add,
                                             op1=ALU.mult).then_inc(sp_poly.sem, 1)
                    dve.wait_ge(prepared, NPREP)
                    dve.wait_ge(*sp_big(b, ps + 1))
                    dve.wait_ge(*sp_sum(b, ps + 1))
                    dve.wait_ge(*sp_poly(b, ps + 1))
                    dve.copy_predicated(dl, big.bitcast(mybir.dt.int32), cut).then_inc(sp_one_of.sem, 1)
                    dve.wait_ge(*sp_pos(b, (1, 2, 4)[ps]))
                    dve.wait_ge(*sp_one_of(b, ps + 1))
                    dve.tensor_tensor(dl, dl, pos, ALU.add).then_inc(step.sem, 1)
                    dve.wait_ge(*step(b, ps + 1))
                    dve.wait_ge(*(f1_sb(b, 2) if ps < 2 else f3_sb(b, 1)))
                    src = f1[:, :] if ps < 2 else f23[:, :]
                    dve.tensor_tensor(ux, dl, src, ALU.mult).then_inc(stepx.sem, 1)
                    dve.wait_ge(*stepx(b, ps + 1))
                    for X, stk in ((dl, dstk), (ux, ustk)):
                        for hh in range(2):
                            r = slice(64 * hh, 64 * hh + 64)
                            dve.tensor_copy(stk[r, hh, at:at + w], X[r, :]).then_inc(heads_in.sem, 1)
                    dve.wait_ge(*heads_in(b, 4 * ps + 4))
                    for X, stk in ((dl, dstk), (ux, ustk)):
                        for hh in range(2):
                            r, ro = slice(64 * hh, 64 * hh + 64), slice(64 - 64 * hh, 128 - 64 * hh)
                            dve.tensor_tensor(stk[ro, hh, at:at + w], X[r, :], stk[r, hh, at:at + w].bitcast(F32),
                                              ALU.subtract).then_inc(rests_in.sem, 1)
                dve.wait_ge(*brep_sb(b, 3))
                for n in range(3 * SG):
                    ps, at = n // SG, PASS_AT[n // SG]
                    slot = 2 + 2 * ((2 * n + 1) % 3)
                    w = PASS_W[ps]
                    dA, dBx, h = work[:, n % 2, :], work[:, 2 + n % 2, :], work[:, 4 + n % 2, :]
                    dve.wait_ge(*u_ps(b, n + 1))
                    src = PS[:, slot:slot + 2, :].rearrange("p a n -> p (a n)")[:, 0:w]
                    dve.tensor_tensor(dBx[:, 0:w], src, Brep[:, at:at + w], ALU.mult).then_inc(dBx_sb.sem, 1)
                    dve.wait_ge(*dBx_sb(b, n + 1))
                    if n >= 2:
                        dve.wait_ge(*hC_sb(b, n - 1))
                    if ps < 2:
                        dve.wait_ge(*dA_sb(b, n + 1))
                        s_, e_ = (0, 1), None
                        if ps == 0:
                            dve.tensor_tensor_scan(h, dA, dBx, 0.0, ALU.mult, ALU.add).then_inc(scanned.sem, 1)
                        else:
                            dve.tensor_tensor_scan(h[:, ::-1], dA[:, ::-1], dBx[:, ::-1], 0.0, ALU.mult,
                                                   ALU.add).then_inc(scanned.sem, 1)
                    else:
                        dve.wait_ge(*dA_sb(b, 32 + 2 * (n - 32) + 2))
                        for a_, e_ in ((0, L2), (L2, W3)):
                            dve.tensor_tensor_scan(h[:, a_:e_], dA[:, a_:e_], dBx[:, a_:e_], 0.0, ALU.mult,
                                                   ALU.add).then_inc(scanned.sem, 1)
                            rev = slice(e_ - 1, a_ - 1 if a_ else None, -1)
                            rev_o = slice(N + e_ - 1, N + a_ - 1, -1)
                            dve.tensor_tensor_scan(h[:, rev_o], dA[:, rev], dBx[:, rev], 0.0, ALU.mult,
                                                   ALU.add).then_inc(scanned.sem, 1)
                    if n == 17 + 1:
                        dve.wait_ge(*y_ps(b, 4))
                        dve.scalar_tensor_tensor(out=yv[:, 0, :], in0=f1[:, :], scalar=v("Dv", 0),
                                                 in1=PS[:, 0:2, :].rearrange("p a n -> p (a n)"),
                                                 op0=ALU.mult, op1=ALU.add).then_inc(y_sb.sem, 1)
                    if n == 33 + 1:
                        dve.wait_ge(*y_ps(b, 8))
                        dve.scalar_tensor_tensor(out=yv[:, 1, :], in0=f1[:, :], scalar=v("Dv", 1),
                                                 in1=PS[:, 0:2, :].rearrange("p a n -> p (a n)"),
                                                 op0=ALU.mult, op1=ALU.add).then_inc(y_sb.sem, 1)
                dve.wait_ge(*y_ps(b, 12))
                for d in range(2):
                    for s, a_, e_ in ((1, 0, L2), (2, L2, W3)):
                        dve.scalar_tensor_tensor(out=yv[:, 2, d * N + a_:d * N + e_], in0=f23[:, a_:e_],
                                                 scalar=v("Dv", s), in1=PS[:, d, a_:e_], op0=ALU.mult,
                                                 op1=ALU.add).then_inc(y_sb.sem, 1)
                for k in range(4):
                    w, ybuf, mb, vb = norm_job(k)
                    dve.wait_ge(*y_sb(b, 6))
                    dve.wait_ge(*lm_ps(b, k + 1))
                    src = PS[:, mb:mb + 2, :].rearrange("p a n -> p (a n)")[:, 0:w] if w > N else PS[:, mb, 0:w]
                    dve.tensor_tensor(ybuf, ybuf, src, ALU.subtract).then_inc(lm_d.sem, 1)
                for k in range(4):
                    w, ybuf, mb, vb = norm_job(k)
                    dve.wait_ge(*lv_rs(b, k + 1))
                    dve.wait_ge(*lm_d(b, k + 1))
                    dve.tensor_tensor(ybuf, ybuf, work[:, 4 + k, 0:w], ALU.mult).then_inc(ln_n.sem, 1)
                nl = [0]

                def chain(ins):
                    nl[0] += 1
                    ins.then_inc(levels.sem, 1)
                    dve.wait_ge(*levels(b, nl[0]))

                dve.wait_ge(*ln_n(b, 4))
                y1, y2, y3 = work[:, 9, :], work[:, 10, 0:L2], work[:, 10, L2:W3]
                chain(dve.tensor_scalar(y3, yv[:, 2, L2:W3], v("g", 2), bes[:, 2:3], ALU.mult, ALU.add))
                chain(dve.scalar_tensor_tensor(out=y3, in0=yv[:, 2, N + L2:N + W3], scalar=v("g", 2), in1=y3,
                                               op0=ALU.mult, op1=ALU.add))
                chain(dve.tensor_scalar(y2, yv[:, 2, 0:L2], v("g", 1), bes[:, 1:2], ALU.mult, ALU.add))
                chain(dve.scalar_tensor_tensor(out=y2, in0=yv[:, 2, N:N + L2], scalar=v("g", 1), in1=y2,
                                               op0=ALU.mult, op1=ALU.add))

                def up(fine, coarse, side):
                    fv = fine.rearrange("p (h i w j) -> p h i w j", i=2, w=side, j=2)
                    cv = coarse.rearrange("p (h w) -> p h w", w=side)
                    for i in range(2):
                        for j in range(2):
                            chain(dve.tensor_tensor(fv[:, :, i, :, j], fv[:, :, i, :, j], cv, ALU.add))

                up(y2, y3, WW // 4)
                chain(dve.tensor_scalar(y1, yv[:, 0, :], v("g", 0), bes[:, 0:1], ALU.mult, ALU.add))
                chain(dve.scalar_tensor_tensor(out=y1, in0=yv[:, 1, :], scalar=v("g", 1), in1=y1,
                                               op0=ALU.mult, op1=ALU.add))
                up(y1, y2, WW // 2)
                dve.wait_ge(*z_sb(b, 2))
                dve.tensor_tensor(work[:, 11, :], y1, work[:, 8, :], ALU.mult).then_inc(gated.sem, 1)
                for m in range(CT):
                    for c in range(NC):
                        n = 2 * m + c
                        cs = slice(c * N, c * N + N)
                        dve.wait_ge(*o_ps(b, n + 1))
                        dve.scalar_tensor_tensor(out=xr[:, m, cs], in0=PS[:, n, :], scalar=v("out_b", m),
                                                 in1=xin[:, m, cs], op0=ALU.add, op1=ALU.add).then_inc(x_new.sem, 1)

            def chan_norm(b, s, X):
                for c in range(NC):
                    n = NC * s + c
                    dve.wait_ge(*cm_ps(b, n + 1))
                    for t in range(CT):
                        cs = slice(c * N, c * N + N)
                        dve.tensor_tensor(X[:, t, cs], X[:, t, cs], PS[:, c, :], ALU.subtract).then_inc(cm_d.sem, 1)
                for c in range(NC):
                    n = NC * s + c
                    dve.wait_ge(*cv_rs(b, n + 1))
                    dve.wait_ge(*cm_d(b, 2 * n + 2))
                    for t in range(CT):
                        cs = slice(c * N, c * N + N)
                        dve.tensor_tensor(X[:, t, cs], X[:, t, cs], rstd[:, c, :], ALU.mult).then_inc(cn_n.sem, 1)

            def attention(b, a):
                bq = ("qkv_b1", "qkv_b3")[a]
                for g in range(GROUPS):
                    for kind in range(2):
                        n = 2 * g + kind
                        dve.wait_ge(*qk_head(b, 4 * a + n + 1))
                        src = PS[:, 2 * n:2 * n + 2, :].rearrange("p a n -> p (a n)")
                        dve.scalar_tensor_tensor(out=piece[:, kind, 1, :], in0=src, scalar=v(bq, 2 * kind + g),
                                                 in1=piece[:, kind, 0, :].bitcast(F32), op0=ALU.add,
                                                 op1=ALU.subtract).then_inc(qk_rest.sem, 1)

                def row_max(n, slot):
                    dve.wait_ge(*r_ps(b, a * HEADS * KT + n + 1))
                    if n == GH * KT:
                        dve.wait_ge(*mt_ps(b, 2 * a + 1))
                    dve.tensor_reduce(mx[:, n % (GH * KT):n % (GH * KT) + 1], PS[:, slot:slot + 2, :], AX.XY,
                                      ALU.max).then_inc(r_max.sem, 1)

                def neg_max(g):
                    dve.wait_ge(*nm_head(b, 2 * a + g + 1))
                    dve.scalar_tensor_tensor(out=nm[:, 1, :], in0=PS[0:GH * KT, 6, 0:P], scalar=-1.0,
                                             in1=nm[:, 0, :].bitcast(F32), op0=ALU.mult,
                                             op1=ALU.subtract).then_inc(nm_rest.sem, 1)

                for n in range(GH * KT):
                    row_max(n, 2 + 2 * (n % 3))
                neg_max(0)
                for g in range(GROUPS):
                    for c in range(NC):
                        if g == 0:
                            for kt in range(2 * KT):
                                row_max(GH * KT + c * 2 * KT + kt, 6)
                            if c == NC - 1:
                                neg_max(1)
                        j = (a * GROUPS + g) * NC + c
                        cs = slice(c * N, c * N + N)
                        dve.wait_ge(*den_rc(b, j + 1))
                        dve.tensor_tensor(oT[:, g, cs], PS[:, 0, :], lr[:, 1, :], ALU.mult).then_inc(o_raw.sem, 1)
                        dve.wait_ge(*o_raw(b, j + 1))
                        dve.tensor_scalar(oT[:, g, cs], oT[:, g, cs], v(bq, 4 + g), None, ALU.add).then_inc(o_sb.sem, 1)

            def residual(b, first, bias, other):
                for m in range(CT):
                    for c in range(NC):
                        n = 2 * m + c
                        cs = slice(c * N, c * N + N)
                        dve.wait_ge(*o_ps(b, first + n + 1))
                        dve.scalar_tensor_tensor(out=xr[:, m, cs], in0=PS[:, n, :], scalar=v(bias, m),
                                                 in1=xr[:, m, cs], op0=ALU.add, op1=ALU.add).then_inc(x_new.sem, 1)

            with dve.Fori(0, B) as b:
                dve.wait_ge(*xin_here(b, 16))
                group_norm(b, 0, xin)
                block0(b)
                dve.wait_ge(*x_new(b, 4))
                group_norm(b, 1, xr)
                attention(b, 0)
                residual(b, 4, "proj_b", None)
                dve.wait_ge(*x_new(b, 8))
                group_norm(b, 2, xr)
                for m in range(CT):
                    for c in range(NC):
                        n = 2 * m + c
                        cs = slice(c * N, c * N + N)
                        dve.wait_ge(*wo_sb(b, n + 1))
                        dve.tensor_tensor(xr[:, m, cs], xr[:, m, cs], rl[:, n, :], ALU.add).then_inc(x_new.sem, 1)
                dve.wait_ge(*x_new(b, 12))
                group_norm(b, 3, xr)
                chan_norm(b, 0, xg)
                for t in range(CT):
                    dve.wait_ge(*cn_x(b, 4))
                    dve.tensor_tensor(xr[:, t, :], xr[:, t, :], xg[:, t, :], ALU.add).then_inc(x3n.sem, 1)
                attention(b, 1)
                dve.wait_ge(*o_sb(b, 8))
                chan_norm(b, 1, oT)
                dve.wait_ge(*x3n(b, 2))
                residual(b, 12, "out3_b", None)
                dve.wait_ge(*stored(b, 16))

        @block.tensor
        def _(pe):
            pe.wait_ge(loaded, NLOAD)
            pe.wait_ge(built, NBUILT)
            for s in range(3):
                pe.matmul(PS[:, s, 0:P], W8[:, s, 0, :], W8[:, s, 1, :], start=True, stop=True).then_inc(folded, 1)
            pe.wait_ge(prepared, NPREP)

            def group_norm(b, s):
                pe.wait_ge(*gn_sum(b, s + 1))
                pe.matmul(PS[:, 7, 0:2], g8[:, :], msum, start=True, stop=True).then_inc(gn_gm.sem, 1)
                pe.wait_ge(*gn_m2(b, s + 1))
                pe.matmul(PS[:, 6, 0:2], g8[:, :], m2, start=True, stop=True).then_inc(gn_gv.sem, 1)
                pe.wait_ge(*gn_xa(b, s + 1))
                pe.wait_ge(*gn_xb(b, s + 1))

            def linear(bank, w, m, X, c, done):
                for k in range(CT):
                    ins = pe.matmul(PS[:, bank, :], w[:, k, m * P:m * P + P], X[:, k, c * N:c * N + N],
                                    start=(k == 0), stop=(k == CT - 1))
                if done is not None:
                    ins.then_inc(done.sem, 1)

            def block0(b):
                for c in range(NC):
                    linear(c, w_in, 0, xg, c, xp_ps)
                for c in range(NC):
                    pe.wait_ge(*xp_sb(b, c + 1))
                    pe.matmul(PS[:, 2 + c, :], w_c1, yv[:, 0, c * N:c * N + N], start=True, stop=True).then_inc(f1_ps.sem, 1)
                pe.wait_ge(*f1_sb(b, 2))
                v1 = f1[:, :].rearrange("p (h i w j) -> p h i w j", i=2, w=WW // 2, j=2)
                for k in range(4):
                    ins = pe.matmul(PS[:, 4, 0:L2], w_c2[:, k, :], v1[:, :, k // 2, :, k % 2], start=(k == 0), stop=(k == 3))
                ins.then_inc(f2_ps.sem, 1)

                def coeff(ps, bank, w, done):
                    if ps < 2:
                        for c in range(NC):
                            ins = pe.matmul(PS[:, bank + c, :], w[:, ps, :], f1[:, c * N:c * N + N], start=True, stop=True)
                    else:
                        pe.matmul(PS[:, bank, 0:L2], w[:, 1, :], f23[:, 0:L2], start=True, stop=True)
                        ins = pe.matmul(PS[:, bank, L2:W3], w[:, 2, :], f23[:, L2:W3], start=True, stop=True)
                    ins.then_inc(done.sem, 1)

                coeff(0, 0, Wd, pre_ps)
                coeff(0, 2, w_xb, brep_ps)
                pe.wait_ge(*f2_sb(b, 1))
                v2 = f23[:, 0:L2].rearrange("p (h i w j) -> p h i w j", i=2, w=WW // 4, j=2)
                for k in range(4):
                    ins = pe.matmul(PS[:, 5, 0:L3], w_c3[:, k, :], v2[:, :, k // 2, :, k % 2], start=(k == 0), stop=(k == 3))
                ins.then_inc(f3_ps.sem, 1)
                coeff(1, 6, Wd, pre_ps)
                pe.wait_ge(*f3_sb(b, 1))
                coeff(0, 4, w_xc, crep_ps)
                pe.wait_ge(*sp_abs(b, 1))
                pe.wait_ge(*sp_pos(b, 1))
                coeff(1, 0, w_xb, brep_ps)
                pe.wait_ge(*brep_sb(b, 1))
                coeff(1, 2, w_xc, crep_ps)
                pe.wait_ge(*crep_sb(b, 1))
                coeff(2, 4, Wd, pre_ps)
                pe.wait_ge(*sp_abs(b, 2))
                pe.wait_ge(*sp_pos(b, 2))
                coeff(2, 6, w_xb, brep_ps)
                pe.wait_ge(*brep_sb(b, 2))
                coeff(2, 0, w_xc, crep_ps)

                def sum_states(q):
                    ps = q // 4
                    pe.wait_ge(*hC_sb(b, 4 * q + 4))
                    if q == 4:
                        pe.wait_ge(*y_sb(b, 1))
                    if q == 8:
                        pe.wait_ge(*y_sb(b, 2))
                    for c in range(NC):
                        for j in range(4):
                            hc = work[:, 6 + (4 * q + j) % 6, :]
                            src = hc[:, c * N:c * N + N] if ps < 2 else hc[:, c * N:c * N + W3]
                            ins = pe.matmul(PS[32 * j:32 * j + 32, c, 0:N if ps < 2 else W3], ysel[:, q % 4, :], src,
                                            start=(q % 4 == 0), stop=(q % 4 == 3), skip_group_check=True)
                    ins.then_inc(y_ps.sem, 1)

                pe.wait_ge(*rests_in(b, 12))
                pe.wait_ge(*crep_sb(b, 3))
                for n in range(3 * SG):
                    ps, at, w = n // SG, PASS_AT[n // SG], PASS_W[n // SG]
                    g = scan_group(n)
                    for kind, (stk, done) in enumerate(((dstk, d_ps), (ustk, u_ps))):
                        job = 2 * n + kind
                        slot = 2 + 2 * (job % 3)
                        if job >= 3:
                            prev = job - 3
                            if prev % 2 == 0:
                                pe.wait_ge(*dA_sb(b, decays(prev // 2)))
                            else:
                                pe.wait_ge(*dBx_sb(b, prev // 2 + 1))
                        for c in range((w + N - 1) // N):
                            wc = min(N, w - c * N)
                            ins = pe.matmul(PS[:, slot + c, 0:wc], sel[:, g % 8, :], stk[:, g // 8, at + c * N:at + c * N + wc],
                                            start=True, stop=True)
                        ins.then_inc(done.sem, 1)
                    if n >= 5 and n % 4 == 1:
                        sum_states((n - 5) // 4)
                sum_states(11)
                pe.wait_ge(*y_sb(b, 6))
                for k in range(4):
                    w, ybuf, mb, vb = norm_job(k)
                    for c in range((w + N - 1) // N):
                        wc = min(N, w - c * N)
                        ins = pe.matmul(PS[:, mb + c, 0:wc], mean128[:, :], ybuf[:, c * N:c * N + wc], start=True, stop=True)
                    ins.then_inc(lm_ps.sem, 1)
                for k in range(4):
                    w, ybuf, mb, vb = norm_job(k)
                    pe.wait_ge(*lm_sq(b, k + 1))
                    if k == 1:
                        pe.wait_ge(*lm_d(b, 2))
                    for c in range((w + N - 1) // N):
                        wc = min(N, w - c * N)
                        ins = pe.matmul(PS[:, vb + c, 0:wc], mean128[:, :], work[:, k, c * N:c * N + wc], start=True, stop=True)
                    ins.then_inc(lv_ps.sem, 1)
                for c in range(NC):
                    linear(6 + c, w_in, 1, xg, c, z_ps)
                pe.wait_ge(*gated(b, 1))
                for m in range(CT):
                    for c in range(NC):
                        pe.matmul(PS[:, 2 * m + c, :], w_out[:, m * P:m * P + P], work[:, 11, c * N:c * N + N],
                                  start=True, stop=True).then_inc(o_ps.sem, 1)

            def chan_norm(b, s, X):
                for c in range(NC):
                    for t in range(CT):
                        ins = pe.matmul(PS[:, c, :], mean256[:, :], X[:, t, c * N:c * N + N], start=(t == 0), stop=(t == CT - 1))
                    ins.then_inc(cm_ps.sem, 1)
                for c in range(NC):
                    n = NC * s + c
                    pe.wait_ge(*cm_sq(b, 2 * n + 2))
                    for t in range(CT):
                        ins = pe.matmul(PS[:, 2 + c, :], mean256[:, :], sq[:, 2 * c + t, :], start=(t == 0), stop=(t == CT - 1))
                    ins.then_inc(cv_ps.sem, 1)

            def attention(b, a, X):
                wq, kd = w_qkv[a], 96
                for g in range(GROUPS):
                    for kind in range(2):
                        for c in range(NC):
                            linear(2 * (2 * g + kind) + c, wq, 2 * kind + g, X, c, qk_ps if c == NC - 1 else None)
                for q in range(2):
                    pe.wait_ge(*qk_rest(b, 4 * a + q + 1))
                    for i in range(4):
                        tt = 4 * q + i
                        for k in range(CT):
                            ins = pe.matmul(PS[:, 2 * q + i // 2, (i % 2) * C:(i % 2) * C + C], X[:, k, tt * P:tt * P + P],
                                            wq[:, k, 2 * C:3 * C], start=(k == 0), stop=(k == CT - 1))
                    ins.then_inc(v_ps.sem, 1)

                def row_scores(n, slot):
                    h, qt = n // KT, n % KT
                    for c in range(NC):
                        ins = pe.matmul(PS[:, slot + c, :], QS[0:kd, h, qt * P:qt * P + P], KS[0:kd, h, c * N:c * N + N],
                                        start=True, stop=True)
                    ins.then_inc(r_ps.sem, 1)

                def turn_max(g):
                    pe.wait_ge(*r_max(b, a * HEADS * KT + (g + 1) * GH * KT))
                    if g == 1:
                        pe.wait_ge(*nm_rest(b, 2 * a + 1))
                    pe.transpose(PS[0:GH * KT, 6, 0:P], mx[:, :], ident[:, :]).then_inc(mt_ps.sem, 1)

                pe.wait_ge(*v_sb(b, 2 * a + 2))
                pe.wait_ge(*qk_rest(b, 4 * a + 4))
                pe.wait_ge(*stackedq[0](b, (a + 1) * 192))
                pe.wait_ge(*stackedk[0](b, (a + 1) * 192))
                for n in range(GH * KT):
                    if n >= 3:
                        pe.wait_ge(*r_max(b, a * HEADS * KT + n - 2))
                    row_scores(n, 2 + 2 * (n % 3))
                turn_max(0)
                steps = [(g, c, kt) for g in range(GROUPS) for c in range(NC) for kt in range(KT)]
                base = a * len(steps)

                def values(i):
                    g, c, kt = steps[i]
                    pe.wait_ge(*p_sb(b, 2 * (base + i) + 2))
                    if kt == 0 and i >= KT:
                        pe.wait_ge(*o_raw(b, (base + i) // KT))
                    for j in range(GH):
                        h = GH * g + j
                        pe.matmul(PS[32 * j:32 * j + 32, 0, :], Vt[:, kt, DH * h:DH * h + DH], PT[:, (base + i) % 3, j, :],
                                  start=(kt == 0), stop=(kt == KT - 1), skip_group_check=True)
                    for j in range(GH):
                        ins = pe.matmul(PS[32 * j:32 * j + 32, 1, :], ones32[:, :], PT[:, (base + i) % 3, j, :],
                                        start=(kt == 0), stop=(kt == KT - 1), skip_group_check=True)
                    ins.then_inc(pv_ps.sem, 1)

                pe.wait_ge(*nm_in[0](b, (a + 1) * 32))
                for i, (g, c, kt) in enumerate(steps):
                    if i == NC * KT:
                        turn_max(1)
                        values(i - 1)
                        pe.wait_ge(*nm_in[1](b, (a + 1) * 32))
                    for pr in range(2):
                        if i >= 1:
                            pe.wait_ge(*p_sb(b, 2 * (base + i - 1) + pr + 1))
                        for jj in range(2):
                            h = GH * g + 2 * pr + jj
                            ins = pe.matmul(PS[:, 2 + 2 * pr + jj, :], KS[:, h, kt * P:kt * P + P], QS[:, h, c * N:c * N + N],
                                            start=True, stop=True)
                        ins.then_inc(s_ps.sem, 1)
                    if i >= 1 and i != NC * KT:
                        values(i - 1)
                    if g == 0:
                        if i == 0:
                            pe.wait_ge(*stackedq[1](b, (a + 1) * 192))
                            pe.wait_ge(*stackedk[1](b, (a + 1) * 192))
                        for r in range(2):
                            n = GH * KT + 2 * i + r
                            pe.wait_ge(*(r_max(b, a * HEADS * KT + n) if n > GH * KT else nm_rest(b, 2 * a + 1)))
                            row_scores(n, 6)
                values(len(steps) - 1)

            def project(b, a, X):
                for m in range(CT):
                    for c in range(NC):
                        if m == 0 and c == 0:
                            pe.wait_ge(*o_raw(b, 4 * a + 4))
                        linear(2 * m + c, w_proj[a], m, X, c, o_ps)

            def block2(b):
                for t in range(2):
                    for c in range(NC):
                        n = 2 * t + c
                        top = c * (HH // NC)
                        for hh, (ky, kx), (y0, y1, x0, x1), first, last in windows(t, c):
                            dy, dx = (ky - 1) * RATES[2 * t + hh], (kx - 1) * RATES[2 * t + hh]
                            dst = PS[64 * hh:64 * hh + 64, n, :].rearrange("p (h w) -> p h w", w=WW)[:, y0 - top:y1 - top, x0:x1]
                            src = xg[:, t, :].rearrange("p (h w) -> p h w", w=WW)[:, y0 + dy:y1 + dy, x0 + dx:x1 + dx]
                            ins = pe.matmul(dst, DW[:, t, ky * 3 + kx, 64 * hh:64 * hh + 64], src,
                                            start=first, stop=last, skip_group_check=True)
                        ins.then_inc(dw_ps.sem, 1)
                for m in range(2):
                    for c in range(NC):
                        pe.wait_ge(*dw_sb(b, 4))
                        linear(4 + 2 * m + c, MX, m, br, c, mix_ps)
                for m in range(2):
                    for c in range(NC):
                        pe.wait_ge(*mix_sb(b, 4))
                        linear(2 * m + c, w_o, m, zm, c, o_ps)

            with pe.Fori(0, B) as b:
                group_norm(b, 0)
                block0(b)
                group_norm(b, 1)
                attention(b, 0, xg)
                pe.wait_ge(*o_sb(b, 4))
                project(b, 0, oT)
                group_norm(b, 2)
                block2(b)
                group_norm(b, 3)
                chan_norm(b, 0, xg)
                pe.wait_ge(*cn_x(b, 4))
                attention(b, 1, xg)
                pe.wait_ge(*o_sb(b, 8))
                chan_norm(b, 1, oT)
                pe.wait_ge(*cn_x(b, 8))
                project(b, 1, oT)
                pe.wait_ge(*x_new(b, 16))


def scan_group(n):
    i, j = (n % SG) // 4, n % 4
    return 4 * j + i


def scans(n):
    return n + 1 if n < 32 else 32 + 4 * (n - 32) + 4


def decays(n):
    return n + 1 if n < 32 else 32 + 2 * (n - 32) + 2


def windows(t, c):
    top, todo = c * (HH // NC), []
    for ky, kx in TAPS:
        for hh in range(2):
            dy, dx = (ky - 1) * RATES[2 * t + hh], (kx - 1) * RATES[2 * t + hh]
            y0, y1 = max(top, -dy), min(top + HH // NC, HH - dy)
            x0, x1 = max(0, -dx), min(WW, WW - dx)
            if y0 < y1 and x0 < x1:
                todo.append((hh, (ky, kx), (y0, y1, x0, x1)))
    ends = {hh: max(i for i, w in enumerate(todo) if w[0] == hh) for hh in range(2)}
    return [(*w, w[1] == (1, 1), i == ends[w[0]]) for i, w in enumerate(todo)]


def kernel(**inputs):
    import numpy as np
    import concourse.bacc as bacc
    from concourse.bass_utils import run_bass_kernel_spmd

    a = {k: np.asarray(t) for k, t in inputs.items()}
    two = lambda t: t.reshape(2, P, -1).transpose(1, 0, 2)
    col = lambda t: np.ascontiguousarray(t.reshape(-1, P).T)
    z0, z1, z2, z3 = (lambda n, i=i: a[f"L{i}_conv_{n}"] for i in range(4))

    taps = lambda w: w.transpose(1, 2, 3, 0).reshape(P, 4 * P)
    part = {
        "in_w": two(z0("in_w").T), "c1": z0("c1_w").T, "c2": taps(z0("c2_w")), "c3": taps(z0("c3_w")),
        "xb": np.concatenate([np.tile(z0(f"xw{s}")[R_DT:R_DT + NST].T, (1, DPG)) for s in (1, 2, 3)], 1),
        "xc": np.concatenate([np.tile(z0(f"xw{s}")[R_DT + NST:].T, (1, DPG)) for s in (1, 2, 3)], 1),
        "out": z0("out_w").T,
        "qkv1": two(z1("qkv_w").T), "proj1": two(z1("proj_w").T),
        "wo": two(z2("wo")[:, :, 0, 0].reshape(C, C // 4, 4).transpose(2, 1, 0).reshape(C, C)),
        "qkv3": two(z3("w_qkv")), "out3": two(z3("w_out")),
    }
    wpack = np.ascontiguousarray(np.concatenate([part[n].reshape(P, w) for n, w in WSEC], 1))

    def bn(n_dw, n_s, n_o):
        return np.concatenate([col(z2(n_dw).reshape(-1)), col(np.repeat(z2(n_s), C // 4)), col(z2(n_o))], 1)

    ws = z2("ws")[:, :, 0, 0]
    vec = {
        "in_b": col(z0("in_b")), "c1_b": col(z0("c1_b")), "c2_b": col(z0("c2_b")), "c3_b": col(z0("c3_b")),
        "out_b": col(z0("out_b")),
        "dtb": np.stack([z0(f"dtb{s}") for s in (1, 2, 3)], 1), "Dv": np.stack([z0(f"Dv{s}") for s in (1, 2, 3)], 1),
        "g": np.stack([z0(f"g{s}") for s in (1, 2, 3)], 1), "be": np.stack([z0(f"be{s}") for s in (1, 2, 3)], 1),
        "Al": np.concatenate([z0(f"Al{s}").reshape(SG, P).T for s in (1, 2, 3)], 1),
        "qkv_b1": col(z1("qkv_b")), "proj_b": col(z1("proj_b")),
        "bn_b": bn("bdw", "bs", "bo"), "bn_g": bn("gdw", "gs", "go"), "bn_be": bn("bedw", "bes", "beo"),
        "bn_m": bn("mdw", "ms", "mo"), "bn_v": bn("vdw", "vs", "vo"),
        "wdw": z2("wdw").reshape(2, P, 9).transpose(1, 0, 2),
        "ws": np.repeat(ws.T.reshape(2, 2, 4).transpose(1, 0, 2), C // 4, 0),
        "qkv_b3": col(z3("b_qkv")), "out3_b": col(z3("b_out")), "gamma1": col(z3("gamma1")),
        "beta1": col(z3("beta1")), "gamma2": col(z3("gamma2")), "beta2": col(z3("beta2")),
    }
    vpack = np.ascontiguousarray(np.concatenate([vec[n].reshape(P, w) for n, w in VSEC], 1))
    w8 = np.ascontiguousarray(np.stack([np.stack([z0(f"xw{s}")[:R_DT], z0(f"dtw{s}").T], 1) for s in (1, 2, 3)], 1))

    arrays = {"x": np.ascontiguousarray(a["x"].reshape(B, C, L)), "wpack": wpack, "vpack": vpack, "w8": w8}
    nc = bacc.Bacc("TRN2", target_bir_lowering=False, num_devices=1)
    args = [nc.dram_tensor(n, t.shape, F32, kind="ExternalInput").ap() for n, t in arrays.items()]
    out = nc.dram_tensor("out", (B, C, L), F32, kind="ExternalOutput").ap()
    build(nc, *args, out)
    r = run_bass_kernel_spmd(nc, [arrays], core_ids=[0])
    return r.results[0]["out"].reshape(B, C, HH, WW)
```

```python
from contextlib import ExitStack

import concourse.bass as bass
from concourse import mybir

F32 = mybir.dt.float32
F32R = mybir.dt.float32r
ACT = mybir.ActivationFunctionType
ALU = mybir.AluOpType
AX = mybir.AxisListType

P = 128
B, C, HH, WW = 8, 256, 32, 32
L = HH * WW
CT = C // P
N = 512
NC = L // N
HEADS, DH = 8, 32
GH = 4
GROUPS = HEADS // GH
KT = L // P
D_IN, NST, R_DT = 128, 16, 8
DPG = P // NST
SG = D_IN // DPG
L2, L3 = L // 4, L // 16
W3 = L2 + L3
COLS = 2 * L + W3
PASS_AT = (0, L, 2 * L)
PASS_W = (L, L, W3)
RATES = (1, 6, 12, 18)
TAPS = [(1, 1)] + [(y, x) for y in range(3) for x in range(3) if (y, x) != (1, 1)]
SCALE = float(DH) ** -0.5
PHASES = GROUPS * NC
ROWS = (3, 3, 2, 3, 3, 2, 0, 0)
TURN_AT = 6
PHASE_ROWS = sum(ROWS)
POOL_SUMS = (0, 1, 2, 4, 6)
DVE_SUMS = (0, 1, 2, 3, 4, 5, 6)
SMALL_U = 1.0 / 128

WSEC = [("in_w", 2 * 256), ("c1", 128), ("c2", 4 * 128), ("c3", 4 * 128),
        ("xb", 3 * 128), ("xc", 3 * 128), ("out", 256),
        ("qkv1", 2 * 768), ("proj1", 2 * 256), ("wo", 2 * 256), ("qkv3", 2 * 768), ("out3", 2 * 256)]
WOFF, WTOT = {}, 0
for _n, _w in WSEC:
    WOFF[_n] = WTOT
    WTOT += _w

VSEC = [("in_b", 2), ("c1_b", 1), ("c2_b", 1), ("c3_b", 1), ("out_b", 2), ("dtb", 3), ("Dv", 3),
        ("g", 3), ("be", 3), ("Al", 3 * SG), ("qkv_b1", 6), ("proj_b", 2),
        ("bn_b", 6), ("bn_g", 6), ("bn_be", 6), ("bn_m", 6), ("bn_v", 6), ("wdw", 18), ("ws", 8),
        ("qkv_b3", 6), ("out3_b", 2), ("gamma1", 2), ("beta1", 2), ("gamma2", 2), ("beta2", 2)]
VOFF, VTOT = {}, 0
for _n, _w in VSEC:
    VOFF[_n] = VTOT
    VTOT += _w


class Signal:

    def __init__(self, sem, per):
        self.sem, self.per = sem, per

    def __call__(self, b, k):
        return self.sem, b * self.per + k


def build(nc, x, wpack, vpack, w8, out):
    with ExitStack() as ctx:
        sb = lambda name, shape, dt=F32: ctx.enter_context(nc.sbuf_tensor(name, shape, dt))

        def sig(name, per):
            return Signal(ctx.enter_context(nc.semaphore(name)), per)

        sem = lambda name: ctx.enter_context(nc.semaphore(name))

        xin = sb("xin", [P, CT, L])
        xr = sb("xr", [P, CT, L])
        xg = sb("xg", [P, CT, L])
        W = sb("W", [P, WTOT])
        V = sb("V", [P, VTOT])
        W8 = sb("W8", [R_DT, 3, 2, P])
        Wd = sb("Wd", [P, 3, P])
        ident = sb("ident", [P, P])
        id2 = sb("id2", [P, 64])
        g8 = sb("g8", [P, P])
        mean128 = sb("mean128", [P, P])
        mean256 = sb("mean256", [P, P])
        ones32 = sb("ones32", [P, 32])
        e8 = sb("e8", [P, DPG])
        ysel = sb("ysel", [P, 4, 32])
        sel = sb("sel", [P, 8, P], F32R)
        DW = sb("DW", [P, 2, 9, P])
        MX = sb("MX", [P, 2, 256])
        Aneg = sb("Aneg", [P, 3 * SG])
        binv = sb("binv", [P, 6])
        bbias = sb("bbias", [P, 6])
        bes = sb("bes", [P, 3])
        eps = sb("eps", [P, 1])
        mhalf = sb("mhalf", [P, 1])
        small = sb("small", [P, 64])
        st = small[:, 0:24].rearrange("p (t c s) -> p t c s", t=2, c=2)
        msum = small[:, 24:26]
        dev = small[:, 46:54].rearrange("p (t q) -> p t q", t=2)
        dd = small[:, 54:62].rearrange("p (t q) -> p t q", t=2)
        m2 = small[:, 30:32]
        lnv = small[:, 32:34]
        rs = small[:, 34:36]
        sh = small[:, 36:38]
        tmp6 = small[:, 40:46]
        PS = ctx.enter_context(nc.psum_tensor("PS", [P, 8, N], F32))

        with ExitStack() as over:
            so = lambda name, shape, dt=F32: over.enter_context(nc.sbuf_tensor(name, shape, dt))
            Brep = so("Brep", [P, COLS])
            Crep = so("Crep", [P, COLS])
            work = so("work", [P, 12, L])
            yv = so("yv", [P, 3, L])
            f1 = so("f1", [P, L])
            f23 = so("f23", [P, W3])
            dstk = so("dstk", [P, 2, COLS], F32R)
            ustk = so("ustk", [P, 2, COLS], F32R)
        with ExitStack() as over:
            so = lambda name, shape, dt=F32: over.enter_context(nc.sbuf_tensor(name, shape, dt))
            QS = so("QS", [98, NC, HEADS, N], F32R)
            KS = so("KS", [98, HEADS, L], F32R)
            piece = so("piece", [P, 2, 2, L], F32R)
            Vt = so("Vt", [P, KT, C])
            PT = so("PT", [P, 3, GH, N])
            oT = so("oT", [P, CT, L])
            lr = so("lr", [P, 2, N])
            mx = so("mx", [P, NC, PHASE_ROWS])
            mboth = so("mboth", [P, PHASE_ROWS])
            nm = so("nm", [PHASE_ROWS, 2, P], F32R)
        with ExitStack() as over:
            so = lambda name, shape, dt=F32: over.enter_context(nc.sbuf_tensor(name, shape, dt))
            br = so("br", [P, 2, L])
            zm = so("zm", [P, 2, L])
            rl = so("rl", [P, 4, N])
        acc = piece.rearrange("p a b n -> p (a b n)").bitcast(F32).rearrange("p (s j n) -> p s j n", s=2, j=GH)
        sel32 = work[:, 0, :].rearrange("p (g m) -> p g m", g=8)
        sq = PT[:, 0, :, :]
        rstd = PT[:, 1, :, :]

        w_in = W[:, WOFF["in_w"]:WOFF["in_w"] + 512].rearrange("p (k m) -> p k m", k=2)
        w_c1 = W[:, WOFF["c1"]:WOFF["c1"] + 128]
        w_c2 = W[:, WOFF["c2"]:WOFF["c2"] + 512].rearrange("p (k m) -> p k m", k=4)
        w_c3 = W[:, WOFF["c3"]:WOFF["c3"] + 512].rearrange("p (k m) -> p k m", k=4)
        w_xb = W[:, WOFF["xb"]:WOFF["xb"] + 384].rearrange("p (s m) -> p s m", s=3)
        w_xc = W[:, WOFF["xc"]:WOFF["xc"] + 384].rearrange("p (s m) -> p s m", s=3)
        w_out = W[:, WOFF["out"]:WOFF["out"] + 256]
        w_qkv = [W[:, WOFF[n]:WOFF[n] + 1536].rearrange("p (k m) -> p k m", k=2) for n in ("qkv1", "qkv3")]
        w_proj = [W[:, WOFF[n]:WOFF[n] + 512].rearrange("p (k m) -> p k m", k=2) for n in ("proj1", "out3")]
        w_o = W[:, WOFF["wo"]:WOFF["wo"] + 512].rearrange("p (k m) -> p k m", k=2)
        v = lambda name, i=0, n=1: V[:, VOFF[name] + i:VOFF[name] + i + n]

        loaded = sem("loaded")
        built = sem("built")
        folded = sem("folded")
        prepared = sem("prepared")
        logged = sem("logged")

        xin_here = sig("xin_here", 16)
        stored = sig("stored", 16)
        gn_st, gn_sum, gn_dev, gn_dd, gn_q = sig("gn_st", 16), sig("gn_sum", 4), sig("gn_dev", 4), sig("gn_dd", 4), sig("gn_q", 4)
        gn_gm, gn_m2, gn_gv = sig("gn_gm", 4), sig("gn_m2", 4), sig("gn_gv", 4)
        gn_ln, gn_rs, gn_sh = sig("gn_ln", 4), sig("gn_rs", 4), sig("gn_sh", 4)
        gn_xa, gn_xb = sig("gn_xa", 4), sig("gn_xb", 4)
        xp_ps, xp_sb = sig("xp_ps", 2), sig("xp_sb", 2)
        f1_ps, f1_sb = sig("f1_ps", 2), sig("f1_sb", 2)
        f2_ps, f2_sb = sig("f2_ps", 1), sig("f2_sb", 1)
        f3_ps, f3_sb = sig("f3_ps", 1), sig("f3_sb", 1)
        pre_ps, brep_ps, crep_ps = sig("pre_ps", 3), sig("brep_ps", 3), sig("crep_ps", 3)
        brep_sb, crep_sb = sig("brep_sb", 3), sig("crep_sb", 3)
        sp_abs, sp_pos, sp_exp, sp_one = sig("sp_abs", 4), sig("sp_pos", 4), sig("sp_exp", 3), sig("sp_one", 3)
        sp_ln, sp_cut, sp_sum = sig("sp_ln", 3), sig("sp_cut", 3), sig("sp_sum", 3)
        sp_q, sp_qu, sp_poly, sp_big, sp_one_of = (sig(n, 3) for n in ("sp_q", "sp_qu", "sp_poly", "sp_big", "sp_one_of"))
        step, stepx = sig("step", 3), sig("stepx", 3)
        heads_in, rests_in = sig("heads_in", 12), sig("rests_in", 12)
        d_ps, u_ps = sig("d_ps", 48), sig("u_ps", 48)
        dA_sb, dBx_sb = sig("dA_sb", 64), sig("dBx_sb", 48)
        scanned, hC_sb, y_ps = sig("scanned", 96), sig("hC_sb", 48), sig("y_ps", 12)
        y_sb = sig("y_sb", 6)
        lm_ps, lm_d, lm_sq, lv_ps = sig("lm_ps", 4), sig("lm_d", 4), sig("lm_sq", 4), sig("lv_ps", 4)
        lv_ln, lv_rs, ln_n = sig("lv_ln", 4), sig("lv_rs", 4), sig("ln_n", 4)
        levels = sig("levels", 14)
        z_ps, z_sb, gated = sig("z_ps", 2), sig("z_sb", 2), sig("gated", 1)
        o_ps, x_new = sig("o_ps", 16), sig("x_new", 16)
        qk_ps, qk_head, qk_rest = sig("qk_ps", 8), sig("qk_head", 8), sig("qk_rest", 8)
        stackedq = [sig(f"stackedq{g}", 2 * 12 * 16) for g in range(GROUPS)]
        stackedk = [[sig(f"stackedk{g}{j}", 2 * 3 * 16) for j in range(GH)] for g in range(GROUPS)]
        ones_in = sig("ones_in", 1)
        v_ps, v_sb = sig("v_ps", 4), sig("v_sb", 4)
        r_ps, r_max = sig("r_ps", 2 * HEADS * KT * NC), sig("r_max", 2 * HEADS * KT * NC)
        m_both = sig("m_both", 2 * PHASES)
        mt_ps, nm_head, nm_rest = (sig(n, 2 * PHASES) for n in ("mt_ps", "nm_head", "nm_rest"))
        nm_in = sig("nm_in", 2 * PHASES * 2 * 16)
        sum_pool = sig("sum_pool", 2 * (PHASES - 1) * (len(POOL_SUMS) - 1))
        sum_dve = sig("sum_dve", 2 * (len(DVE_SUMS) - 1))
        s_ps, p_sb = sig("s_ps", 128), sig("p_sb", 128)
        pv_ps, den_ln, den_rc = sig("pv_ps", 64), sig("den_ln", 8), sig("den_rc", 8)
        o_raw, o_sb = sig("o_raw", 8), sig("o_sb", 8)
        cm_ps, cm_d, cm_sq, cv_ps = sig("cm_ps", 4), sig("cm_d", 8), sig("cm_sq", 8), sig("cv_ps", 4)
        cv_ln, cv_rs, cn_n, cn_x = sig("cv_ln", 4), sig("cv_rs", 4), sig("cn_n", 8), sig("cn_x", 8)
        x3n = sig("x3n", 2)
        dw_ps, dw_sb, mix_ps, mix_sb = sig("dw_ps", 4), sig("dw_sb", 4), sig("mix_ps", 4), sig("mix_sb", 4)
        wo_sb = sig("wo_sb", 4)

        NLOAD = 16 * 8
        NBUILT = 21
        NPREP = 38

        def norm_job(k):
            return [(L, yv[:, 0, :], 2, 0), (L, yv[:, 1, :], 4, 2),
                    (W3, yv[:, 2, 0:W3], 6, 4), (W3, yv[:, 2, N:N + W3], 7, 5)][k]

        by_chunk = lambda t: t.rearrange("p (c n) -> p c n", c=NC)
        out_v = out.rearrange("b (t p) n -> b p t n", p=P)
        x_v = x.rearrange("b (t p) n -> b p t n", p=P)

        block = ctx.enter_context(nc.Block())

        @block.sync
        def _(sp):
            sp.dma_start(xin[:, :, :], x_v[0]).then_inc(xin_here.sem, 16)
            sp.dma_start(V[:, :], vpack).then_inc(loaded, 16)
            sp.dma_start(W8[:, :, :, :], w8).then_inc(loaded, 16)
            cuts = [0, WOFF["c1"], WOFF["xb"], WOFF["qkv1"], WOFF["wo"], WOFF["qkv3"], WTOT]
            for a, e in zip(cuts, cuts[1:]):
                sp.dma_start(W[:, a:e], wpack[:, a:e]).then_inc(loaded, 16)

            def attention(b, a):
                for g in range(GROUPS):
                    n = 4 * a + 2 * g
                    if a == 0 and g == 0:
                        sp.wait_ge(*ones_in(b, 1))
                    for part, ready, blks in ((0, qk_head, (0, 2)), (1, qk_rest, (1,))):
                        sp.wait_ge(*ready(b, n + 1))
                        for j in range(GH):
                            for blk in blks:
                                sp.dma_start(QS[32 * blk:32 * blk + 32, :, GH * g + j, :].bitcast(F32),
                                             by_chunk(piece[32 * j:32 * j + 32, 0, part, :]).bitcast(F32)).then_inc(stackedq[g].sem, 16)
                    sp.wait_ge(*qk_head(b, n + 2))
                    sp.wait_ge(*qk_rest(b, n + 2))
                    for j in range(GH):
                        for blk, part in enumerate((0, 0, 1)):
                            sp.dma_start(KS[32 * blk:32 * blk + 32, GH * g + j, :].bitcast(F32),
                                         piece[32 * j:32 * j + 32, 1, part, :].bitcast(F32)).then_inc(stackedk[g][j].sem, 16)
                for ph in range(PHASES):
                    g, c = divmod(ph, NC)
                    sp.wait_ge(*nm_rest(b, PHASES * a + ph + 1))
                    for part in range(2):
                        sp.dma_start(QS[96 + part:97 + part, c, GH * g:GH * g + GH, :].bitcast(F32),
                                     nm[:, part, :].bitcast(F32)).then_inc(nm_in.sem, 16)

            def sample(b, last):
                sp.wait_ge(*x_new(b, 4))
                if not last:
                    sp.dma_start(xin[:, :, :], x_v[b + 1]).then_inc(xin_here.sem, 16)
                attention(b, 0)
                attention(b, 1)
                sp.wait_ge(*x_new(b, 16))
                sp.dma_start(out_v[b], xr[:, :, :]).then_inc(stored.sem, 16)

            with sp.Fori(0, B - 1) as b:
                sample(b, False)
            sample(B - 1, True)
            sp.wait_ge(*stored(B - 1, 16))

        @block.gpsimd
        def _(pool):
            nb = [0]

            def step_(ins):
                nb[0] += 1
                ins.then_inc(built, 1)
                pool.wait_ge(built, nb[0])

            step_(pool.memset(ident[:, :], 0.0))
            step_(pool.affine_select(out=ident[:, :], in_=ident[:, :], compare_op=ALU.not_equal, fill=1.0,
                                     base=0, pattern=[[-1, P]], channel_multiplier=1))
            step_(pool.memset(g8[:, :], 1.0 / 32))
            gv = g8[:, :].rearrange("p (k r) -> p k r", r=8)
            step_(pool.affine_select(out=gv, in_=gv, compare_op=ALU.is_ge, fill=0.0, base=0,
                                     pattern=[[-8, 16], [0, 8]], channel_multiplier=1))
            step_(pool.affine_select(out=gv, in_=gv, compare_op=ALU.is_ge, fill=0.0, base=7,
                                     pattern=[[8, 16], [0, 8]], channel_multiplier=-1))
            step_(pool.memset(e8[:, :], 1.0))
            step_(pool.affine_select(out=e8[:, :], in_=e8[:, :], compare_op=ALU.is_ge, fill=0.0, base=0,
                                     pattern=[[-NST, DPG]], channel_multiplier=1))
            step_(pool.affine_select(out=e8[:, :], in_=e8[:, :], compare_op=ALU.is_ge, fill=0.0, base=NST - 1,
                                     pattern=[[NST, DPG]], channel_multiplier=-1))
            step_(pool.memset(ysel[:, :, :], 0.0))
            for i in range(4):
                step_(pool.tensor_copy(ysel[:, i, 8 * i:8 * i + 8], e8[:, :]))
            step_(pool.memset(sel32[:, :, :], 0.0))
            for base in (0, -64):
                s4 = sel32[:, :, :].rearrange("p g (d n) -> p g d n", n=NST)
                step_(pool.affine_select(out=s4, in_=s4, compare_op=ALU.not_equal, fill=1.0, base=base,
                                         pattern=[[-8, 8], [-1, 8], [0, NST]], channel_multiplier=1))
            step_(pool.memset(mean128[:, :], 1.0 / 128))
            step_(pool.memset(mean256[:, :], 1.0 / 256))
            step_(pool.memset(ones32[:, :], 1.0))
            step_(pool.memset(eps[:, :], 1e-5))
            step_(pool.memset(mhalf[:, :], -0.5))

            def sample(b):
                for n in range(3 * SG):
                    ps, at = n // SG, PASS_AT[n // SG]
                    if n >= 6:
                        pool.wait_ge(*y_ps(b, (n - 6) // 4 + 1))
                    if n == 0:
                        pool.wait_ge(*crep_sb(b, 3))
                    slot = work[:, 6 + n % 6, :]
                    h = work[:, 4 + n % 2, :]
                    if ps < 2:
                        pool.wait_ge(*scanned(b, n + 1))
                        pool.tensor_tensor(slot, h, Crep[:, at:at + L], ALU.mult).then_inc(hC_sb.sem, 1)
                    else:
                        pool.wait_ge(*scanned(b, 32 + 4 * (n - 32) + 4))
                        two = lambda t: t.rearrange("p (d w) -> p d w", d=2)[:, :, 0:W3]
                        pool.tensor_tensor(two(slot), two(h), Crep[:, None, at:at + W3].broadcast_to((P, 2, W3)),
                                           ALU.mult).then_inc(hC_sb.sem, 1)
                pool.wait_ge(*x_new(b, 4))
                one = ones32[96:98, 0:1].broadcast_to((2, HEADS * L))
                pool.tensor_tensor(KS[96:98, :, :].rearrange("p h n -> p (h n)"), one, one,
                                   ALU.mult).then_inc(ones_in.sem, 1)
                for a in range(2):
                    pool.wait_ge(*stackedq[1](b, (a + 1) * 192))
                    for j in range(GH):
                        pool.wait_ge(*stackedk[1][j](b, (a + 1) * 48))
                    for ph in range(PHASES - 1):
                        if ph == 2:
                            pool.wait_ge(*pv_ps(b, (PHASES * a + 1) * KT))
                        for k in range(1, len(POOL_SUMS)):
                            i, total = key_step(a, ph, POOL_SUMS[k]), acc[:, ph % 2, :, :]
                            first = PT[:, key_step(a, ph, 0) % 3, :, :] if k == 1 else total
                            if k > 1:
                                pool.wait_ge(*sum_pool(b, pool_sums(a, ph, k - 1)))
                            pool.wait_ge(*p_sb(b, 2 * i + 2))
                            pool.tensor_tensor(total, first, PT[:, i % 3, :, :], ALU.add).then_inc(sum_pool.sem, 1)
                pool.wait_ge(*x_new(b, 16))

            with pool.Fori(0, B) as b:
                sample(b)

        @block.scalar
        def _(act):
            act.preload_act_table_set("natural_log_exp_and_others")
            act.wait_ge(loaded, NLOAD)
            act.wait_ge(built, NBUILT)
            act.activation(Aneg[:, :], v("Al", 0, 3 * SG), ACT.Exp).then_inc(logged, 1)
            act.activation(tmp6, v("bn_v", 0, 6), ACT.Ln, bias=eps[:, :]).then_inc(logged, 1)
            act.wait_ge(logged, 2)
            act.activation(tmp6, tmp6, ACT.Exp, scale=-0.5).then_inc(logged, 1)

            def group_norm(b, s, X):
                act.wait_ge(*gn_gv(b, s + 1))
                act.activation(lnv, PS[:, 6, 0:2], ACT.Ln, scale=4.0 / L, bias=eps[:, :]).then_inc(gn_ln.sem, 1)
                act.wait_ge(*gn_ln(b, s + 1))
                act.activation(rs, lnv, ACT.Exp, scale=-0.5).then_inc(gn_rs.sem, 1)
                act.wait_ge(*gn_rs(b, s + 1))
                act.wait_ge(*gn_sh(b, s + 1))
                act.activation(xg[:, 1, :], X[:, 1, :], ACT.Identity, scale=rs[:, 1:2],
                               bias=sh[:, 1:2]).then_inc(gn_xb.sem, 1)

            def block0(b):
                for c in range(NC):
                    act.wait_ge(*xp_ps(b, c + 1))
                    act.activation(yv[:, 0, c * N:c * N + N], PS[:, c, :], ACT.Identity,
                                   bias=v("in_b", 0)).then_inc(xp_sb.sem, 1)
                act.wait_ge(*f2_ps(b, 1))
                act.activation(f23[:, 0:L2], PS[:, 4, 0:L2], ACT.Identity, bias=v("c2_b")).then_inc(f2_sb.sem, 1)
                act.wait_ge(*f3_ps(b, 1))
                act.activation(f23[:, L2:W3], PS[:, 5, 0:L3], ACT.Identity, bias=v("c3_b")).then_inc(f3_sb.sem, 1)
                for ps in range(3):
                    at, w = PASS_AT[ps], PASS_W[ps]
                    tu, tl = work[:, ps % 2, 0:w], work[:, 2 + ps % 2, 0:w]
                    act.wait_ge(*pre_ps(b, ps + 1))
                    if ps == 2:
                        act.wait_ge(*step(b, 1))
                    if ps < 2:
                        src = PS[:, (0, 6)[ps]:(0, 6)[ps] + 2, :].rearrange("p a n -> p (a n)")
                        act.activation(tu, src, ACT.Abs, bias=v("dtb", ps)).then_inc(sp_abs.sem, 1)
                    else:
                        act.activation(tu[:, 0:L2], PS[:, 4, 0:L2], ACT.Abs, bias=v("dtb", 1)).then_inc(sp_abs.sem, 1)
                        act.activation(tu[:, L2:W3], PS[:, 4, L2:W3], ACT.Abs, bias=v("dtb", 2)).then_inc(sp_abs.sem, 1)
                    for a_, e_, bias in (((0, w, v("dtb", ps)),) if ps < 2 else ((0, L2, v("dtb", 1)), (L2, W3, v("dtb", 2)))):
                        if ps < 2:
                            act.activation(work[:, 4 + ps, :], src, ACT.Relu, bias=bias).then_inc(sp_pos.sem, 1)
                        else:
                            act.activation(work[:, 4, a_:e_], PS[:, 4, a_:e_], ACT.Relu, bias=bias).then_inc(sp_pos.sem, 1)
                    act.wait_ge(*sp_abs(b, (1, 2, 4)[ps]))
                    act.activation(tu, tu, ACT.Exp, scale=-1.0).then_inc(sp_exp.sem, 1)
                    act.wait_ge(*sp_exp(b, ps + 1))
                    if ps == 2:
                        act.wait_ge(*sp_sum(b, 1))
                    act.activation(tl, tu, ACT.Ln, bias=1.0).then_inc(sp_ln.sem, 1)
                    if ps >= 1:
                        act.wait_ge(*sp_cut(b, ps))
                        act.wait_ge(*sp_poly(b, ps))
                    act.activation(work[:, 9, 0:w], tu, ACT.Identity, bias=1.0).then_inc(sp_one.sem, 1)
                    act.activation(work[:, 10, 0:w], tu, ACT.Identity, scale=1.0 / 3, bias=mhalf[:, :]).then_inc(sp_q.sem, 1)
                    for dst, src_ps, done, bank in ((Brep, brep_ps, brep_sb, (2, 0, 6)), (Crep, crep_ps, crep_sb, (4, 2, 0))):
                        act.wait_ge(*src_ps(b, ps + 1))
                        src = PS[:, bank[ps]:bank[ps] + 2, :].rearrange("p a n -> p (a n)")[:, 0:w]
                        act.activation(dst[:, at:at + w], src, ACT.Copy).then_inc(done.sem, 1)
                act.wait_ge(*rests_in(b, 12))
                for n in range(3 * SG):
                    ps = n // SG
                    g = scan_group(n)
                    slot = 2 + 2 * ((2 * n) % 3)
                    if n >= 2:
                        act.wait_ge(*scanned(b, scans(n - 2)))
                    act.wait_ge(*d_ps(b, n + 1))
                    dst = work[:, n % 2, :]
                    src = PS[:, slot:slot + 2, :].rearrange("p a n -> p (a n)")
                    if ps < 2:
                        act.activation(dst, src, ACT.Exp, scale=Aneg[:, ps * SG + g:ps * SG + g + 1]).then_inc(dA_sb.sem, 1)
                    else:
                        act.activation(dst[:, 0:L2], src[:, 0:L2], ACT.Exp,
                                       scale=Aneg[:, SG + g:SG + g + 1]).then_inc(dA_sb.sem, 1)
                        act.activation(dst[:, L2:W3], src[:, L2:W3], ACT.Exp,
                                       scale=Aneg[:, 2 * SG + g:2 * SG + g + 1]).then_inc(dA_sb.sem, 1)
                for k in range(4):
                    w, ybuf, mb, vb = norm_job(k)
                    act.wait_ge(*lm_d(b, k + 1))
                    t = work[:, k, 0:w]
                    act.activation(t, ybuf, ACT.Square).then_inc(lm_sq.sem, 1)
                    act.wait_ge(*lv_ps(b, k + 1))
                    src = PS[:, vb:vb + 2, :].rearrange("p a n -> p (a n)")[:, 0:w]
                    t2 = work[:, 4 + k, 0:w]
                    act.activation(t2, src, ACT.Ln, bias=eps[:, :]).then_inc(lv_ln.sem, 1)
                    act.wait_ge(*lv_ln(b, k + 1))
                    act.activation(t2, t2, ACT.Exp, scale=-0.5).then_inc(lv_rs.sem, 1)
                for c in range(NC):
                    act.wait_ge(*z_ps(b, c + 1))
                    act.activation(work[:, 8, c * N:c * N + N], PS[:, 6 + c, :], ACT.Silu,
                                   bias=v("in_b", 1)).then_inc(z_sb.sem, 1)
                act.preload_act_table_set("natural_log_exp_and_others")

            def chan_norm(b, s, X, gamma, beta):
                for c in range(NC):
                    n = NC * s + c
                    for t in range(CT):
                        act.wait_ge(*cm_d(b, 2 * n + t + 1))
                        act.activation(sq[:, 2 * c + t, :], X[:, t, c * N:c * N + N], ACT.Square).then_inc(cm_sq.sem, 1)
                for c in range(NC):
                    n = NC * s + c
                    act.wait_ge(*cv_ps(b, n + 1))
                    act.activation(rstd[:, c, :], PS[:, 2 + c, :], ACT.Ln, bias=eps[:, :]).then_inc(cv_ln.sem, 1)
                    act.wait_ge(*cv_ln(b, n + 1))
                    act.activation(rstd[:, c, :], rstd[:, c, :], ACT.Exp, scale=-0.5).then_inc(cv_rs.sem, 1)
                for c in range(NC):
                    n = NC * s + c
                    for t in range(CT):
                        act.wait_ge(*cn_n(b, 2 * n + t + 1))
                        act.activation(X[:, t, c * N:c * N + N], X[:, t, c * N:c * N + N], ACT.Identity,
                                       scale=v(gamma, t), bias=v(beta, t)).then_inc(cn_x.sem, 1)

            def attention(b, a):
                bq = ("qkv_b1", "qkv_b3")[a]
                for g in range(GROUPS):
                    for kind in range(2):
                        n = 2 * g + kind
                        act.wait_ge(*qk_ps(b, 4 * a + n + 1))
                        if g == 1:
                            if kind == 0:
                                act.wait_ge(*stackedq[0](b, (a + 1) * 192))
                            else:
                                for j in range(GH):
                                    act.wait_ge(*stackedk[0][j](b, (a + 1) * 48))
                        src = PS[:, 2 * kind:2 * kind + 2, :].rearrange("p a n -> p (a n)")
                        act.activation(piece[:, kind, 0, :], src, ACT.Identity,
                                       bias=v(bq, 2 * kind + g)).then_inc(qk_head.sem, 1)
                for q in range(2):
                    act.wait_ge(*v_ps(b, 2 * a + q + 1))
                    act.activation(Vt[:, 4 * q:4 * q + 4, :].rearrange("p k c -> p (k c)"),
                                   PS[:, 2 * q:2 * q + 2, :].rearrange("p a n -> p (a n)"), ACT.Copy).then_inc(v_sb.sem, 1)

                def neg_max(ph):
                    n = PHASES * a + ph
                    act.wait_ge(*mt_ps(b, n + 1))
                    if ph >= 1:
                        act.wait_ge(*nm_in(b, 32 * n))
                    act.activation(nm[:, 0, :], PS[0:PHASE_ROWS, 6, 0:P], ACT.Copy, scale=-1.0).then_inc(nm_head.sem, 1)

                def reciprocals(j):
                    act.wait_ge(*pv_ps(b, (j + 1) * KT))
                    act.activation(lr[:, 0, :], PS[:, 1, :], ACT.Ln).then_inc(den_ln.sem, 1)
                    act.wait_ge(*den_ln(b, j + 1))
                    if j % PHASES >= 1:
                        act.wait_ge(*o_raw(b, j))
                    act.activation(lr[:, 1, :], lr[:, 0, :], ACT.Exp, scale=-1.0).then_inc(den_rc.sem, 1)

                neg_max(0)
                for ph in range(PHASES):
                    for kt in range(KT):
                        i = key_step(a, ph, kt)
                        if kt == TURN_AT and ph < PHASES - 1:
                            neg_max(ph + 1)
                        if i % (PHASES * KT) >= 3:
                            act.wait_ge(*pv_ps(b, i - 2))
                            done = summed(a, *divmod(i % (PHASES * KT) - 3, KT))
                            if done:
                                act.wait_ge(*(sum_pool, sum_dve)[done[0]](b, done[1]))
                        for pr in range(2):
                            act.wait_ge(*s_ps(b, 2 * i + pr + 1))
                            act.activation(PT[:, i % 3, 2 * pr:2 * pr + 2, :], PS[:, 2 + 2 * pr:4 + 2 * pr, :],
                                           ACT.Exp, scale=SCALE).then_inc(p_sb.sem, 1)
                        if kt == 0 and ph >= 1:
                            reciprocals(PHASES * a + ph - 1)
                reciprocals(PHASES * a + PHASES - 1)

            def block2(b):
                for t in range(2):
                    for c in range(NC):
                        n = 2 * t + c
                        act.wait_ge(*dw_ps(b, n + 1))
                        act.activation(br[:, t, c * N:c * N + N], PS[:, n, :], ACT.Relu, scale=binv[:, t:t + 1],
                                       bias=bbias[:, t:t + 1]).then_inc(dw_sb.sem, 1)
                for m in range(2):
                    for c in range(NC):
                        n = 2 * m + c
                        act.wait_ge(*mix_ps(b, n + 1))
                        act.activation(zm[:, m, c * N:c * N + N], PS[:, 4 + n, :], ACT.Relu, scale=binv[:, 2 + m:3 + m],
                                       bias=bbias[:, 2 + m:3 + m]).then_inc(mix_sb.sem, 1)
                for m in range(2):
                    for c in range(NC):
                        n = 2 * m + c
                        act.wait_ge(*o_ps(b, 8 + n + 1))
                        act.activation(rl[:, n, :], PS[:, n, :], ACT.Relu, scale=binv[:, 4 + m:5 + m],
                                       bias=bbias[:, 4 + m:5 + m]).then_inc(wo_sb.sem, 1)

            with act.Fori(0, B) as b:
                act.wait_ge(*xin_here(b, 16))
                group_norm(b, 0, xin)
                block0(b)
                act.wait_ge(*x_new(b, 4))
                group_norm(b, 1, xr)
                attention(b, 0)
                act.wait_ge(*x_new(b, 8))
                group_norm(b, 2, xr)
                block2(b)
                act.wait_ge(*x_new(b, 12))
                group_norm(b, 3, xr)
                chan_norm(b, 0, xg, "gamma1", "beta1")
                attention(b, 1)
                chan_norm(b, 1, oT, "gamma2", "beta2")
                act.wait_ge(*x_new(b, 16))

        @block.vector
        def _(dve):
            dve.wait_ge(loaded, NLOAD)
            dve.wait_ge(built, NBUILT)
            dve.wait_ge(logged, 3)
            nprep = [0]

            def prep(ins):
                nprep[0] += 1
                ins.then_inc(prepared, 1)
                dve.wait_ge(prepared, nprep[0])

            prep(dve.tensor_copy(sel[:, :, :], sel32[:, :, :]))
            prep(dve.tensor_scalar(Aneg[:, :], Aneg[:, :], -1.0, None, ALU.mult))
            prep(dve.tensor_tensor(binv[:, :], tmp6, v("bn_g", 0, 6), ALU.mult))
            prep(dve.tensor_tensor(bbias[:, :], v("bn_b", 0, 6), v("bn_m", 0, 6), ALU.subtract))
            prep(dve.tensor_tensor(bbias[:, :], bbias[:, :], binv[:, :], ALU.mult))
            prep(dve.tensor_tensor(bbias[:, :], bbias[:, :], v("bn_be", 0, 6), ALU.add))
            prep(dve.tensor_tensor(bes[:, 0:1], v("be", 0), v("be", 1), ALU.add))
            prep(dve.tensor_tensor(bes[:, 1:3], v("be", 1, 2), v("be", 1, 2), ALU.add))
            prep(dve.tensor_tensor(id2[:, :], ident[:, 0:64], ident[:, 64:128], ALU.add))
            for t in range(2):
                for tap in range(9):
                    prep(dve.tensor_scalar(DW[:, t, tap, :], ident[:, :], v("wdw", 9 * t + tap), None, ALU.mult))
                for o in range(4):
                    prep(dve.tensor_scalar(MX[:, t, 64 * o:64 * o + 64], id2[:, :], v("ws", 4 * t + o), None, ALU.mult))
            for s in range(3):
                dve.wait_ge(folded, s + 1)
                prep(dve.tensor_copy(Wd[:, s, :], PS[:, s, 0:P]))

            def group_norm(b, s, X):
                for t in range(CT):
                    for c in range(NC):
                        dve.bn_stats(st[:, t, c, :], X[:, t, c * N:c * N + N]).then_inc(gn_st.sem, 1)
                quarter = st.rearrange("p t c (e k) -> p t (c e) k", e=2)
                dve.wait_ge(*gn_st(b, 4 * s + 4))
                dve.tensor_reduce(msum, quarter[:, :, :, 1], AX.X, ALU.add).then_inc(gn_sum.sem, 1)
                dve.wait_ge(*gn_gm(b, s + 1))
                dve.tensor_tensor(dev, quarter[:, :, :, 1], PS[:, 7, 0:2, None].broadcast_to((P, CT, 4)),
                                  ALU.subtract).then_inc(gn_dev.sem, 1)
                dve.wait_ge(*gn_dev(b, s + 1))
                dve.tensor_tensor(dd, dev, dev, ALU.mult).then_inc(gn_dd.sem, 1)
                dve.wait_ge(*gn_dd(b, s + 1))
                dve.scalar_tensor_tensor(out=dd, in0=dd, scalar=float(L // 4), in1=quarter[:, :, :, 2],
                                         op0=ALU.mult, op1=ALU.add).then_inc(gn_q.sem, 1)
                dve.wait_ge(*gn_q(b, s + 1))
                dve.tensor_reduce(m2, dd, AX.X, ALU.add).then_inc(gn_m2.sem, 1)
                dve.wait_ge(*gn_rs(b, s + 1))
                dve.scalar_tensor_tensor(out=sh, in0=PS[:, 7, 0:2], scalar=-1.0, in1=rs, op0=ALU.mult,
                                         op1=ALU.mult).then_inc(gn_sh.sem, 1)
                dve.wait_ge(*gn_sh(b, s + 1))
                dve.tensor_scalar(xg[:, 0, :], X[:, 0, :], rs[:, 0:1], sh[:, 0:1], ALU.mult, ALU.add).then_inc(gn_xa.sem, 1)

            def block0(b):
                for c in range(NC):
                    dve.wait_ge(*f1_ps(b, c + 1))
                    dve.tensor_scalar(f1[:, c * N:c * N + N], PS[:, 2 + c, :], v("c1_b"), None, ALU.add).then_inc(f1_sb.sem, 1)
                for ps in range(3):
                    at, w = PASS_AT[ps], PASS_W[ps]
                    tu, tl = work[:, ps % 2, 0:w], work[:, 2 + ps % 2, 0:w]
                    pos, cut = work[:, 4 + ps % 2, 0:w], work[:, 6, 0:w]
                    dl, ux = work[:, 7, 0:w], work[:, 8, 0:w]
                    one, qu, big = work[:, 9, 0:w], work[:, 10, 0:w], work[:, 11, 0:w]
                    dve.wait_ge(*sp_exp(b, ps + 1))
                    dve.tensor_scalar(big, tu, SMALL_U, None, ALU.is_ge).then_inc(sp_big.sem, 1)
                    dve.wait_ge(*sp_one(b, ps + 1))
                    dve.scalar_tensor_tensor(out=cut, in0=one, scalar=-1.0, in1=tu, op0=ALU.add,
                                             op1=ALU.subtract).then_inc(sp_cut.sem, 1)
                    dve.wait_ge(*sp_q(b, ps + 1))
                    dve.tensor_tensor(qu, qu, tu, ALU.mult).then_inc(sp_qu.sem, 1)
                    dve.wait_ge(*sp_cut(b, ps + 1))
                    dve.tensor_tensor(cut, tl, cut, ALU.subtract).then_inc(sp_sum.sem, 1)
                    dve.wait_ge(*sp_qu(b, ps + 1))
                    dve.scalar_tensor_tensor(out=dl, in0=qu, scalar=1.0, in1=tu, op0=ALU.add,
                                             op1=ALU.mult).then_inc(sp_poly.sem, 1)
                    dve.wait_ge(prepared, NPREP)
                    dve.wait_ge(*sp_big(b, ps + 1))
                    dve.wait_ge(*sp_sum(b, ps + 1))
                    dve.wait_ge(*sp_poly(b, ps + 1))
                    dve.copy_predicated(dl, big.bitcast(mybir.dt.int32), cut).then_inc(sp_one_of.sem, 1)
                    dve.wait_ge(*sp_pos(b, (1, 2, 4)[ps]))
                    dve.wait_ge(*sp_one_of(b, ps + 1))
                    dve.tensor_tensor(dl, dl, pos, ALU.add).then_inc(step.sem, 1)
                    dve.wait_ge(*step(b, ps + 1))
                    dve.wait_ge(*(f1_sb(b, 2) if ps < 2 else f3_sb(b, 1)))
                    src = f1[:, :] if ps < 2 else f23[:, :]
                    dve.tensor_tensor(ux, dl, src, ALU.mult).then_inc(stepx.sem, 1)
                    dve.wait_ge(*stepx(b, ps + 1))
                    for X, stk in ((dl, dstk), (ux, ustk)):
                        for hh in range(2):
                            r = slice(64 * hh, 64 * hh + 64)
                            dve.tensor_copy(stk[r, hh, at:at + w], X[r, :]).then_inc(heads_in.sem, 1)
                    dve.wait_ge(*heads_in(b, 4 * ps + 4))
                    for X, stk in ((dl, dstk), (ux, ustk)):
                        for hh in range(2):
                            r, ro = slice(64 * hh, 64 * hh + 64), slice(64 - 64 * hh, 128 - 64 * hh)
                            dve.tensor_tensor(stk[ro, hh, at:at + w], X[r, :], stk[r, hh, at:at + w].bitcast(F32),
                                              ALU.subtract).then_inc(rests_in.sem, 1)
                dve.wait_ge(*brep_sb(b, 3))
                for n in range(3 * SG):
                    ps, at = n // SG, PASS_AT[n // SG]
                    slot = 2 + 2 * ((2 * n + 1) % 3)
                    w = PASS_W[ps]
                    dA, dBx, h = work[:, n % 2, :], work[:, 2 + n % 2, :], work[:, 4 + n % 2, :]
                    dve.wait_ge(*u_ps(b, n + 1))
                    src = PS[:, slot:slot + 2, :].rearrange("p a n -> p (a n)")[:, 0:w]
                    dve.tensor_tensor(dBx[:, 0:w], src, Brep[:, at:at + w], ALU.mult).then_inc(dBx_sb.sem, 1)
                    dve.wait_ge(*dBx_sb(b, n + 1))
                    if n >= 2:
                        dve.wait_ge(*hC_sb(b, n - 1))
                    if ps < 2:
                        dve.wait_ge(*dA_sb(b, n + 1))
                        if ps == 0:
                            dve.tensor_tensor_scan(h, dA, dBx, 0.0, ALU.mult, ALU.add).then_inc(scanned.sem, 1)
                        else:
                            dve.tensor_tensor_scan(h[:, ::-1], dA[:, ::-1], dBx[:, ::-1], 0.0, ALU.mult,
                                                   ALU.add).then_inc(scanned.sem, 1)
                    else:
                        dve.wait_ge(*dA_sb(b, 32 + 2 * (n - 32) + 2))
                        for a_, e_ in ((0, L2), (L2, W3)):
                            dve.tensor_tensor_scan(h[:, a_:e_], dA[:, a_:e_], dBx[:, a_:e_], 0.0, ALU.mult,
                                                   ALU.add).then_inc(scanned.sem, 1)
                            rev = slice(e_ - 1, a_ - 1 if a_ else None, -1)
                            rev_o = slice(N + e_ - 1, N + a_ - 1, -1)
                            dve.tensor_tensor_scan(h[:, rev_o], dA[:, rev], dBx[:, rev], 0.0, ALU.mult,
                                                   ALU.add).then_inc(scanned.sem, 1)
                    if n == 17 + 1:
                        dve.wait_ge(*y_ps(b, 4))
                        dve.scalar_tensor_tensor(out=yv[:, 0, :], in0=f1[:, :], scalar=v("Dv", 0),
                                                 in1=PS[:, 0:2, :].rearrange("p a n -> p (a n)"),
                                                 op0=ALU.mult, op1=ALU.add).then_inc(y_sb.sem, 1)
                    if n == 33 + 1:
                        dve.wait_ge(*y_ps(b, 8))
                        dve.scalar_tensor_tensor(out=yv[:, 1, :], in0=f1[:, :], scalar=v("Dv", 1),
                                                 in1=PS[:, 0:2, :].rearrange("p a n -> p (a n)"),
                                                 op0=ALU.mult, op1=ALU.add).then_inc(y_sb.sem, 1)
                dve.wait_ge(*y_ps(b, 12))
                for d in range(2):
                    for s, a_, e_ in ((1, 0, L2), (2, L2, W3)):
                        dve.scalar_tensor_tensor(out=yv[:, 2, d * N + a_:d * N + e_], in0=f23[:, a_:e_],
                                                 scalar=v("Dv", s), in1=PS[:, d, a_:e_], op0=ALU.mult,
                                                 op1=ALU.add).then_inc(y_sb.sem, 1)
                for k in range(4):
                    w, ybuf, mb, vb = norm_job(k)
                    dve.wait_ge(*y_sb(b, 6))
                    dve.wait_ge(*lm_ps(b, k + 1))
                    src = PS[:, mb:mb + 2, :].rearrange("p a n -> p (a n)")[:, 0:w] if w > N else PS[:, mb, 0:w]
                    dve.tensor_tensor(ybuf, ybuf, src, ALU.subtract).then_inc(lm_d.sem, 1)
                for k in range(4):
                    w, ybuf, mb, vb = norm_job(k)
                    dve.wait_ge(*lv_rs(b, k + 1))
                    dve.wait_ge(*lm_d(b, k + 1))
                    dve.tensor_tensor(ybuf, ybuf, work[:, 4 + k, 0:w], ALU.mult).then_inc(ln_n.sem, 1)
                nl = [0]

                def chain(ins):
                    nl[0] += 1
                    ins.then_inc(levels.sem, 1)
                    dve.wait_ge(*levels(b, nl[0]))

                dve.wait_ge(*ln_n(b, 4))
                y1, y2, y3 = work[:, 9, :], work[:, 10, 0:L2], work[:, 10, L2:W3]
                chain(dve.tensor_scalar(y3, yv[:, 2, L2:W3], v("g", 2), bes[:, 2:3], ALU.mult, ALU.add))
                chain(dve.scalar_tensor_tensor(out=y3, in0=yv[:, 2, N + L2:N + W3], scalar=v("g", 2), in1=y3,
                                               op0=ALU.mult, op1=ALU.add))
                chain(dve.tensor_scalar(y2, yv[:, 2, 0:L2], v("g", 1), bes[:, 1:2], ALU.mult, ALU.add))
                chain(dve.scalar_tensor_tensor(out=y2, in0=yv[:, 2, N:N + L2], scalar=v("g", 1), in1=y2,
                                               op0=ALU.mult, op1=ALU.add))

                def up(fine, coarse, side):
                    fv = fine.rearrange("p (h i w j) -> p h i w j", i=2, w=side, j=2)
                    cv = coarse.rearrange("p (h w) -> p h w", w=side)
                    for i in range(2):
                        for j in range(2):
                            chain(dve.tensor_tensor(fv[:, :, i, :, j], fv[:, :, i, :, j], cv, ALU.add))

                up(y2, y3, WW // 4)
                chain(dve.tensor_scalar(y1, yv[:, 0, :], v("g", 0), bes[:, 0:1], ALU.mult, ALU.add))
                chain(dve.scalar_tensor_tensor(out=y1, in0=yv[:, 1, :], scalar=v("g", 1), in1=y1,
                                               op0=ALU.mult, op1=ALU.add))
                up(y1, y2, WW // 2)
                dve.wait_ge(*z_sb(b, 2))
                dve.tensor_tensor(work[:, 11, :], y1, work[:, 8, :], ALU.mult).then_inc(gated.sem, 1)
                for m in range(CT):
                    for c in range(NC):
                        n = 2 * m + c
                        cs = slice(c * N, c * N + N)
                        dve.wait_ge(*o_ps(b, n + 1))
                        dve.scalar_tensor_tensor(out=xr[:, m, cs], in0=PS[:, n, :], scalar=v("out_b", m),
                                                 in1=xin[:, m, cs], op0=ALU.add, op1=ALU.add).then_inc(x_new.sem, 1)

            def chan_norm(b, s, X):
                for c in range(NC):
                    n = NC * s + c
                    dve.wait_ge(*cm_ps(b, n + 1))
                    for t in range(CT):
                        cs = slice(c * N, c * N + N)
                        dve.tensor_tensor(X[:, t, cs], X[:, t, cs], PS[:, c, :], ALU.subtract).then_inc(cm_d.sem, 1)
                for c in range(NC):
                    n = NC * s + c
                    dve.wait_ge(*cv_rs(b, n + 1))
                    dve.wait_ge(*cm_d(b, 2 * n + 2))
                    for t in range(CT):
                        cs = slice(c * N, c * N + N)
                        dve.tensor_tensor(X[:, t, cs], X[:, t, cs], rstd[:, c, :], ALU.mult).then_inc(cn_n.sem, 1)

            def attention(b, a):
                bq = ("qkv_b1", "qkv_b3")[a]

                def rest(g, kind):
                    n = 2 * g + kind
                    dve.wait_ge(*qk_head(b, 4 * a + n + 1))
                    src = PS[:, 2 * kind:2 * kind + 2, :].rearrange("p a n -> p (a n)")
                    dve.scalar_tensor_tensor(out=piece[:, kind, 1, :], in0=src, scalar=v(bq, 2 * kind + g),
                                             in1=piece[:, kind, 0, :].bitcast(F32), op0=ALU.add,
                                             op1=ALU.subtract).then_inc(qk_rest.sem, 1)

                def row_max(n):
                    at = n % PHASE_ROWS
                    for cc in range(NC):
                        dve.wait_ge(*r_ps(b, halves(a, n, cc) + 1))
                        dve.tensor_reduce(mx[:, cc, at:at + 1], PS[:, row_slot(n, cc), :], AX.X,
                                          ALU.max).then_inc(r_max.sem, 1)
                    if at == PHASE_ROWS - 1:
                        ph = n // PHASE_ROWS
                        dve.wait_ge(*r_max(b, halves(a, n, NC - 1) + 1))
                        if ph > 0:
                            dve.wait_ge(*mt_ps(b, PHASES * a + ph))
                        dve.tensor_tensor(mboth[:, :], mx[:, 0, :], mx[:, 1, :], ALU.max).then_inc(m_both.sem, 1)

                def neg_max(ph):
                    dve.wait_ge(*nm_head(b, PHASES * a + ph + 1))
                    dve.scalar_tensor_tensor(out=nm[:, 1, :], in0=PS[0:PHASE_ROWS, 6, 0:P], scalar=-1.0,
                                             in1=nm[:, 0, :].bitcast(F32), op0=ALU.mult,
                                             op1=ALU.subtract).then_inc(nm_rest.sem, 1)

                def normalize(ph):
                    g, c = divmod(ph, NC)
                    j, cs = PHASES * a + ph, slice(c * N, c * N + N)
                    dve.wait_ge(*den_rc(b, j + 1))
                    dve.tensor_tensor(oT[:, g, cs], PS[:, 0, :], lr[:, 1, :], ALU.mult).then_inc(o_raw.sem, 1)
                    dve.wait_ge(*o_raw(b, j + 1))
                    dve.tensor_scalar(oT[:, g, cs], oT[:, g, cs], v(bq, 4 + g), None, ALU.add).then_inc(o_sb.sem, 1)

                rest(0, 0)
                rest(0, 1)
                rest(1, 0)
                for n in range(PHASE_ROWS):
                    row_max(n)
                    if n == 2:
                        rest(1, 1)
                neg_max(0)
                for ph in range(PHASES - 1):
                    n = PHASE_ROWS * (ph + 1)
                    for kt in range(KT):
                        if kt == TURN_AT:
                            neg_max(ph + 1)
                        for _ in range(ROWS[kt]):
                            row_max(n)
                            n += 1
                        if kt == 0 and ph >= 1:
                            normalize(ph - 1)
                ph = PHASES - 1
                normalize(ph - 1)
                dve.wait_ge(*pv_ps(b, (PHASES * a + 2) * KT))
                for k in range(1, len(DVE_SUMS)):
                    i, total = key_step(a, ph, DVE_SUMS[k]), acc[:, ph % 2, :, :]
                    first = PT[:, key_step(a, ph, 0) % 3, :, :] if k == 1 else total
                    if k > 1:
                        dve.wait_ge(*sum_dve(b, dve_sums(a, k - 1)))
                    dve.wait_ge(*p_sb(b, 2 * i + 2))
                    dve.tensor_tensor(total, first, PT[:, i % 3, :, :], ALU.add).then_inc(sum_dve.sem, 1)
                normalize(ph)

            def residual(b, first, bias):
                for m in range(CT):
                    for c in range(NC):
                        n = 2 * m + c
                        cs = slice(c * N, c * N + N)
                        dve.wait_ge(*o_ps(b, first + n + 1))
                        dve.scalar_tensor_tensor(out=xr[:, m, cs], in0=PS[:, n, :], scalar=v(bias, m),
                                                 in1=xr[:, m, cs], op0=ALU.add, op1=ALU.add).then_inc(x_new.sem, 1)

            with dve.Fori(0, B) as b:
                dve.wait_ge(*xin_here(b, 16))
                group_norm(b, 0, xin)
                block0(b)
                dve.wait_ge(*x_new(b, 4))
                group_norm(b, 1, xr)
                attention(b, 0)
                residual(b, 4, "proj_b")
                dve.wait_ge(*x_new(b, 8))
                group_norm(b, 2, xr)
                for m in range(CT):
                    for c in range(NC):
                        n = 2 * m + c
                        cs = slice(c * N, c * N + N)
                        dve.wait_ge(*wo_sb(b, n + 1))
                        dve.tensor_tensor(xr[:, m, cs], xr[:, m, cs], rl[:, n, :], ALU.add).then_inc(x_new.sem, 1)
                dve.wait_ge(*x_new(b, 12))
                group_norm(b, 3, xr)
                chan_norm(b, 0, xg)
                for t in range(CT):
                    dve.wait_ge(*cn_x(b, 4))
                    dve.tensor_tensor(xr[:, t, :], xr[:, t, :], xg[:, t, :], ALU.add).then_inc(x3n.sem, 1)
                attention(b, 1)
                dve.wait_ge(*o_sb(b, 8))
                chan_norm(b, 1, oT)
                dve.wait_ge(*x3n(b, 2))
                residual(b, 12, "out3_b")
                dve.wait_ge(*stored(b, 16))

        @block.tensor
        def _(pe):
            pe.wait_ge(loaded, NLOAD)
            pe.wait_ge(built, NBUILT)
            for s in range(3):
                pe.matmul(PS[:, s, 0:P], W8[:, s, 0, :], W8[:, s, 1, :], start=True, stop=True).then_inc(folded, 1)
            pe.wait_ge(prepared, NPREP)

            def group_norm(b, s):
                pe.wait_ge(*gn_sum(b, s + 1))
                pe.matmul(PS[:, 7, 0:2], g8[:, :], msum, start=True, stop=True).then_inc(gn_gm.sem, 1)
                pe.wait_ge(*gn_m2(b, s + 1))
                pe.matmul(PS[:, 6, 0:2], g8[:, :], m2, start=True, stop=True).then_inc(gn_gv.sem, 1)
                pe.wait_ge(*gn_xa(b, s + 1))
                pe.wait_ge(*gn_xb(b, s + 1))

            def linear(bank, w, m, X, c, done):
                for k in range(CT):
                    ins = pe.matmul(PS[:, bank, :], w[:, k, m * P:m * P + P], X[:, k, c * N:c * N + N],
                                    start=(k == 0), stop=(k == CT - 1))
                if done is not None:
                    ins.then_inc(done.sem, 1)

            def block0(b):
                for c in range(NC):
                    linear(c, w_in, 0, xg, c, xp_ps)
                for c in range(NC):
                    pe.wait_ge(*xp_sb(b, c + 1))
                    pe.matmul(PS[:, 2 + c, :], w_c1, yv[:, 0, c * N:c * N + N], start=True, stop=True).then_inc(f1_ps.sem, 1)
                pe.wait_ge(*f1_sb(b, 2))
                v1 = f1[:, :].rearrange("p (h i w j) -> p h i w j", i=2, w=WW // 2, j=2)
                for k in range(4):
                    ins = pe.matmul(PS[:, 4, 0:L2], w_c2[:, k, :], v1[:, :, k // 2, :, k % 2], start=(k == 0), stop=(k == 3))
                ins.then_inc(f2_ps.sem, 1)

                def coeff(ps, bank, w, done):
                    if ps < 2:
                        for c in range(NC):
                            ins = pe.matmul(PS[:, bank + c, :], w[:, ps, :], f1[:, c * N:c * N + N], start=True, stop=True)
                    else:
                        pe.matmul(PS[:, bank, 0:L2], w[:, 1, :], f23[:, 0:L2], start=True, stop=True)
                        ins = pe.matmul(PS[:, bank, L2:W3], w[:, 2, :], f23[:, L2:W3], start=True, stop=True)
                    ins.then_inc(done.sem, 1)

                coeff(0, 0, Wd, pre_ps)
                coeff(0, 2, w_xb, brep_ps)
                pe.wait_ge(*f2_sb(b, 1))
                v2 = f23[:, 0:L2].rearrange("p (h i w j) -> p h i w j", i=2, w=WW // 4, j=2)
                for k in range(4):
                    ins = pe.matmul(PS[:, 5, 0:L3], w_c3[:, k, :], v2[:, :, k // 2, :, k % 2], start=(k == 0), stop=(k == 3))
                ins.then_inc(f3_ps.sem, 1)
                coeff(1, 6, Wd, pre_ps)
                pe.wait_ge(*f3_sb(b, 1))
                coeff(0, 4, w_xc, crep_ps)
                pe.wait_ge(*sp_abs(b, 1))
                pe.wait_ge(*sp_pos(b, 1))
                coeff(1, 0, w_xb, brep_ps)
                pe.wait_ge(*brep_sb(b, 1))
                coeff(1, 2, w_xc, crep_ps)
                pe.wait_ge(*crep_sb(b, 1))
                coeff(2, 4, Wd, pre_ps)
                pe.wait_ge(*sp_abs(b, 2))
                pe.wait_ge(*sp_pos(b, 2))
                coeff(2, 6, w_xb, brep_ps)
                pe.wait_ge(*brep_sb(b, 2))
                coeff(2, 0, w_xc, crep_ps)

                def sum_states(q):
                    ps = q // 4
                    pe.wait_ge(*hC_sb(b, 4 * q + 4))
                    if q == 4:
                        pe.wait_ge(*y_sb(b, 1))
                    if q == 8:
                        pe.wait_ge(*y_sb(b, 2))
                    for c in range(NC):
                        for j in range(4):
                            hc = work[:, 6 + (4 * q + j) % 6, :]
                            src = hc[:, c * N:c * N + N] if ps < 2 else hc[:, c * N:c * N + W3]
                            ins = pe.matmul(PS[32 * j:32 * j + 32, c, 0:N if ps < 2 else W3], ysel[:, q % 4, :], src,
                                            start=(q % 4 == 0), stop=(q % 4 == 3), skip_group_check=True)
                    ins.then_inc(y_ps.sem, 1)

                pe.wait_ge(*rests_in(b, 12))
                pe.wait_ge(*crep_sb(b, 3))
                for n in range(3 * SG):
                    ps, at, w = n // SG, PASS_AT[n // SG], PASS_W[n // SG]
                    g = scan_group(n)
                    for kind, (stk, done) in enumerate(((dstk, d_ps), (ustk, u_ps))):
                        job = 2 * n + kind
                        slot = 2 + 2 * (job % 3)
                        if job >= 3:
                            prev = job - 3
                            if prev % 2 == 0:
                                pe.wait_ge(*dA_sb(b, decays(prev // 2)))
                            else:
                                pe.wait_ge(*dBx_sb(b, prev // 2 + 1))
                        for c in range((w + N - 1) // N):
                            wc = min(N, w - c * N)
                            ins = pe.matmul(PS[:, slot + c, 0:wc], sel[:, g % 8, :], stk[:, g // 8, at + c * N:at + c * N + wc],
                                            start=True, stop=True)
                        ins.then_inc(done.sem, 1)
                    if n >= 5 and n % 4 == 1:
                        sum_states((n - 5) // 4)
                sum_states(11)
                pe.wait_ge(*y_sb(b, 6))
                for k in range(4):
                    w, ybuf, mb, vb = norm_job(k)
                    for c in range((w + N - 1) // N):
                        wc = min(N, w - c * N)
                        ins = pe.matmul(PS[:, mb + c, 0:wc], mean128[:, :], ybuf[:, c * N:c * N + wc], start=True, stop=True)
                    ins.then_inc(lm_ps.sem, 1)
                for k in range(4):
                    w, ybuf, mb, vb = norm_job(k)
                    pe.wait_ge(*lm_sq(b, k + 1))
                    if k == 1:
                        pe.wait_ge(*lm_d(b, 2))
                    for c in range((w + N - 1) // N):
                        wc = min(N, w - c * N)
                        ins = pe.matmul(PS[:, vb + c, 0:wc], mean128[:, :], work[:, k, c * N:c * N + wc], start=True, stop=True)
                    ins.then_inc(lv_ps.sem, 1)
                for c in range(NC):
                    linear(6 + c, w_in, 1, xg, c, z_ps)
                pe.wait_ge(*gated(b, 1))
                for m in range(CT):
                    for c in range(NC):
                        pe.matmul(PS[:, 2 * m + c, :], w_out[:, m * P:m * P + P], work[:, 11, c * N:c * N + N],
                                  start=True, stop=True).then_inc(o_ps.sem, 1)

            def chan_norm(b, s, X):
                for c in range(NC):
                    for t in range(CT):
                        ins = pe.matmul(PS[:, c, :], mean256[:, :], X[:, t, c * N:c * N + N], start=(t == 0), stop=(t == CT - 1))
                    ins.then_inc(cm_ps.sem, 1)
                for c in range(NC):
                    n = NC * s + c
                    pe.wait_ge(*cm_sq(b, 2 * n + 2))
                    for t in range(CT):
                        ins = pe.matmul(PS[:, 2 + c, :], mean256[:, :], sq[:, 2 * c + t, :], start=(t == 0), stop=(t == CT - 1))
                    ins.then_inc(cv_ps.sem, 1)

            def attention(b, a, X):
                wq, kd = w_qkv[a], 96

                def project_qk(g, kind, c):
                    linear(2 * kind + c, wq, 2 * kind + g, X, c, qk_ps if c == NC - 1 else None)

                def project_v(tt):
                    for k in range(CT):
                        ins = pe.matmul(PS[:, tt // 2, (tt % 2) * C:(tt % 2) * C + C], X[:, k, tt * P:tt * P + P],
                                        wq[:, k, 2 * C:3 * C], start=(k == 0), stop=(k == CT - 1))
                    if tt % 4 == 3:
                        ins.then_inc(v_ps.sem, 1)

                def row_scores(n):
                    ph, j, q = n // PHASE_ROWS, n % PHASE_ROWS // 4, n % 4
                    g, c = divmod(ph, NC)
                    h = GH * g + j
                    if c == 0 and q == 0:
                        pe.wait_ge(*stackedk[g][j](b, (a + 1) * 48))
                    for cc in range(NC):
                        ahead = 2 if ph == 0 else 1
                        if n % PHASE_ROWS >= ahead:
                            pe.wait_ge(*r_max(b, halves(a, n - ahead, cc) + 1))
                        pe.matmul(PS[:, row_slot(n, cc), :], QS[0:kd, c, h, q * P:q * P + P], KS[0:kd, h, cc * N:cc * N + N],
                                  start=True, stop=True).then_inc(r_ps.sem, 1)

                def turn_max(ph):
                    pe.wait_ge(*m_both(b, a * PHASES + ph + 1))
                    pe.transpose(PS[0:PHASE_ROWS, 6, 0:P], mboth[:, :], ident[:, :]).then_inc(mt_ps.sem, 1)

                for kind in range(2):
                    for c in range(NC):
                        project_qk(0, kind, c)
                pe.wait_ge(*qk_rest(b, 4 * a + 1))
                for c in range(NC):
                    project_qk(1, 0, c)
                pe.wait_ge(*stackedq[0](b, (a + 1) * 192))
                for n in range(PHASE_ROWS):
                    row_scores(n)
                    if n < NC:
                        if n == 0:
                            pe.wait_ge(*qk_rest(b, 4 * a + 2))
                        project_qk(1, 1, n)
                    elif n < NC + KT:
                        if n - NC in (0, 4):
                            pe.wait_ge(*qk_rest(b, 4 * a + 3 + (n - NC) // 4))
                        project_v(n - NC)
                turn_max(0)
                pe.wait_ge(*v_sb(b, 2 * a + 2))

                def values(i, between):
                    ph, kt = divmod(i % (PHASES * KT), KT)
                    g = ph // NC
                    sums = POOL_SUMS if ph < PHASES - 1 else DVE_SUMS
                    direct = [k for k in range(KT) if k not in sums]
                    pe.wait_ge(*p_sb(b, 2 * i + 2))
                    if kt == 0 and ph > 0:
                        pe.wait_ge(*o_raw(b, i // KT))
                    for j in range(GH):
                        h = GH * g + j
                        ins = pe.matmul(PS[32 * j:32 * j + 32, 0, :], Vt[:, kt, DH * h:DH * h + DH], PT[:, i % 3, j, :],
                                        start=(kt == 0), stop=(kt == KT - 1), skip_group_check=True)
                    if kt not in direct:
                        ins.then_inc(pv_ps.sem, 1)
                    between()
                    if kt in direct:
                        for j in range(GH):
                            ins = pe.matmul(PS[32 * j:32 * j + 32, 1, :], ones32[:, :], PT[:, i % 3, j, :],
                                            start=(kt == direct[0]), stop=False, skip_group_check=True)
                        if kt == KT - 1:
                            if ph < PHASES - 1:
                                pe.wait_ge(*sum_pool(b, pool_sums(a, ph, len(POOL_SUMS) - 1)))
                            else:
                                pe.wait_ge(*sum_dve(b, dve_sums(a, len(DVE_SUMS) - 1)))
                            for j in range(GH):
                                ins = pe.matmul(PS[32 * j:32 * j + 32, 1, :], ones32[:, :], acc[:, ph % 2, j, :],
                                                start=False, stop=True, skip_group_check=True)
                        ins.then_inc(pv_ps.sem, 1)

                for ph in range(PHASES):
                    g, c = divmod(ph, NC)
                    row = [PHASE_ROWS * (ph + 1), 0]

                    def next_row():
                        if ph == PHASES - 1 or row[1] == 0:
                            return
                        n = row[0]
                        if n % PHASE_ROWS == 0:
                            pe.wait_ge(*nm_rest(b, PHASES * a + ph + 1))
                            if ph == 1:
                                pe.wait_ge(*stackedq[1](b, (a + 1) * 192))
                        row_scores(n)
                        row[0], row[1] = n + 1, row[1] - 1

                    pe.wait_ge(*nm_in(b, 32 * (PHASES * a + ph + 1)))
                    for kt in range(KT):
                        i = key_step(a, ph, kt)
                        row[1] = ROWS[kt]
                        if kt == TURN_AT and ph < PHASES - 1:
                            turn_max(ph + 1)
                        for pr in range(2):
                            if ph + kt > 0:
                                pe.wait_ge(*p_sb(b, 2 * i - 2 + pr + 1))
                            for jj in range(2):
                                h = GH * g + 2 * pr + jj
                                ins = pe.matmul(PS[:, 2 + 2 * pr + jj, :], KS[:, h, kt * P:kt * P + P], QS[:, c, h, :],
                                                start=True, stop=True)
                            ins.then_inc(s_ps.sem, 1)
                            if pr == 0:
                                next_row()
                        if ph + kt > 0:
                            values(i - 1, next_row)
                        else:
                            next_row()
                        next_row()
                values(key_step(a, PHASES - 1, KT - 1), lambda: None)

            def project(b, a, X):
                for m in range(CT):
                    for c in range(NC):
                        if m == 0 and c == 0:
                            pe.wait_ge(*o_raw(b, 4 * a + 4))
                        linear(2 * m + c, w_proj[a], m, X, c, o_ps)

            def block2(b):
                for t in range(2):
                    for c in range(NC):
                        n = 2 * t + c
                        top = c * (HH // NC)
                        for hh, (ky, kx), (y0, y1, x0, x1), first, last in windows(t, c):
                            dy, dx = (ky - 1) * RATES[2 * t + hh], (kx - 1) * RATES[2 * t + hh]
                            dst = PS[64 * hh:64 * hh + 64, n, :].rearrange("p (h w) -> p h w", w=WW)[:, y0 - top:y1 - top, x0:x1]
                            src = xg[:, t, :].rearrange("p (h w) -> p h w", w=WW)[:, y0 + dy:y1 + dy, x0 + dx:x1 + dx]
                            ins = pe.matmul(dst, DW[:, t, ky * 3 + kx, 64 * hh:64 * hh + 64], src,
                                            start=first, stop=last, skip_group_check=True)
                        ins.then_inc(dw_ps.sem, 1)
                for m in range(2):
                    for c in range(NC):
                        pe.wait_ge(*dw_sb(b, 4))
                        linear(4 + 2 * m + c, MX, m, br, c, mix_ps)
                for m in range(2):
                    for c in range(NC):
                        pe.wait_ge(*mix_sb(b, 4))
                        linear(2 * m + c, w_o, m, zm, c, o_ps)

            with pe.Fori(0, B) as b:
                group_norm(b, 0)
                block0(b)
                group_norm(b, 1)
                attention(b, 0, xg)
                pe.wait_ge(*o_sb(b, 4))
                project(b, 0, oT)
                group_norm(b, 2)
                block2(b)
                group_norm(b, 3)
                chan_norm(b, 0, xg)
                pe.wait_ge(*cn_x(b, 4))
                attention(b, 1, xg)
                pe.wait_ge(*o_sb(b, 8))
                chan_norm(b, 1, oT)
                pe.wait_ge(*cn_x(b, 8))
                project(b, 1, oT)
                pe.wait_ge(*x_new(b, 16))


def row_slot(n, cc):
    return (4 + 2 * (n % 2) if n < PHASE_ROWS else 6) + cc


def halves(a, n, cc):
    return (a * PHASES * PHASE_ROWS + n) * NC + cc


def key_step(a, ph, kt):
    return (PHASES * a + ph) * KT + kt


def pool_sums(a, ph, k):
    return ((PHASES - 1) * a + ph) * (len(POOL_SUMS) - 1) + k


def dve_sums(a, k):
    return (len(DVE_SUMS) - 1) * a + k


def summed(a, ph, kt):
    sums = POOL_SUMS if ph < PHASES - 1 else DVE_SUMS
    if kt not in sums:
        return None
    k = max(1, sums.index(kt))
    return (0, pool_sums(a, ph, k)) if ph < PHASES - 1 else (1, dve_sums(a, k))


def scan_group(n):
    i, j = (n % SG) // 4, n % 4
    return 4 * j + i


def scans(n):
    return n + 1 if n < 32 else 32 + 4 * (n - 32) + 4


def decays(n):
    return n + 1 if n < 32 else 32 + 2 * (n - 32) + 2


def windows(t, c):
    top, todo = c * (HH // NC), []
    for ky, kx in TAPS:
        for hh in range(2):
            dy, dx = (ky - 1) * RATES[2 * t + hh], (kx - 1) * RATES[2 * t + hh]
            y0, y1 = max(top, -dy), min(top + HH // NC, HH - dy)
            x0, x1 = max(0, -dx), min(WW, WW - dx)
            if y0 < y1 and x0 < x1:
                todo.append((hh, (ky, kx), (y0, y1, x0, x1)))
    ends = {hh: max(i for i, w in enumerate(todo) if w[0] == hh) for hh in range(2)}
    return [(*w, w[1] == (1, 1), i == ends[w[0]]) for i, w in enumerate(todo)]


def kernel(**inputs):
    import numpy as np
    import concourse.bacc as bacc
    from concourse.bass_utils import run_bass_kernel_spmd

    a = {k: np.asarray(t) for k, t in inputs.items()}
    two = lambda t: t.reshape(2, P, -1).transpose(1, 0, 2)
    col = lambda t: np.ascontiguousarray(t.reshape(-1, P).T)
    z0, z1, z2, z3 = (lambda n, i=i: a[f"L{i}_conv_{n}"] for i in range(4))

    taps = lambda w: w.transpose(1, 2, 3, 0).reshape(P, 4 * P)
    part = {
        "in_w": two(z0("in_w").T), "c1": z0("c1_w").T, "c2": taps(z0("c2_w")), "c3": taps(z0("c3_w")),
        "xb": np.concatenate([np.tile(z0(f"xw{s}")[R_DT:R_DT + NST].T, (1, DPG)) for s in (1, 2, 3)], 1),
        "xc": np.concatenate([np.tile(z0(f"xw{s}")[R_DT + NST:].T, (1, DPG)) for s in (1, 2, 3)], 1),
        "out": z0("out_w").T,
        "qkv1": two(z1("qkv_w").T), "proj1": two(z1("proj_w").T),
        "wo": two(z2("wo")[:, :, 0, 0].reshape(C, C // 4, 4).transpose(2, 1, 0).reshape(C, C)),
        "qkv3": two(z3("w_qkv")), "out3": two(z3("w_out")),
    }
    wpack = np.ascontiguousarray(np.concatenate([part[n].reshape(P, w) for n, w in WSEC], 1))

    def bn(n_dw, n_s, n_o):
        return np.concatenate([col(z2(n_dw).reshape(-1)), col(np.repeat(z2(n_s), C // 4)), col(z2(n_o))], 1)

    ws = z2("ws")[:, :, 0, 0]
    vec = {
        "in_b": col(z0("in_b")), "c1_b": col(z0("c1_b")), "c2_b": col(z0("c2_b")), "c3_b": col(z0("c3_b")),
        "out_b": col(z0("out_b")),
        "dtb": np.stack([z0(f"dtb{s}") for s in (1, 2, 3)], 1), "Dv": np.stack([z0(f"Dv{s}") for s in (1, 2, 3)], 1),
        "g": np.stack([z0(f"g{s}") for s in (1, 2, 3)], 1), "be": np.stack([z0(f"be{s}") for s in (1, 2, 3)], 1),
        "Al": np.concatenate([z0(f"Al{s}").reshape(SG, P).T for s in (1, 2, 3)], 1),
        "qkv_b1": col(z1("qkv_b")), "proj_b": col(z1("proj_b")),
        "bn_b": bn("bdw", "bs", "bo"), "bn_g": bn("gdw", "gs", "go"), "bn_be": bn("bedw", "bes", "beo"),
        "bn_m": bn("mdw", "ms", "mo"), "bn_v": bn("vdw", "vs", "vo"),
        "wdw": z2("wdw").reshape(2, P, 9).transpose(1, 0, 2),
        "ws": np.repeat(ws.T.reshape(2, 2, 4).transpose(1, 0, 2), C // 4, 0),
        "qkv_b3": col(z3("b_qkv")), "out3_b": col(z3("b_out")), "gamma1": col(z3("gamma1")),
        "beta1": col(z3("beta1")), "gamma2": col(z3("gamma2")), "beta2": col(z3("beta2")),
    }
    vpack = np.ascontiguousarray(np.concatenate([vec[n].reshape(P, w) for n, w in VSEC], 1))
    w8 = np.ascontiguousarray(np.stack([np.stack([z0(f"xw{s}")[:R_DT], z0(f"dtw{s}").T], 1) for s in (1, 2, 3)], 1))

    arrays = {"x": np.ascontiguousarray(a["x"].reshape(B, C, L)), "wpack": wpack, "vpack": vpack, "w8": w8}
    nc = bacc.Bacc("TRN2", target_bir_lowering=False, num_devices=1)
    args = [nc.dram_tensor(n, t.shape, F32, kind="ExternalInput").ap() for n, t in arrays.items()]
    out = nc.dram_tensor("out", (B, C, L), F32, kind="ExternalOutput").ap()
    build(nc, *args, out)
    r = run_bass_kernel_spmd(nc, [arrays], core_ids=[0])
    return r.results[0]["out"].reshape(B, C, HH, WW)
```

```python
from contextlib import ExitStack

import concourse.bass as bass
from concourse import mybir

F32 = mybir.dt.float32
F32R = mybir.dt.float32r
ACT = mybir.ActivationFunctionType
ALU = mybir.AluOpType
AX = mybir.AxisListType

P = 128
B, C, HH, WW = 8, 256, 32, 32
L = HH * WW
CT = C // P
N = 512
NC = L // N
HEADS, DH = 8, 32
GH = 4
GROUPS = HEADS // GH
KT = L // P
D_IN, NST, R_DT = 128, 16, 8
DPG = P // NST
SG = D_IN // DPG
L2, L3 = L // 4, L // 16
W3 = L2 + L3
COLS = 2 * L + W3
PASS_AT = (0, L, 2 * L)
PASS_W = (L, L, W3)
SUM_LATE = 6
SUM_AFTER_NORM = 8
Y_AT, MEAN_AT, CENTER_AT, SQUARE_AT, VAR_AT, ROOT_AT, SCALE_AT = 3, 5, 4, 5, 7, 7, 8
RATES = (1, 6, 12, 18)
TAPS = [(1, 1)] + [(y, x) for y in range(3) for x in range(3) if (y, x) != (1, 1)]
SCALE = float(DH) ** -0.5
PHASES = GROUPS * NC
HALF_ROWS = (5, 4, 4, 4, 5, 5, 5, 0)
TURN_AT = 7
AHEAD = 3
NORM_AT = 4
PHASE_ROWS = sum(HALF_ROWS) // NC
POOL_SUMS = (0, 1, 2, 3, 5, 6)
DVE_SUMS = (0, 1, 2, 3, 4, 5, 6)
SMALL_U = 1.0 / 128

WSEC = [("in_w", 2 * 256), ("c1", 128), ("c2", 4 * 128), ("c3", 4 * 128),
        ("xb", 3 * 128), ("xc", 3 * 128), ("out", 256),
        ("qkv1", 2 * 768), ("proj1", 2 * 256), ("wo", 2 * 256), ("qkv3", 2 * 768), ("out3", 2 * 256)]
WOFF, WTOT = {}, 0
for _n, _w in WSEC:
    WOFF[_n] = WTOT
    WTOT += _w

VSEC = [("in_b", 2), ("c1_b", 1), ("c2_b", 1), ("c3_b", 1), ("out_b", 2), ("dtb", 3), ("Dv", 3),
        ("g", 3), ("be", 3), ("Al", 3 * SG), ("qkv_b1", 6), ("proj_b", 2),
        ("bn_b", 6), ("bn_g", 6), ("bn_be", 6), ("bn_m", 6), ("bn_v", 6), ("wdw", 18), ("ws", 8),
        ("qkv_b3", 6), ("out3_b", 2), ("gamma1", 2), ("beta1", 2), ("gamma2", 2), ("beta2", 2)]
VOFF, VTOT = {}, 0
for _n, _w in VSEC:
    VOFF[_n] = VTOT
    VTOT += _w


class Signal:

    def __init__(self, sem, per):
        self.sem, self.per = sem, per

    def __call__(self, b, k):
        return self.sem, b * self.per + k


def build(nc, x, wpack, vpack, w8, out):
    with ExitStack() as ctx:
        sb = lambda name, shape, dt=F32: ctx.enter_context(nc.sbuf_tensor(name, shape, dt))

        def sig(name, per):
            return Signal(ctx.enter_context(nc.semaphore(name)), per)

        sem = lambda name: ctx.enter_context(nc.semaphore(name))

        xin = sb("xin", [P, CT, L])
        xr = sb("xr", [P, CT, L])
        xg = sb("xg", [P, CT, L])
        W = sb("W", [P, WTOT])
        V = sb("V", [P, VTOT])
        W8 = sb("W8", [R_DT, 3, 2, P])
        Wd = sb("Wd", [P, 3, P])
        ident = sb("ident", [P, P])
        id2 = sb("id2", [P, 64])
        g8 = sb("g8", [P, P])
        mean128 = sb("mean128", [P, P])
        mean256 = sb("mean256", [P, P])
        ones32 = sb("ones32", [P, 32])
        e8 = sb("e8", [P, DPG])
        ysel = sb("ysel", [P, 4, 32])
        sel = sb("sel", [P, 8, P], F32R)
        DW = sb("DW", [P, 2, 9, P])
        MX = sb("MX", [P, 2, 256])
        Aneg = sb("Aneg", [P, 3 * SG])
        binv = sb("binv", [P, 6])
        bbias = sb("bbias", [P, 6])
        bes = sb("bes", [P, 3])
        eps = sb("eps", [P, 1])
        mhalf = sb("mhalf", [P, 1])
        small = sb("small", [P, 64])
        st = small[:, 0:24].rearrange("p (t c s) -> p t c s", t=2, c=2)
        msum = small[:, 24:26]
        dev = small[:, 46:54].rearrange("p (t q) -> p t q", t=2)
        dd = small[:, 54:62].rearrange("p (t q) -> p t q", t=2)
        m2 = small[:, 30:32]
        lnv = small[:, 32:34]
        rs = small[:, 34:36]
        sh = small[:, 36:38]
        tmp6 = small[:, 40:46]
        PS = ctx.enter_context(nc.psum_tensor("PS", [P, 8, N], F32))

        with ExitStack() as over:
            so = lambda name, shape, dt=F32: over.enter_context(nc.sbuf_tensor(name, shape, dt))
            Brep = so("Brep", [P, COLS])
            Crep = so("Crep", [P, COLS])
            work = so("work", [P, 12, L])
            yv = so("yv", [P, 3, L])
            f1 = so("f1", [P, L])
            f23 = so("f23", [P, W3])
            dstk = so("dstk", [P, 2, COLS], F32R)
            ustk = so("ustk", [P, 2, COLS], F32R)
        with ExitStack() as over:
            so = lambda name, shape, dt=F32: over.enter_context(nc.sbuf_tensor(name, shape, dt))
            QS = so("QS", [98, NC, HEADS, N], F32R)
            KS = so("KS", [98, HEADS, L], F32R)
            piece = so("piece", [P, 2, 2, L], F32R)
            Vt = so("Vt", [P, KT, C])
            PT = so("PT", [P, 3, GH, N])
            oT = so("oT", [P, CT, L])
            lr = so("lr", [P, 2, N])
            mx = so("mx", [P, NC, PHASE_ROWS])
            mboth = so("mboth", [P, PHASE_ROWS])
            nm = so("nm", [PHASE_ROWS, 2, P], F32R)
        with ExitStack() as over:
            so = lambda name, shape, dt=F32: over.enter_context(nc.sbuf_tensor(name, shape, dt))
            br = so("br", [P, 2, L])
            zm = so("zm", [P, 2, L])
            rl = so("rl", [P, 4, N])
        acc = piece.rearrange("p a b n -> p (a b n)").bitcast(F32).rearrange("p (s j n) -> p s j n", s=2, j=GH)
        pair = lambda a, e: lambda ps: (work[:, a, :], yv[:, e, :])[ps % 2][:, 0:PASS_W[ps]]
        cut_of, dl_of, ux_of = pair(6, 2), pair(7, 0), pair(8, 1)
        dBx_slot = lambda n: (work[:, 2, :], work[:, 3, :], yv[:, 2, :])[n % 3]
        sel32 = work[:, 0, :].rearrange("p (g m) -> p g m", g=8)
        sq = PT[:, 0, :, :]
        rstd = PT[:, 1, :, :]

        w_in = W[:, WOFF["in_w"]:WOFF["in_w"] + 512].rearrange("p (k m) -> p k m", k=2)
        w_c1 = W[:, WOFF["c1"]:WOFF["c1"] + 128]
        w_c2 = W[:, WOFF["c2"]:WOFF["c2"] + 512].rearrange("p (k m) -> p k m", k=4)
        w_c3 = W[:, WOFF["c3"]:WOFF["c3"] + 512].rearrange("p (k m) -> p k m", k=4)
        w_xb = W[:, WOFF["xb"]:WOFF["xb"] + 384].rearrange("p (s m) -> p s m", s=3)
        w_xc = W[:, WOFF["xc"]:WOFF["xc"] + 384].rearrange("p (s m) -> p s m", s=3)
        w_out = W[:, WOFF["out"]:WOFF["out"] + 256]
        w_qkv = [W[:, WOFF[n]:WOFF[n] + 1536].rearrange("p (k m) -> p k m", k=2) for n in ("qkv1", "qkv3")]
        w_proj = [W[:, WOFF[n]:WOFF[n] + 512].rearrange("p (k m) -> p k m", k=2) for n in ("proj1", "out3")]
        w_o = W[:, WOFF["wo"]:WOFF["wo"] + 512].rearrange("p (k m) -> p k m", k=2)
        v = lambda name, i=0, n=1: V[:, VOFF[name] + i:VOFF[name] + i + n]

        loaded = sem("loaded")
        built = sem("built")
        folded = sem("folded")
        prepared = sem("prepared")
        logged = sem("logged")

        xin_here = sig("xin_here", 16)
        xr_free = sig("xr_free", 16)
        gn_st, gn_sum, gn_dev, gn_dd, gn_q = sig("gn_st", 16), sig("gn_sum", 4), sig("gn_dev", 4), sig("gn_dd", 4), sig("gn_q", 4)
        gn_gm, gn_m2, gn_gv = sig("gn_gm", 4), sig("gn_m2", 4), sig("gn_gv", 4)
        gn_ln, gn_rs, gn_sh = sig("gn_ln", 4), sig("gn_rs", 4), sig("gn_sh", 4)
        gn_xa, gn_xb = sig("gn_xa", 4), sig("gn_xb", 4)
        xp_ps, xp_sb = sig("xp_ps", 2), sig("xp_sb", 2)
        f1_ps, f1_sb = sig("f1_ps", 2), sig("f1_sb", 2)
        f2_ps, f2_sb = sig("f2_ps", 1), sig("f2_sb", 1)
        f3_ps, f3_sb = sig("f3_ps", 1), sig("f3_sb", 1)
        pre_ps, brep_ps, crep_ps = sig("pre_ps", 3), sig("brep_ps", 3), sig("crep_ps", 3)
        brep_sb, crep_sb = sig("brep_sb", 3), sig("crep_sb", 3)
        sp_abs, sp_pos, sp_exp, sp_one = sig("sp_abs", 4), sig("sp_pos", 4), sig("sp_exp", 3), sig("sp_one", 3)
        sp_ln, sp_cut, sp_sum = sig("sp_ln", 3), sig("sp_cut", 3), sig("sp_sum", 3)
        sp_q, sp_qu, sp_poly, sp_big, sp_one_of = (sig(n, 3) for n in ("sp_q", "sp_qu", "sp_poly", "sp_big", "sp_one_of"))
        step, stepx, stepx_short = sig("step", 3), sig("stepx", 2), sig("stepx_short", 1)
        heads_d, heads_u = sig("heads_d", 8), sig("heads_u", 4)
        rests_in = sig("rests_in", 8)
        rests_pool = sig("rests_pool", 4)
        d_ps, u_ps = sig("d_ps", 48), sig("u_ps", 48)
        dA_sb, dBx_sb = sig("dA_sb", 64), sig("dBx_sb", 48)
        scanned, hC_sb, y_ps = sig("scanned", 96), sig("hC_sb", 48), sig("y_ps", 12)
        y_sb = sig("y_sb", 6)
        lm_ps, lm_d, lm_sq, lv_ps = sig("lm_ps", 4), sig("lm_d", 4), sig("lm_sq", 4), sig("lv_ps", 4)
        lv_ln, lv_rs, ln_n = sig("lv_ln", 4), sig("lv_rs", 4), sig("ln_n", 4)
        levels = sig("levels", 10)
        z_ps, z_sb, gated = sig("z_ps", 2), sig("z_sb", 1), sig("gated", 1)
        o_ps, x_new = sig("o_ps", 16), sig("x_new", 16)
        qk_ps, qk_head, qk_rest = sig("qk_ps", 8), sig("qk_head", 8), sig("qk_rest", 8)
        stackedq = [[sig(f"stackedq{g}{j}", 2 * 3 * 16) for j in range(GH)] for g in range(GROUPS)]
        stackedk = [[sig(f"stackedk{g}{j}", 2 * 3 * 16) for j in range(GH)] for g in range(GROUPS)]
        ones_in = sig("ones_in", 1)
        v_ps, v_sb = sig("v_ps", 4), sig("v_sb", 4)
        r_ps, r_max = sig("r_ps", 2 * HEADS * KT * NC), sig("r_max", 2 * HEADS * KT * NC)
        m_both = sig("m_both", 2 * PHASES)
        mt_ps, nm_head, nm_rest = (sig(n, 2 * PHASES) for n in ("mt_ps", "nm_head", "nm_rest"))
        nm_in = sig("nm_in", 2 * PHASES * 2 * 16)
        sum_pool = sig("sum_pool", 2 * (PHASES - 1) * (len(POOL_SUMS) - 1))
        sum_dve = sig("sum_dve", 2 * (len(DVE_SUMS) - 1))
        s_ps, p_sb = sig("s_ps", 128), sig("p_sb", 128)
        pv_ps, den_ln, den_rc = sig("pv_ps", 64), sig("den_ln", 8), sig("den_rc", 8)
        o_raw, o_sb = sig("o_raw", 8), sig("o_sb", 8)
        cm_ps, cm_d, cm_sq, cv_ps = sig("cm_ps", 4), sig("cm_d", 8), sig("cm_sq", 8), sig("cv_ps", 4)
        cv_ln, cv_rs, cn_n, cn_xa, cn_xb = sig("cv_ln", 4), sig("cv_rs", 4), sig("cn_n", 8), sig("cn_xa", 4), sig("cn_xb", 4)
        x3n = sig("x3n", 2)
        dw_ps, dw_sb, mix_ps, mix_sb = sig("dw_ps", 4), sig("dw_sb", 4), sig("mix_ps", 4), sig("mix_sb", 4)
        wo_sb = sig("wo_sb", 4)

        NLOAD = 16 * 7
        NBUILT = 21
        NPREP = 38

        def norm_job(k):
            return [(L, yv[:, 0, :], xg[:, 1, :], 0, 0), (L, yv[:, 1, :], xg[:, 1, :], 0, 0),
                    (W3, yv[:, 2, 0:W3], work[:, 2, 0:W3], 6, 4),
                    (W3, yv[:, 2, N:N + W3], work[:, 3, 0:W3], 7, 5)][k]

        by_chunk = lambda t: t.rearrange("p (c n) -> p c n", c=NC)
        out_v = out.rearrange("b (t p) n -> b p t n", p=P)
        x_v = x.rearrange("b (t p) n -> b p t n", p=P)

        block = ctx.enter_context(nc.Block())

        @block.sync
        def _(sp):
            sp.dma_start(xin[:, :, :], x_v[0]).then_inc(xin_here.sem, 16)
            sp.dma_start(V[:, :], vpack).then_inc(xr_free.sem, 16)
            sp.dma_start(W8[:, :, :, :], w8).then_inc(loaded, 16)
            cuts = [0, WOFF["c1"], WOFF["xb"], WOFF["qkv1"], WOFF["wo"], WOFF["qkv3"], WTOT]
            for a, e in zip(cuts, cuts[1:]):
                sp.dma_start(W[:, a:e], wpack[:, a:e]).then_inc(loaded, 16)

            def attention(b, a):
                for g in range(GROUPS):
                    n = 4 * a + 2 * g
                    def queries(j):
                        for blk, part in enumerate((0, 1, 0)):
                            sp.dma_start(QS[32 * blk:32 * blk + 32, :, GH * g + j, :].bitcast(F32),
                                         by_chunk(piece[32 * j:32 * j + 32, 0, part, :]).bitcast(F32)).then_inc(stackedq[g][j].sem, 16)

                    sp.wait_ge(*qk_rest(b, n + 1))
                    for j in range(AHEAD):
                        queries(j)
                    sp.wait_ge(*qk_rest(b, n + 2))
                    for j in range(GH):
                        for blk, part in enumerate((0, 0, 1)):
                            sp.dma_start(KS[32 * blk:32 * blk + 32, GH * g + j, :].bitcast(F32),
                                         piece[32 * j:32 * j + 32, 1, part, :].bitcast(F32)).then_inc(stackedk[g][j].sem, 16)
                        if j + AHEAD < GH:
                            queries(j + AHEAD)
                for ph in range(PHASES):
                    g, c = divmod(ph, NC)
                    sp.wait_ge(*nm_rest(b, PHASES * a + ph + 1))
                    for part in range(2):
                        sp.dma_start(QS[96 + part:97 + part, c, GH * g:GH * g + GH, :].bitcast(F32),
                                     nm[:, part, :].bitcast(F32)).then_inc(nm_in.sem, 16)

            def sample(b, last):
                sp.wait_ge(*x_new(b, 4))
                if not last:
                    sp.dma_start(xin[:, :, :], x_v[b + 1]).then_inc(xin_here.sem, 16)
                else:
                    sp.dma_start(xin[0:1, 0, 0:N], x_v[b][0:1, 0, 0:N]).then_inc(xin_here.sem, 16)
                attention(b, 0)
                attention(b, 1)
                sp.wait_ge(*x_new(b, 16))
                sp.dma_start(out_v[b], xr[:, :, :]).then_inc(xr_free.sem, 16)

            with sp.Fori(0, B - 1) as b:
                sample(b, False)
            sample(B - 1, True)
            sp.wait_ge(*xr_free(B - 1, 32))

        @block.gpsimd
        def _(pool):
            nb = [0]

            def step_(ins):
                nb[0] += 1
                ins.then_inc(built, 1)
                pool.wait_ge(built, nb[0])

            step_(pool.memset(ident[:, :], 0.0))
            step_(pool.affine_select(out=ident[:, :], in_=ident[:, :], compare_op=ALU.not_equal, fill=1.0,
                                     base=0, pattern=[[-1, P]], channel_multiplier=1))
            step_(pool.memset(g8[:, :], 1.0 / 32))
            gv = g8[:, :].rearrange("p (k r) -> p k r", r=8)
            step_(pool.affine_select(out=gv, in_=gv, compare_op=ALU.is_ge, fill=0.0, base=0,
                                     pattern=[[-8, 16], [0, 8]], channel_multiplier=1))
            step_(pool.affine_select(out=gv, in_=gv, compare_op=ALU.is_ge, fill=0.0, base=7,
                                     pattern=[[8, 16], [0, 8]], channel_multiplier=-1))
            step_(pool.memset(e8[:, :], 1.0))
            step_(pool.affine_select(out=e8[:, :], in_=e8[:, :], compare_op=ALU.is_ge, fill=0.0, base=0,
                                     pattern=[[-NST, DPG]], channel_multiplier=1))
            step_(pool.affine_select(out=e8[:, :], in_=e8[:, :], compare_op=ALU.is_ge, fill=0.0, base=NST - 1,
                                     pattern=[[NST, DPG]], channel_multiplier=-1))
            step_(pool.memset(ysel[:, :, :], 0.0))
            for i in range(4):
                step_(pool.tensor_copy(ysel[:, i, 8 * i:8 * i + 8], e8[:, :]))
            step_(pool.memset(sel32[:, :, :], 0.0))
            for base in (0, -64):
                s4 = sel32[:, :, :].rearrange("p g (d n) -> p g d n", n=NST)
                step_(pool.affine_select(out=s4, in_=s4, compare_op=ALU.not_equal, fill=1.0, base=base,
                                         pattern=[[-8, 8], [-1, 8], [0, NST]], channel_multiplier=1))
            step_(pool.memset(mean128[:, :], 1.0 / 128))
            step_(pool.memset(mean256[:, :], 1.0 / 256))
            step_(pool.memset(ones32[:, :], 1.0))
            step_(pool.memset(eps[:, :], 1e-5))
            step_(pool.memset(mhalf[:, :], -0.5))

            def sample(b):
                def rests(ps):
                    at, w = PASS_AT[ps], PASS_W[ps]
                    pool.wait_ge(*(sp_qu(b, 2) if ps == 0 else stepx(b, 2)))
                    pool.wait_ge(*heads_u(b, 2 * ps + 2))
                    for hh in range(2):
                        if hh == 1:
                            pool.wait_ge(*rests_pool(b, 2 * ps + 1))
                        r, ro = slice(64 * hh, 64 * hh + 64), slice(64 - 64 * hh, 128 - 64 * hh)
                        pool.tensor_tensor(ustk[ro, hh, at:at + w], ux_of(ps)[r, :], ustk[r, hh, at:at + w].bitcast(F32),
                                           ALU.subtract).then_inc(rests_pool.sem, 1)

                for ps in range(2):
                    at, w = PASS_AT[ps], PASS_W[ps]
                    tu, qu = work[:, ps % 2, 0:w], work[:, 10, 0:w]
                    pool.wait_ge(*sp_q(b, ps + 1))
                    pool.tensor_tensor(qu, qu, tu, ALU.mult).then_inc(sp_qu.sem, 1)
                    if ps >= 1:
                        rests(ps - 1)
                    if ps >= 1:
                        pool.wait_ge(*rests_pool(b, 2 * ps))
                    pool.wait_ge(*step(b, ps + 1))
                    pool.wait_ge(*f1_sb(b, 2))
                    pool.tensor_tensor(ux_of(ps), dl_of(ps), f1[:, :], ALU.mult).then_inc(stepx.sem, 1)
                rests(1)
                pool.wait_ge(*rests_pool(b, 4))
                for n in range(3 * SG):
                    ps, at = n // SG, PASS_AT[n // SG]
                    if n >= 6:
                        pool.wait_ge(*y_ps(b, (n - 6) // 4 + 1))
                    if n == 0:
                        pool.wait_ge(*crep_sb(b, 3))
                    slot = work[:, 6 + n % 6, :]
                    h = work[:, 4 + n % 2, :]
                    if ps < 2:
                        pool.wait_ge(*scanned(b, n + 1))
                        pool.tensor_tensor(slot, h, Crep[:, at:at + L], ALU.mult).then_inc(hC_sb.sem, 1)
                    else:
                        pool.wait_ge(*scanned(b, 32 + 4 * (n - 32) + 4))
                        two = lambda t: t.rearrange("p (d w) -> p d w", d=2)[:, :, 0:W3]
                        pool.tensor_tensor(two(slot), two(h), Crep[:, None, at:at + W3].broadcast_to((P, 2, W3)),
                                           ALU.mult).then_inc(hC_sb.sem, 1)
                pool.wait_ge(*x_new(b, 4))
                one = ones32[96:98, 0:1].broadcast_to((2, HEADS * L))
                pool.tensor_tensor(KS[96:98, :, :].rearrange("p h n -> p (h n)"), one, one,
                                   ALU.mult).then_inc(ones_in.sem, 1)
                for a in range(2):
                    for j in range(GH):
                        pool.wait_ge(*stackedq[1][j](b, (a + 1) * 48))
                        pool.wait_ge(*stackedk[1][j](b, (a + 1) * 48))
                    for ph in range(PHASES - 1):
                        if ph == 2:
                            pool.wait_ge(*pv_ps(b, (PHASES * a + 1) * KT))
                        for k in range(1, len(POOL_SUMS)):
                            i, total = key_step(a, ph, POOL_SUMS[k]), acc[:, ph % 2, :, :]
                            first = PT[:, key_step(a, ph, 0) % 3, :, :] if k == 1 else total
                            if k > 1:
                                pool.wait_ge(*sum_pool(b, pool_sums(a, ph, k - 1)))
                            pool.wait_ge(*p_sb(b, 2 * i + 2))
                            pool.tensor_tensor(total, first, PT[:, i % 3, :, :], ALU.add).then_inc(sum_pool.sem, 1)
                pool.wait_ge(*x_new(b, 16))

            with pool.Fori(0, B) as b:
                sample(b)

        @block.scalar
        def _(act):
            act.preload_act_table_set("natural_log_exp_and_others")
            act.wait_ge(loaded, NLOAD)
            act.wait_ge(xr_free.sem, 16)
            act.wait_ge(built, NBUILT)
            act.activation(Aneg[:, :], v("Al", 0, 3 * SG), ACT.Exp).then_inc(logged, 1)
            act.activation(tmp6, v("bn_v", 0, 6), ACT.Ln, bias=eps[:, :]).then_inc(logged, 1)
            act.wait_ge(logged, 2)
            act.activation(tmp6, tmp6, ACT.Exp, scale=-0.5).then_inc(logged, 1)

            def group_norm(b, s, X):
                act.wait_ge(*gn_gv(b, s + 1))
                act.activation(lnv, PS[:, 6, 0:2], ACT.Ln, scale=4.0 / L, bias=eps[:, :]).then_inc(gn_ln.sem, 1)
                act.wait_ge(*gn_ln(b, s + 1))
                act.activation(rs, lnv, ACT.Exp, scale=-0.5).then_inc(gn_rs.sem, 1)
                act.wait_ge(*gn_rs(b, s + 1))
                act.wait_ge(*gn_sh(b, s + 1))
                act.activation(xg[:, 1, :], X[:, 1, :], ACT.Identity, scale=rs[:, 1:2],
                               bias=sh[:, 1:2]).then_inc(gn_xb.sem, 1)

            def block0(b):
                for c in range(NC):
                    act.wait_ge(*xp_ps(b, c + 1))
                    act.activation(yv[:, 0, c * N:c * N + N], PS[:, c, :], ACT.Identity,
                                   bias=v("in_b", 0)).then_inc(xp_sb.sem, 1)
                def head_of_input(ps):
                    at, w = PASS_AT[ps], PASS_W[ps]
                    act.wait_ge(*stepx(b, ps + 1))
                    for hh in range(2):
                        r = slice(64 * hh, 64 * hh + 64)
                        act.activation(ustk[r, hh, at:at + w], ux_of(ps)[r, :], ACT.Copy).then_inc(heads_u.sem, 1)

                for ps in range(3):
                    at, w = PASS_AT[ps], PASS_W[ps]
                    tu, tl = work[:, ps % 2, 0:w], work[:, 2 + ps % 2, 0:w]
                    act.wait_ge(*pre_ps(b, ps + 1))
                    if ps == 2:
                        act.wait_ge(*step(b, 1))
                    if ps < 2:
                        src = PS[:, (0, 6)[ps]:(0, 6)[ps] + 2, :].rearrange("p a n -> p (a n)")
                        act.activation(tu, src, ACT.Abs, bias=v("dtb", ps)).then_inc(sp_abs.sem, 1)
                    else:
                        act.activation(tu[:, 0:L2], PS[:, 4, 0:L2], ACT.Abs, bias=v("dtb", 1)).then_inc(sp_abs.sem, 1)
                        act.activation(tu[:, L2:W3], PS[:, 4, L2:W3], ACT.Abs, bias=v("dtb", 2)).then_inc(sp_abs.sem, 1)
                    for a_, e_, bias in (((0, w, v("dtb", ps)),) if ps < 2 else ((0, L2, v("dtb", 1)), (L2, W3, v("dtb", 2)))):
                        if ps < 2:
                            act.activation(work[:, 4 + ps, :], src, ACT.Relu, bias=bias).then_inc(sp_pos.sem, 1)
                        else:
                            act.activation(work[:, 4, a_:e_], PS[:, 4, a_:e_], ACT.Relu, bias=bias).then_inc(sp_pos.sem, 1)
                    if ps == 0:
                        act.wait_ge(*f2_ps(b, 1))
                        act.activation(f23[:, 0:L2], PS[:, 4, 0:L2], ACT.Identity, bias=v("c2_b")).then_inc(f2_sb.sem, 1)
                    act.wait_ge(*sp_abs(b, (1, 2, 4)[ps]))
                    act.activation(tu, tu, ACT.Exp, scale=-1.0).then_inc(sp_exp.sem, 1)
                    act.wait_ge(*sp_exp(b, ps + 1))
                    if ps == 2:
                        act.wait_ge(*sp_sum(b, 1))
                    act.activation(tl, tu, ACT.Ln, bias=1.0).then_inc(sp_ln.sem, 1)
                    if ps == 0:
                        act.wait_ge(*f3_ps(b, 1))
                        act.activation(f23[:, L2:W3], PS[:, 5, 0:L3], ACT.Identity, bias=v("c3_b")).then_inc(f3_sb.sem, 1)
                    if ps >= 1:
                        act.wait_ge(*sp_cut(b, ps))
                        act.wait_ge(*sp_poly(b, ps))
                    act.activation(work[:, 9, 0:w], tu, ACT.Identity, bias=1.0).then_inc(sp_one.sem, 1)
                    act.activation(work[:, 10, 0:w], tu, ACT.Identity, scale=1.0 / 3, bias=mhalf[:, :]).then_inc(sp_q.sem, 1)
                    for dst, src_ps, done, bank in ((Brep, brep_ps, brep_sb, (2, 0, 6)), (Crep, crep_ps, crep_sb, (4, 2, 0))):
                        act.wait_ge(*src_ps(b, ps + 1))
                        src = PS[:, bank[ps]:bank[ps] + 2, :].rearrange("p a n -> p (a n)")[:, 0:w]
                        act.activation(dst[:, at:at + w], src, ACT.Copy).then_inc(done.sem, 1)
                    if ps == 1:
                        head_of_input(0)
                act.wait_ge(*z_ps(b, 2))
                act.activation(xg[:, 0, :], PS[:, 2:4, :].rearrange("p a n -> p (a n)"), ACT.Silu,
                               bias=v("in_b", 1)).then_inc(z_sb.sem, 1)
                act.preload_act_table_set("natural_log_exp_and_others")
                head_of_input(1)

                def norm_squares(k):
                    w, ybuf, t, mb, vb = norm_job(k)
                    act.wait_ge(*lm_d(b, k + 1))
                    act.activation(t, ybuf, ACT.Square).then_inc(lm_sq.sem, 1)

                def norm_roots(k):
                    w, ybuf, t, mb, vb = norm_job(k)
                    act.wait_ge(*lv_ps(b, k + 1))
                    src = PS[:, vb:vb + 2, :].rearrange("p a n -> p (a n)")[:, 0:w] if w > N else PS[:, vb, 0:w]
                    act.activation(t, src, ACT.Ln, bias=eps[:, :]).then_inc(lv_ln.sem, 1)
                    act.wait_ge(*lv_ln(b, k + 1))
                    act.activation(t, t, ACT.Exp, scale=-0.5).then_inc(lv_rs.sem, 1)

                act.wait_ge(*rests_in(b, 8))
                act.wait_ge(*rests_pool(b, 4))
                for n in range(3 * SG):
                    ps = n // SG
                    g = scan_group(n)
                    slot = 2 + 2 * ((2 * n + 1) % 3)
                    if n >= 2:
                        act.wait_ge(*scanned(b, scans(n - 2)))
                    act.wait_ge(*d_ps(b, n + 1))
                    dst = work[:, n % 2, :]
                    src = PS[:, slot:slot + 2, :].rearrange("p a n -> p (a n)")
                    if ps < 2:
                        act.activation(dst, src, ACT.Exp, scale=Aneg[:, ps * SG + g:ps * SG + g + 1]).then_inc(dA_sb.sem, 1)
                    else:
                        act.activation(dst[:, 0:L2], src[:, 0:L2], ACT.Exp,
                                       scale=Aneg[:, SG + g:SG + g + 1]).then_inc(dA_sb.sem, 1)
                        act.activation(dst[:, L2:W3], src[:, L2:W3], ACT.Exp,
                                       scale=Aneg[:, 2 * SG + g:2 * SG + g + 1]).then_inc(dA_sb.sem, 1)
                    for k in range(2):
                        if n == SG * (k + 1) + SQUARE_AT:
                            norm_squares(k)
                        if n == SG * (k + 1) + ROOT_AT:
                            norm_roots(k)
                for k in (2, 3):
                    norm_squares(k)
                for k in (2, 3):
                    norm_roots(k)

            def chan_norm(b, s, X, gamma, beta):
                for c in range(NC):
                    n = NC * s + c
                    for t in range(CT):
                        act.wait_ge(*cm_d(b, 2 * n + t + 1))
                        act.activation(sq[:, 2 * c + t, :], X[:, t, c * N:c * N + N], ACT.Square).then_inc(cm_sq.sem, 1)
                for c in range(NC):
                    n = NC * s + c
                    act.wait_ge(*cv_ps(b, n + 1))
                    act.activation(rstd[:, c, :], PS[:, 2 + c, :], ACT.Ln, bias=eps[:, :]).then_inc(cv_ln.sem, 1)
                    act.wait_ge(*cv_ln(b, n + 1))
                    act.activation(rstd[:, c, :], rstd[:, c, :], ACT.Exp, scale=-0.5).then_inc(cv_rs.sem, 1)
                for c in range(NC):
                    n = NC * s + c
                    act.wait_ge(*cn_n(b, 2 * n + 2))
                    act.activation(X[:, 1, c * N:c * N + N], X[:, 1, c * N:c * N + N], ACT.Identity,
                                   scale=v(gamma, 1), bias=v(beta, 1)).then_inc(cn_xb.sem, 1)

            def attention(b, a):
                bq = ("qkv_b1", "qkv_b3")[a]
                for g in range(GROUPS):
                    for kind in range(2):
                        n = 2 * g + kind
                        act.wait_ge(*qk_ps(b, 4 * a + n + 1))
                        if g == 1:
                            for done in (stackedq, stackedk)[kind][0]:
                                act.wait_ge(*done(b, (a + 1) * 48))
                        src = PS[:, 2 * kind:2 * kind + 2, :].rearrange("p a n -> p (a n)")
                        act.activation(piece[:, kind, 0, :], src, ACT.Identity,
                                       bias=v(bq, 2 * kind + g)).then_inc(qk_head.sem, 1)
                for q in range(2):
                    act.wait_ge(*v_ps(b, 2 * a + q + 1))
                    act.activation(Vt[:, 4 * q:4 * q + 4, :].rearrange("p k c -> p (k c)"),
                                   PS[:, 2 * q:2 * q + 2, :].rearrange("p a n -> p (a n)"), ACT.Copy).then_inc(v_sb.sem, 1)

                def neg_max(ph):
                    n = PHASES * a + ph
                    act.wait_ge(*mt_ps(b, n + 1))
                    if ph >= 1:
                        act.wait_ge(*nm_in(b, 32 * n))
                    act.activation(nm[:, 0, :], PS[0:PHASE_ROWS, 6, 0:P], ACT.Copy, scale=-1.0).then_inc(nm_head.sem, 1)

                def reciprocals(j):
                    act.wait_ge(*pv_ps(b, (j + 1) * KT))
                    act.activation(lr[:, 0, :], PS[:, 1, :], ACT.Ln).then_inc(den_ln.sem, 1)
                    act.wait_ge(*den_ln(b, j + 1))
                    if j % PHASES >= 1:
                        act.wait_ge(*o_raw(b, j))
                    act.activation(lr[:, 1, :], lr[:, 0, :], ACT.Exp, scale=-1.0).then_inc(den_rc.sem, 1)

                neg_max(0)
                for ph in range(PHASES):
                    for kt in range(KT):
                        i = key_step(a, ph, kt)
                        if kt == 0 and ph >= 1:
                            reciprocals(PHASES * a + ph - 1)
                        if i % (PHASES * KT) >= 3:
                            act.wait_ge(*pv_ps(b, i - 2))
                            done = summed(a, *divmod(i % (PHASES * KT) - 3, KT))
                            if done:
                                act.wait_ge(*(sum_pool, sum_dve)[done[0]](b, done[1]))
                        for pr in range(2):
                            act.wait_ge(*s_ps(b, 2 * i + pr + 1))
                            act.activation(PT[:, i % 3, 2 * pr:2 * pr + 2, :], PS[:, 2 + 2 * pr:4 + 2 * pr, :],
                                           ACT.Exp, scale=SCALE).then_inc(p_sb.sem, 1)
                        if kt == TURN_AT and ph < PHASES - 1:
                            neg_max(ph + 1)
                reciprocals(PHASES * a + PHASES - 1)

            def block2(b):
                for t in range(2):
                    for c in range(NC):
                        n = 2 * t + c
                        act.wait_ge(*dw_ps(b, n + 1))
                        act.activation(br[:, t, c * N:c * N + N], PS[:, n, :], ACT.Relu, scale=binv[:, t:t + 1],
                                       bias=bbias[:, t:t + 1]).then_inc(dw_sb.sem, 1)
                for m in range(2):
                    for c in range(NC):
                        n = 2 * m + c
                        act.wait_ge(*mix_ps(b, n + 1))
                        act.activation(zm[:, m, c * N:c * N + N], PS[:, 4 + n, :], ACT.Relu, scale=binv[:, 2 + m:3 + m],
                                       bias=bbias[:, 2 + m:3 + m]).then_inc(mix_sb.sem, 1)
                for m in range(2):
                    for c in range(NC):
                        n = 2 * m + c
                        act.wait_ge(*o_ps(b, 8 + n + 1))
                        act.activation(rl[:, n, :], PS[:, n, :], ACT.Relu, scale=binv[:, 4 + m:5 + m],
                                       bias=bbias[:, 4 + m:5 + m]).then_inc(wo_sb.sem, 1)

            group_norm(0, 0, xin)
            with act.Fori(0, B) as b:
                block0(b)
                act.wait_ge(*x_new(b, 4))
                group_norm(b, 1, xr)
                attention(b, 0)
                act.wait_ge(*x_new(b, 8))
                group_norm(b, 2, xr)
                block2(b)
                act.wait_ge(*x_new(b, 12))
                group_norm(b, 3, xr)
                chan_norm(b, 0, xg, "gamma1", "beta1")
                attention(b, 1)
                chan_norm(b, 1, oT, "gamma2", "beta2")
                group_norm(b, 4, xin)
                act.wait_ge(*x_new(b, 16))

        @block.vector
        def _(dve):
            dve.wait_ge(loaded, NLOAD)
            dve.wait_ge(xr_free.sem, 16)
            dve.wait_ge(built, NBUILT)
            dve.wait_ge(logged, 3)
            nprep = [0]

            def prep(ins):
                nprep[0] += 1
                ins.then_inc(prepared, 1)
                dve.wait_ge(prepared, nprep[0])

            prep(dve.tensor_copy(sel[:, :, :], sel32[:, :, :]))
            prep(dve.tensor_scalar(Aneg[:, :], Aneg[:, :], -1.0, None, ALU.mult))
            prep(dve.tensor_tensor(binv[:, :], tmp6, v("bn_g", 0, 6), ALU.mult))
            prep(dve.tensor_tensor(bbias[:, :], v("bn_b", 0, 6), v("bn_m", 0, 6), ALU.subtract))
            prep(dve.tensor_tensor(bbias[:, :], bbias[:, :], binv[:, :], ALU.mult))
            prep(dve.tensor_tensor(bbias[:, :], bbias[:, :], v("bn_be", 0, 6), ALU.add))
            prep(dve.tensor_tensor(bes[:, 0:1], v("be", 0), v("be", 1), ALU.add))
            prep(dve.tensor_tensor(bes[:, 1:3], v("be", 1, 2), v("be", 1, 2), ALU.add))
            prep(dve.tensor_tensor(id2[:, :], ident[:, 0:64], ident[:, 64:128], ALU.add))
            for t in range(2):
                for tap in range(9):
                    prep(dve.tensor_scalar(DW[:, t, tap, :], ident[:, :], v("wdw", 9 * t + tap), None, ALU.mult))
                for o in range(4):
                    prep(dve.tensor_scalar(MX[:, t, 64 * o:64 * o + 64], id2[:, :], v("ws", 4 * t + o), None, ALU.mult))
            for s in range(3):
                dve.wait_ge(folded, s + 1)
                prep(dve.tensor_copy(Wd[:, s, :], PS[:, s, 0:P]))

            def stats(X, n):
                t, c = divmod(n, NC)
                dve.bn_stats(st[:, t, c, :], X[:, t, c * N:c * N + N]).then_inc(gn_st.sem, 1)

            def stats_of_new(b, n):
                dve.wait_ge(*x_new(b, n + 1))
                stats(xr, n % 4)

            quarter = st.rearrange("p t c (e k) -> p t (c e) k", e=2)

            def norm_sum(b, s):
                dve.wait_ge(*gn_st(b, 4 * s + 4))
                dve.tensor_reduce(msum, quarter[:, :, :, 1], AX.X, ALU.add).then_inc(gn_sum.sem, 1)

            def norm_squares(b, s):
                dve.wait_ge(*gn_gm(b, s + 1))
                dve.tensor_tensor(dev, quarter[:, :, :, 1], PS[:, 7, 0:2, None].broadcast_to((P, CT, 4)),
                                  ALU.subtract).then_inc(gn_dev.sem, 1)
                dve.wait_ge(*gn_dev(b, s + 1))
                dve.tensor_tensor(dd, dev, dev, ALU.mult).then_inc(gn_dd.sem, 1)
                dve.wait_ge(*gn_dd(b, s + 1))
                dve.scalar_tensor_tensor(out=dd, in0=dd, scalar=float(L // 4), in1=quarter[:, :, :, 2],
                                         op0=ALU.mult, op1=ALU.add).then_inc(gn_q.sem, 1)
                dve.wait_ge(*gn_q(b, s + 1))
                dve.tensor_reduce(m2, dd, AX.X, ALU.add).then_inc(gn_m2.sem, 1)

            def norm_apply(b, s, X):
                dve.wait_ge(*gn_rs(b, s + 1))
                dve.scalar_tensor_tensor(out=sh, in0=PS[:, 7, 0:2], scalar=-1.0, in1=rs, op0=ALU.mult,
                                         op1=ALU.mult).then_inc(gn_sh.sem, 1)
                dve.wait_ge(*gn_sh(b, s + 1))
                dve.tensor_scalar(xg[:, 0, :], X[:, 0, :], rs[:, 0:1], sh[:, 0:1], ALU.mult, ALU.add).then_inc(gn_xa.sem, 1)

            def group_norm(b, s, X):
                norm_sum(b, s)
                norm_squares(b, s)
                norm_apply(b, s, X)

            def block0(b):
                for c in range(NC):
                    dve.wait_ge(*f1_ps(b, c + 1))
                    dve.tensor_scalar(f1[:, c * N:c * N + N], PS[:, 2 + c, :], v("c1_b"), None, ALU.add).then_inc(f1_sb.sem, 1)
                for ps in range(3):
                    at, w = PASS_AT[ps], PASS_W[ps]
                    tu, tl = work[:, ps % 2, 0:w], work[:, 2 + ps % 2, 0:w]
                    pos, cut, dl = work[:, 4 + ps % 2, 0:w], cut_of(ps), dl_of(ps)
                    one, qu, big = work[:, 9, 0:w], work[:, 10, 0:w], work[:, 11, 0:w]
                    dve.wait_ge(*sp_exp(b, ps + 1))
                    dve.tensor_scalar(big, tu, SMALL_U, None, ALU.is_ge).then_inc(sp_big.sem, 1)
                    dve.wait_ge(*sp_one(b, ps + 1))
                    dve.scalar_tensor_tensor(out=cut, in0=one, scalar=-1.0, in1=tu, op0=ALU.add,
                                             op1=ALU.subtract).then_inc(sp_cut.sem, 1)
                    dve.wait_ge(*sp_cut(b, ps + 1))
                    dve.tensor_tensor(cut, tl, cut, ALU.subtract).then_inc(sp_sum.sem, 1)
                    if ps == 2:
                        dve.wait_ge(*sp_q(b, 3))
                        dve.tensor_tensor(qu, qu, tu, ALU.mult).then_inc(sp_qu.sem, 1)
                    dve.wait_ge(*sp_qu(b, ps + 1))
                    if ps == 1:
                        dve.wait_ge(*f1_ps(b, 2))
                    if ps == 2:
                        dve.wait_ge(*stepx(b, 1))
                    dve.scalar_tensor_tensor(out=dl, in0=qu, scalar=1.0, in1=tu, op0=ALU.add,
                                             op1=ALU.mult).then_inc(sp_poly.sem, 1)
                    dve.wait_ge(prepared, NPREP)
                    dve.wait_ge(*sp_big(b, ps + 1))
                    dve.wait_ge(*sp_sum(b, ps + 1))
                    dve.wait_ge(*sp_poly(b, ps + 1))
                    dve.copy_predicated(dl, big.bitcast(mybir.dt.int32), cut).then_inc(sp_one_of.sem, 1)
                    dve.wait_ge(*sp_pos(b, (1, 2, 4)[ps]))
                    dve.wait_ge(*sp_one_of(b, ps + 1))
                    dve.tensor_tensor(dl, dl, pos, ALU.add).then_inc(step.sem, 1)
                    dve.wait_ge(*step(b, ps + 1))
                    for hh in range(2):
                        r = slice(64 * hh, 64 * hh + 64)
                        dve.tensor_copy(dstk[r, hh, at:at + w], dl[r, :]).then_inc(heads_d.sem, 1)
                    dve.wait_ge(*heads_d(b, 2 * ps + 2))
                    for hh in range(2):
                        r, ro = slice(64 * hh, 64 * hh + 64), slice(64 - 64 * hh, 128 - 64 * hh)
                        dve.tensor_tensor(dstk[ro, hh, at:at + w], dl[r, :], dstk[r, hh, at:at + w].bitcast(F32),
                                          ALU.subtract).then_inc(rests_in.sem, 1)
                    if ps == 2:
                        ux = ux_of(2)
                        dve.wait_ge(*rests_pool(b, 2))
                        dve.wait_ge(*f3_sb(b, 1))
                        dve.tensor_tensor(ux, dl, f23[:, :], ALU.mult).then_inc(stepx_short.sem, 1)
                        dve.wait_ge(*stepx_short(b, 1))
                        for hh in range(2):
                            r = slice(64 * hh, 64 * hh + 64)
                            dve.tensor_copy(ustk[r, hh, at:at + w], ux[r, :]).then_inc(heads_d.sem, 1)
                        dve.wait_ge(*heads_d(b, 8))
                        for hh in range(2):
                            r, ro = slice(64 * hh, 64 * hh + 64), slice(64 - 64 * hh, 128 - 64 * hh)
                            dve.tensor_tensor(ustk[ro, hh, at:at + w], ux[r, :], ustk[r, hh, at:at + w].bitcast(F32),
                                              ALU.subtract).then_inc(rests_in.sem, 1)
                dve.wait_ge(*brep_sb(b, 3))
                def center(k):
                    w, y, t, mb, vb = norm_job(k)
                    dve.wait_ge(*lm_ps(b, k + 1))
                    src = PS[:, mb:mb + 2, :].rearrange("p a n -> p (a n)") if w > N else PS[:, mb, 0:w]
                    dve.tensor_tensor(y, y, src, ALU.subtract).then_inc(lm_d.sem, 1)

                def scale(k):
                    w, y, t, mb, vb = norm_job(k)
                    dve.wait_ge(*lv_rs(b, k + 1))
                    dve.wait_ge(*lm_d(b, k + 1))
                    dve.tensor_tensor(y, y, t, ALU.mult).then_inc(ln_n.sem, 1)

                nl = [0]

                def chain(ins):
                    nl[0] += 1
                    ins.then_inc(levels.sem, 1)
                    dve.wait_ge(*levels(b, nl[0]))

                def state_inputs(n):
                    ps, at, w = n // SG, PASS_AT[n // SG], PASS_W[n // SG]
                    slot = 2 + 2 * ((2 * n) % 3)
                    dve.wait_ge(*u_ps(b, n + 1))
                    if n >= 3:
                        dve.wait_ge(*scanned(b, scans(n - 3)))
                    src = PS[:, slot:slot + 2, :].rearrange("p a n -> p (a n)")[:, 0:w]
                    dve.tensor_tensor(dBx_slot(n)[:, 0:w], src, Brep[:, at:at + w], ALU.mult).then_inc(dBx_sb.sem, 1)

                dve.wait_ge(*rests_pool(b, 4))
                state_inputs(0)
                for n in range(3 * SG):
                    ps = n // SG
                    dA, dBx, h = work[:, n % 2, :], dBx_slot(n), work[:, 4 + n % 2, :]
                    if n + 1 < 3 * SG:
                        state_inputs(n + 1)
                    dve.wait_ge(*dBx_sb(b, n + 1))
                    if n >= 2:
                        dve.wait_ge(*hC_sb(b, n - 1))
                    if ps < 2:
                        dve.wait_ge(*dA_sb(b, n + 1))
                        if ps == 0:
                            dve.tensor_tensor_scan(h, dA, dBx, 0.0, ALU.mult, ALU.add).then_inc(scanned.sem, 1)
                        else:
                            dve.tensor_tensor_scan(h[:, ::-1], dA[:, ::-1], dBx[:, ::-1], 0.0, ALU.mult,
                                                   ALU.add).then_inc(scanned.sem, 1)
                    else:
                        dve.wait_ge(*dA_sb(b, 32 + 2 * (n - 32) + 2))
                        for a_, e_ in ((0, L2), (L2, W3)):
                            dve.tensor_tensor_scan(h[:, a_:e_], dA[:, a_:e_], dBx[:, a_:e_], 0.0, ALU.mult,
                                                   ALU.add).then_inc(scanned.sem, 1)
                            rev = slice(e_ - 1, a_ - 1 if a_ else None, -1)
                            rev_o = slice(N + e_ - 1, N + a_ - 1, -1)
                            dve.tensor_tensor_scan(h[:, rev_o], dA[:, rev], dBx[:, rev], 0.0, ALU.mult,
                                                   ALU.add).then_inc(scanned.sem, 1)
                    for k in range(2):
                        at0 = SG * (k + 1)
                        y = yv[:, k, :]
                        if n == at0 + Y_AT:
                            dve.wait_ge(*y_ps(b, 4 * k + 4))
                            dve.scalar_tensor_tensor(out=y, in0=f1[:, :], scalar=v("Dv", k),
                                                     in1=PS[:, 0:2, :].rearrange("p a n -> p (a n)"),
                                                     op0=ALU.mult, op1=ALU.add).then_inc(y_sb.sem, 1)
                        if n == at0 + CENTER_AT:
                            center(k)
                        if n == at0 + SCALE_AT:
                            scale(k)
                        if n == at0 + SCALE_AT + 2:
                            dve.wait_ge(*ln_n(b, k + 1))
                            if k == 0:
                                chain(dve.tensor_scalar(y, y, v("g", 0), bes[:, 0:1], ALU.mult, ALU.add))
                            else:
                                chain(dve.scalar_tensor_tensor(out=yv[:, 0, :], in0=y, scalar=v("g", 1), in1=yv[:, 0, :],
                                                               op0=ALU.mult, op1=ALU.add))
                dve.wait_ge(*y_ps(b, 12))
                for d in range(2):
                    for s, a_, e_ in ((1, 0, L2), (2, L2, W3)):
                        dve.scalar_tensor_tensor(out=yv[:, 2, d * N + a_:d * N + e_], in0=f23[:, a_:e_],
                                                 scalar=v("Dv", s), in1=PS[:, d, a_:e_], op0=ALU.mult,
                                                 op1=ALU.add).then_inc(y_sb.sem, 1)
                for k in (2, 3):
                    center(k)
                for k in (2, 3):
                    scale(k)
                dve.wait_ge(*ln_n(b, 4))
                y1, y2, y3 = yv[:, 0, :], work[:, 10, 0:L2], work[:, 10, L2:W3]
                chain(dve.tensor_scalar(y3, yv[:, 2, L2:W3], v("g", 2), bes[:, 2:3], ALU.mult, ALU.add))
                chain(dve.scalar_tensor_tensor(out=y3, in0=yv[:, 2, N + L2:N + W3], scalar=v("g", 2), in1=y3,
                                               op0=ALU.mult, op1=ALU.add))
                chain(dve.tensor_scalar(y2, yv[:, 2, 0:L2], v("g", 1), bes[:, 1:2], ALU.mult, ALU.add))
                chain(dve.scalar_tensor_tensor(out=y2, in0=yv[:, 2, N:N + L2], scalar=v("g", 1), in1=y2,
                                               op0=ALU.mult, op1=ALU.add))

                def up(fine, coarse, side):
                    fv = fine.rearrange("p (h i w j) -> p h i w j", i=2, w=side, j=2)
                    cv = coarse.rearrange("p (h w) -> p h w", w=side)
                    wide = cv[:, :, :, None].broadcast_to((P, side, side, 2))
                    for i in range(2):
                        chain(dve.tensor_tensor(fv[:, :, i, :, :], fv[:, :, i, :, :], wide, ALU.add))

                up(y2, y3, WW // 4)
                up(y1, y2, WW // 2)
                dve.wait_ge(*xr_free(b, 16))
                dve.wait_ge(*z_sb(b, 1))
                dve.tensor_tensor(work[:, 11, :], y1, xg[:, 0, :], ALU.mult).then_inc(gated.sem, 1)
                for m in range(CT):
                    for c in range(NC):
                        n = 2 * m + c
                        cs = slice(c * N, c * N + N)
                        dve.wait_ge(*o_ps(b, n + 1))
                        dve.scalar_tensor_tensor(out=xr[:, m, cs], in0=PS[:, n, :], scalar=v("out_b", m),
                                                 in1=xin[:, m, cs], op0=ALU.add, op1=ALU.add).then_inc(x_new.sem, 1)
                        if n > 0:
                            stats_of_new(b, n - 1)
                stats_of_new(b, 3)

            def chan_norm(b, s, X, gamma, beta):
                for c in range(NC):
                    n = NC * s + c
                    dve.wait_ge(*cm_ps(b, n + 1))
                    for t in range(CT):
                        cs = slice(c * N, c * N + N)
                        dve.tensor_tensor(X[:, t, cs], X[:, t, cs], PS[:, c, :], ALU.subtract).then_inc(cm_d.sem, 1)
                for c in range(NC):
                    n = NC * s + c
                    dve.wait_ge(*cv_rs(b, n + 1))
                    dve.wait_ge(*cm_d(b, 2 * n + 2))
                    for t in range(CT):
                        cs = slice(c * N, c * N + N)
                        dve.tensor_tensor(X[:, t, cs], X[:, t, cs], rstd[:, c, :], ALU.mult).then_inc(cn_n.sem, 1)
                    dve.wait_ge(*cn_n(b, 2 * n + 1))
                    dve.tensor_scalar(X[:, 0, cs], X[:, 0, cs], v(gamma, 0), v(beta, 0), ALU.mult,
                                      ALU.add).then_inc(cn_xa.sem, 1)

            def attention(b, a):
                bq = ("qkv_b1", "qkv_b3")[a]

                def rest(g, kind):
                    n = 2 * g + kind
                    dve.wait_ge(*qk_head(b, 4 * a + n + 1))
                    src = PS[:, 2 * kind:2 * kind + 2, :].rearrange("p a n -> p (a n)")
                    dve.scalar_tensor_tensor(out=piece[:, kind, 1, :], in0=src, scalar=v(bq, 2 * kind + g),
                                             in1=piece[:, kind, 0, :].bitcast(F32), op0=ALU.add,
                                             op1=ALU.subtract).then_inc(qk_rest.sem, 1)

                def row_max(n, cc):
                    at = n % PHASE_ROWS
                    dve.wait_ge(*r_ps(b, halves(a, n, cc) + 1))
                    dve.tensor_reduce(mx[:, cc, at:at + 1], PS[:, row_slot(n, cc), :], AX.X,
                                      ALU.max).then_inc(r_max.sem, 1)
                    if at == PHASE_ROWS - 1 and cc == NC - 1:
                        ph = n // PHASE_ROWS
                        dve.wait_ge(*r_max(b, halves(a, n, NC - 1) + 1))
                        if ph > 0:
                            dve.wait_ge(*mt_ps(b, PHASES * a + ph))
                        dve.tensor_tensor(mboth[:, :], mx[:, 0, :], mx[:, 1, :], ALU.max).then_inc(m_both.sem, 1)

                def neg_max(ph):
                    dve.wait_ge(*nm_head(b, PHASES * a + ph + 1))
                    dve.scalar_tensor_tensor(out=nm[:, 1, :], in0=PS[0:PHASE_ROWS, 6, 0:P], scalar=-1.0,
                                             in1=nm[:, 0, :].bitcast(F32), op0=ALU.mult,
                                             op1=ALU.subtract).then_inc(nm_rest.sem, 1)

                def normalize(ph):
                    g, c = divmod(ph, NC)
                    j, cs = PHASES * a + ph, slice(c * N, c * N + N)
                    dve.wait_ge(*den_rc(b, j + 1))
                    dve.tensor_tensor(oT[:, g, cs], PS[:, 0, :], lr[:, 1, :], ALU.mult).then_inc(o_raw.sem, 1)
                    dve.wait_ge(*o_raw(b, j + 1))
                    dve.tensor_scalar(oT[:, g, cs], oT[:, g, cs], v(bq, 4 + g), None, ALU.add).then_inc(o_sb.sem, 1)

                rest(0, 0)
                rest(0, 1)
                rest(1, 0)
                for n in range(PHASE_ROWS):
                    for cc in range(NC):
                        row_max(n, cc)
                    if n == 2:
                        rest(1, 1)
                neg_max(0)
                for ph in range(PHASES - 1):
                    n = NC * PHASE_ROWS * (ph + 1)
                    for kt in range(KT):
                        if kt == TURN_AT:
                            neg_max(ph + 1)
                        for k in range(HALF_ROWS[kt]):
                            if kt == 0 and k == NORM_AT and ph >= 1:
                                normalize(ph - 1)
                            row_max(*divmod(n, NC))
                            n += 1
                ph = PHASES - 1
                normalize(ph - 1)
                dve.wait_ge(*pv_ps(b, (PHASES * a + 2) * KT))
                for k in range(1, len(DVE_SUMS)):
                    i, total = key_step(a, ph, DVE_SUMS[k]), acc[:, ph % 2, :, :]
                    first = PT[:, key_step(a, ph, 0) % 3, :, :] if k == 1 else total
                    if k > 1:
                        dve.wait_ge(*sum_dve(b, dve_sums(a, k - 1)))
                    dve.wait_ge(*p_sb(b, 2 * i + 2))
                    dve.tensor_tensor(total, first, PT[:, i % 3, :, :], ALU.add).then_inc(sum_dve.sem, 1)
                normalize(ph)

            def residual(b, first, bias, between=None):
                for m in range(CT):
                    for c in range(NC):
                        n = 2 * m + c
                        cs = slice(c * N, c * N + N)
                        dve.wait_ge(*o_ps(b, first + n + 1))
                        dve.scalar_tensor_tensor(out=xr[:, m, cs], in0=PS[:, n, :], scalar=v(bias, m),
                                                 in1=xr[:, m, cs], op0=ALU.add, op1=ALU.add).then_inc(x_new.sem, 1)
                        if between is not None and n == 1:
                            between()
                        if n > 0 and first < 12:
                            stats_of_new(b, first + n - 1)
                if first < 12:
                    stats_of_new(b, first + 3)

            dve.wait_ge(*xin_here(0, 16))
            for n in range(CT * NC):
                stats(xin, n)
            group_norm(0, 0, xin)
            with dve.Fori(0, B) as b:
                block0(b)
                group_norm(b, 1, xr)
                attention(b, 0)
                residual(b, 4, "proj_b")
                group_norm(b, 2, xr)
                for m in range(CT):
                    for c in range(NC):
                        n = 2 * m + c
                        cs = slice(c * N, c * N + N)
                        dve.wait_ge(*wo_sb(b, n + 1))
                        dve.tensor_tensor(xr[:, m, cs], xr[:, m, cs], rl[:, n, :], ALU.add).then_inc(x_new.sem, 1)
                        if n > 0:
                            stats_of_new(b, 8 + n - 1)
                stats_of_new(b, 11)
                group_norm(b, 3, xr)
                chan_norm(b, 0, xg, "gamma1", "beta1")
                for t in range(CT):
                    dve.wait_ge(*(cn_xa, cn_xb)[t](b, 2))
                    dve.tensor_tensor(xr[:, t, :], xr[:, t, :], xg[:, t, :], ALU.add).then_inc(x3n.sem, 1)
                attention(b, 1)
                dve.wait_ge(*o_sb(b, 8))
                dve.wait_ge(*xin_here(b, 32))
                for n in range(CT * NC):
                    stats(xin, n)
                norm_sum(b, 4)
                chan_norm(b, 1, oT, "gamma2", "beta2")
                norm_squares(b, 4)
                dve.wait_ge(*x3n(b, 2))
                residual(b, 12, "out3_b", lambda: norm_apply(b, 4, xin))

        @block.tensor
        def _(pe):
            pe.wait_ge(loaded, NLOAD)
            pe.wait_ge(built, NBUILT)
            for s in range(3):
                pe.matmul(PS[:, s, 0:P], W8[:, s, 0, :], W8[:, s, 1, :], start=True, stop=True).then_inc(folded, 1)
            pe.wait_ge(prepared, NPREP)

            def norm_means(b, s):
                pe.wait_ge(*gn_sum(b, s + 1))
                pe.matmul(PS[:, 7, 0:2], g8[:, :], msum, start=True, stop=True).then_inc(gn_gm.sem, 1)

            def norm_variances(b, s):
                pe.wait_ge(*gn_m2(b, s + 1))
                pe.matmul(PS[:, 6, 0:2], g8[:, :], m2, start=True, stop=True).then_inc(gn_gv.sem, 1)

            def group_norm(b, s):
                norm_means(b, s)
                norm_variances(b, s)
                pe.wait_ge(*gn_xa(b, s + 1))
                pe.wait_ge(*gn_xb(b, s + 1))

            def linear(bank, w, m, X, c, done):
                for k in range(CT):
                    ins = pe.matmul(PS[:, bank, :], w[:, k, m * P:m * P + P], X[:, k, c * N:c * N + N],
                                    start=(k == 0), stop=(k == CT - 1))
                if done is not None:
                    ins.then_inc(done.sem, 1)

            def block0(b):
                for c in range(NC):
                    linear(c, w_in, 0, xg, c, xp_ps)
                for c in range(NC):
                    pe.wait_ge(*xp_sb(b, c + 1))
                    pe.matmul(PS[:, 2 + c, :], w_c1, yv[:, 0, c * N:c * N + N], start=True, stop=True).then_inc(f1_ps.sem, 1)
                pe.wait_ge(*f1_sb(b, 2))
                def coeff(ps, bank, w, done):
                    if ps < 2:
                        for c in range(NC):
                            ins = pe.matmul(PS[:, bank + c, :], w[:, ps, :], f1[:, c * N:c * N + N], start=True, stop=True)
                    else:
                        pe.matmul(PS[:, bank, 0:L2], w[:, 1, :], f23[:, 0:L2], start=True, stop=True)
                        ins = pe.matmul(PS[:, bank, L2:W3], w[:, 2, :], f23[:, L2:W3], start=True, stop=True)
                    ins.then_inc(done.sem, 1)

                coeff(0, 0, Wd, pre_ps)
                v1 = f1[:, :].rearrange("p (h i w j) -> p h i w j", i=2, w=WW // 2, j=2)
                for k in range(4):
                    ins = pe.matmul(PS[:, 4, 0:L2], w_c2[:, k, :], v1[:, :, k // 2, :, k % 2], start=(k == 0), stop=(k == 3))
                ins.then_inc(f2_ps.sem, 1)
                coeff(0, 2, w_xb, brep_ps)
                pe.wait_ge(*f2_sb(b, 1))
                v2 = f23[:, 0:L2].rearrange("p (h i w j) -> p h i w j", i=2, w=WW // 4, j=2)
                for k in range(4):
                    ins = pe.matmul(PS[:, 5, 0:L3], w_c3[:, k, :], v2[:, :, k // 2, :, k % 2], start=(k == 0), stop=(k == 3))
                ins.then_inc(f3_ps.sem, 1)
                coeff(1, 6, Wd, pre_ps)
                pe.wait_ge(*f3_sb(b, 1))
                coeff(0, 4, w_xc, crep_ps)
                pe.wait_ge(*sp_abs(b, 1))
                pe.wait_ge(*sp_pos(b, 1))
                coeff(1, 0, w_xb, brep_ps)
                pe.wait_ge(*brep_sb(b, 1))
                coeff(1, 2, w_xc, crep_ps)
                pe.wait_ge(*crep_sb(b, 1))
                coeff(2, 4, Wd, pre_ps)
                pe.wait_ge(*sp_abs(b, 2))
                pe.wait_ge(*sp_pos(b, 2))
                coeff(2, 6, w_xb, brep_ps)
                pe.wait_ge(*brep_sb(b, 2))
                coeff(2, 0, w_xc, crep_ps)

                def sum_states(q, c):
                    ps = q // 4
                    pe.wait_ge(*hC_sb(b, 4 * q + 4))
                    if q == 4:
                        pe.wait_ge(*y_sb(b, 1))
                    if q == 8:
                        pe.wait_ge(*y_sb(b, 2))
                    for j in range(4):
                        hc = work[:, 6 + (4 * q + j) % 6, :]
                        src = hc[:, c * N:c * N + N] if ps < 2 else hc[:, c * N:c * N + W3]
                        ins = pe.matmul(PS[32 * j:32 * j + 32, c, 0:N if ps < 2 else W3], ysel[:, q % 4, :], src,
                                        start=(q % 4 == 0), stop=(q % 4 == 3), skip_group_check=True)
                    if c == NC - 1:
                        ins.then_inc(y_ps.sem, 1)

                def level_means(k):
                    w, ybuf, t, mb, vb = norm_job(k)
                    pe.wait_ge(*y_sb(b, k + 1 if k < 2 else 6))
                    for c in range((w + N - 1) // N):
                        wc = min(N, w - c * N)
                        ins = pe.matmul(PS[:, mb + c, 0:wc], mean128[:, :], ybuf[:, c * N:c * N + wc], start=True, stop=True)
                    ins.then_inc(lm_ps.sem, 1)

                def level_variances(k):
                    w, ybuf, t, mb, vb = norm_job(k)
                    pe.wait_ge(*lm_sq(b, k + 1))
                    for c in range((w + N - 1) // N):
                        wc = min(N, w - c * N)
                        ins = pe.matmul(PS[:, vb + c, 0:wc], mean128[:, :], t[:, c * N:c * N + wc], start=True, stop=True)
                    ins.then_inc(lv_ps.sem, 1)

                pe.wait_ge(*crep_sb(b, 2))
                for c in range(NC):
                    linear(2 + c, w_in, 1, xg, c, z_ps)
                pe.wait_ge(*crep_sb(b, 3))
                pe.wait_ge(*z_sb(b, 1))
                for n in range(3 * SG):
                    ps, at, w = n // SG, PASS_AT[n // SG], PASS_W[n // SG]
                    g = scan_group(n)
                    if n % SG == 0:
                        pe.wait_ge(*rests_in(b, (2, 4, 8)[ps]))
                        pe.wait_ge(*rests_pool(b, (2, 4, 4)[ps]))
                    for kind, (stk, done) in enumerate(((ustk, u_ps), (dstk, d_ps))):
                        job = 2 * n + kind
                        slot = 2 + 2 * (job % 3)
                        if job >= 3:
                            prev = job - 3
                            if prev % 2 == 1:
                                pe.wait_ge(*dA_sb(b, decays(prev // 2)))
                            else:
                                pe.wait_ge(*dBx_sb(b, prev // 2 + 1))
                        for c in range((w + N - 1) // N):
                            wc = min(N, w - c * N)
                            ins = pe.matmul(PS[:, slot + c, 0:wc], sel[:, g % 8, :], stk[:, g // 8, at + c * N:at + c * N + wc],
                                            start=True, stop=True)
                        ins.then_inc(done.sem, 1)
                    for k in range(2):
                        if n == SG * (k + 1) + MEAN_AT:
                            level_means(k)
                        if n == SG * (k + 1) + VAR_AT:
                            level_variances(k)
                    for q in range(12):
                        if n == sum_at(q):
                            if q in (4, 8):
                                pe.wait_ge(*lv_ln(b, q // 4))
                            sum_states(q, 0)
                        if n == sum_at(q) + 1:
                            sum_states(q, 1)
                for q in range(12):
                    for c in range(NC):
                        if sum_at(q) + c >= 3 * SG:
                            sum_states(q, c)
                for k in (2, 3):
                    level_means(k)
                for k in (2, 3):
                    level_variances(k)
                pe.wait_ge(*gated(b, 1))
                for m in range(CT):
                    for c in range(NC):
                        pe.matmul(PS[:, 2 * m + c, :], w_out[:, m * P:m * P + P], work[:, 11, c * N:c * N + N],
                                  start=True, stop=True).then_inc(o_ps.sem, 1)

            def chan_norm(b, s, X):
                for c in range(NC):
                    for t in range(CT):
                        ins = pe.matmul(PS[:, c, :], mean256[:, :], X[:, t, c * N:c * N + N], start=(t == 0), stop=(t == CT - 1))
                    ins.then_inc(cm_ps.sem, 1)
                for c in range(NC):
                    n = NC * s + c
                    pe.wait_ge(*cm_sq(b, 2 * n + 2))
                    for t in range(CT):
                        ins = pe.matmul(PS[:, 2 + c, :], mean256[:, :], sq[:, 2 * c + t, :], start=(t == 0), stop=(t == CT - 1))
                    ins.then_inc(cv_ps.sem, 1)

            def attention(b, a, X):
                wq, kd = w_qkv[a], 96

                def project_qk(g, kind, c):
                    linear(2 * kind + c, wq, 2 * kind + g, X, c, qk_ps if c == NC - 1 else None)

                def project_v(tt):
                    for k in range(CT):
                        ins = pe.matmul(PS[:, tt // 2, (tt % 2) * C:(tt % 2) * C + C], X[:, k, tt * P:tt * P + P],
                                        wq[:, k, 2 * C:3 * C], start=(k == 0), stop=(k == CT - 1))
                    if tt % 4 == 3:
                        ins.then_inc(v_ps.sem, 1)

                def row_scores(n, cc):
                    ph, j, q = n // PHASE_ROWS, n % PHASE_ROWS // 4, n % 4
                    g, c = divmod(ph, NC)
                    h = GH * g + j
                    if c == 0 and q == 0 and cc == 0:
                        pe.wait_ge(*stackedq[g][j](b, (a + 1) * 48))
                        pe.wait_ge(*stackedk[g][j](b, (a + 1) * 48))
                    ahead = 2 if ph == 0 else 1
                    if n % PHASE_ROWS >= ahead:
                        pe.wait_ge(*r_max(b, halves(a, n - ahead, cc) + 1))
                    pe.matmul(PS[:, row_slot(n, cc), :], QS[0:kd, c, h, q * P:q * P + P], KS[0:kd, h, cc * N:cc * N + N],
                              start=True, stop=True).then_inc(r_ps.sem, 1)

                def turn_max(ph):
                    pe.wait_ge(*m_both(b, a * PHASES + ph + 1))
                    pe.transpose(PS[0:PHASE_ROWS, 6, 0:P], mboth[:, :], ident[:, :]).then_inc(mt_ps.sem, 1)

                for kind in range(2):
                    for c in range(NC):
                        if a == 1 and kind == 0:
                            chunk_ready(b, c)
                        project_qk(0, kind, c)
                pe.wait_ge(*qk_rest(b, 4 * a + 1))
                for c in range(NC):
                    project_qk(1, 0, c)
                for n in range(PHASE_ROWS):
                    for cc in range(NC):
                        row_scores(n, cc)
                    if n < NC:
                        if n == 0:
                            pe.wait_ge(*qk_rest(b, 4 * a + 2))
                        project_qk(1, 1, n)
                    elif n < NC + KT:
                        if n - NC in (0, 4):
                            pe.wait_ge(*qk_rest(b, 4 * a + 3 + (n - NC) // 4))
                        project_v(n - NC)
                turn_max(0)
                pe.wait_ge(*v_sb(b, 2 * a + 2))
                pe.wait_ge(*ones_in(b, 1))

                def values(i, between, turn=None):
                    ph, kt = divmod(i % (PHASES * KT), KT)
                    g = ph // NC
                    sums = POOL_SUMS if ph < PHASES - 1 else DVE_SUMS
                    direct = [k for k in range(KT) if k not in sums]
                    pe.wait_ge(*p_sb(b, 2 * i + 2))
                    if kt == 0 and ph > 0:
                        pe.wait_ge(*o_raw(b, i // KT))
                    for j in range(GH):
                        h = GH * g + j
                        ins = pe.matmul(PS[32 * j:32 * j + 32, 0, :], Vt[:, kt, DH * h:DH * h + DH], PT[:, i % 3, j, :],
                                        start=(kt == 0), stop=(kt == KT - 1), skip_group_check=True)
                    if kt not in direct:
                        ins.then_inc(pv_ps.sem, 1)
                    between(1 if kt in direct else 2)
                    if turn is not None:
                        turn_max(turn)
                    if kt in direct:
                        for j in range(GH):
                            ins = pe.matmul(PS[32 * j:32 * j + 32, 1, :], ones32[:, :], PT[:, i % 3, j, :],
                                            start=(kt == direct[0]), stop=False, skip_group_check=True)
                        if kt == KT - 1:
                            between(1)
                            if ph < PHASES - 1:
                                pe.wait_ge(*sum_pool(b, pool_sums(a, ph, len(POOL_SUMS) - 1)))
                            else:
                                pe.wait_ge(*sum_dve(b, dve_sums(a, len(DVE_SUMS) - 1)))
                            for j in range(GH):
                                ins = pe.matmul(PS[32 * j:32 * j + 32, 1, :], ones32[:, :], acc[:, ph % 2, j, :],
                                                start=False, stop=True, skip_group_check=True)
                        ins.then_inc(pv_ps.sem, 1)

                for ph in range(PHASES):
                    g, c = divmod(ph, NC)
                    row = [NC * PHASE_ROWS * (ph + 1), 0]

                    def next_rows(most):
                        for _ in range(min(most, row[1]) if ph < PHASES - 1 else 0):
                            if row[0] % (NC * PHASE_ROWS) == 0:
                                pe.wait_ge(*nm_rest(b, PHASES * a + ph + 1))
                            row_scores(*divmod(row[0], NC))
                            row[0], row[1] = row[0] + 1, row[1] - 1

                    for kt in range(KT):
                        i = key_step(a, ph, kt)
                        row[1] = HALF_ROWS[kt]
                        if kt == 0:
                            if ph > 0:
                                values(i - 1, next_rows)
                            else:
                                next_rows(NC)
                            pe.wait_ge(*nm_in(b, 32 * (PHASES * a + ph + 1)))
                        for pr in range(2):
                            if ph + kt > 0:
                                pe.wait_ge(*p_sb(b, 2 * i - 2 + pr + 1))
                            for jj in range(2):
                                h = GH * g + 2 * pr + jj
                                ins = pe.matmul(PS[:, 2 + 2 * pr + jj, :], KS[:, h, kt * P:kt * P + P], QS[:, c, h, :],
                                                start=True, stop=True)
                            ins.then_inc(s_ps.sem, 1)
                            next_rows(1)
                        if kt > 0:
                            values(i - 1, next_rows, ph + 1 if kt == TURN_AT and ph < PHASES - 1 else None)
                        next_rows(row[1])
                values(key_step(a, PHASES - 1, KT - 1), lambda most: None)

            def chunk_ready(b, n):
                pe.wait_ge(*cn_xa(b, n + 1))
                pe.wait_ge(*cn_xb(b, n + 1))

            def project(b, a, X, between=None):
                for m in range(CT):
                    for c in range(NC):
                        if a == 1 and m == 0:
                            chunk_ready(b, NC + c)
                        if between is not None and m == 0 and c == 1:
                            between()
                        if m == 0 and c == 0:
                            pe.wait_ge(*o_raw(b, 4 * a + 4))
                        linear(2 * m + c, w_proj[a], m, X, c, o_ps)

            def block2(b):
                for t in range(2):
                    for c in range(NC):
                        n = 2 * t + c
                        top = c * (HH // NC)
                        for hh, (ky, kx), (y0, y1, x0, x1), first, last in windows(t, c):
                            dy, dx = (ky - 1) * RATES[2 * t + hh], (kx - 1) * RATES[2 * t + hh]
                            dst = PS[64 * hh:64 * hh + 64, n, :].rearrange("p (h w) -> p h w", w=WW)[:, y0 - top:y1 - top, x0:x1]
                            src = xg[:, t, :].rearrange("p (h w) -> p h w", w=WW)[:, y0 + dy:y1 + dy, x0 + dx:x1 + dx]
                            ins = pe.matmul(dst, DW[:, t, ky * 3 + kx, 64 * hh:64 * hh + 64], src,
                                            start=first, stop=last, skip_group_check=True)
                        ins.then_inc(dw_ps.sem, 1)
                for m in range(2):
                    for c in range(NC):
                        pe.wait_ge(*dw_sb(b, 4))
                        linear(4 + 2 * m + c, MX, m, br, c, mix_ps)
                for m in range(2):
                    for c in range(NC):
                        pe.wait_ge(*mix_sb(b, 4))
                        linear(2 * m + c, w_o, m, zm, c, o_ps)

            group_norm(0, 0)
            with pe.Fori(0, B) as b:
                block0(b)
                group_norm(b, 1)
                attention(b, 0, xg)
                pe.wait_ge(*o_sb(b, 4))
                project(b, 0, oT)
                group_norm(b, 2)
                block2(b)
                group_norm(b, 3)
                chan_norm(b, 0, xg)
                attention(b, 1, xg)
                pe.wait_ge(*o_sb(b, 8))
                chan_norm(b, 1, oT)
                norm_means(b, 4)
                project(b, 1, oT, lambda: norm_variances(b, 4))
                pe.wait_ge(*gn_xa(b, 5))
                pe.wait_ge(*gn_xb(b, 5))
                pe.wait_ge(*x_new(b, 16))


def row_slot(n, cc):
    return (4 + 2 * (n % 2) if n < PHASE_ROWS else 6) + cc


def halves(a, n, cc):
    return (a * PHASES * PHASE_ROWS + n) * NC + cc


def key_step(a, ph, kt):
    return (PHASES * a + ph) * KT + kt


def pool_sums(a, ph, k):
    return ((PHASES - 1) * a + ph) * (len(POOL_SUMS) - 1) + k


def dve_sums(a, k):
    return (len(DVE_SUMS) - 1) * a + k


def summed(a, ph, kt):
    sums = POOL_SUMS if ph < PHASES - 1 else DVE_SUMS
    if kt not in sums:
        return None
    k = max(1, sums.index(kt))
    return (0, pool_sums(a, ph, k)) if ph < PHASES - 1 else (1, dve_sums(a, k))


def scan_group(n):
    i, j = (n % SG) // 4, n % 4
    return 4 * j + i


def sum_at(q):
    return 4 * q + (SUM_AFTER_NORM if q in (4, 8) else SUM_LATE)


def scans(n):
    return n + 1 if n < 32 else 32 + 4 * (n - 32) + 4


def decays(n):
    return n + 1 if n < 32 else 32 + 2 * (n - 32) + 2


def windows(t, c):
    top, todo = c * (HH // NC), []
    for ky, kx in TAPS:
        for hh in range(2):
            dy, dx = (ky - 1) * RATES[2 * t + hh], (kx - 1) * RATES[2 * t + hh]
            y0, y1 = max(top, -dy), min(top + HH // NC, HH - dy)
            x0, x1 = max(0, -dx), min(WW, WW - dx)
            if y0 < y1 and x0 < x1:
                todo.append((hh, (ky, kx), (y0, y1, x0, x1)))
    ends = {hh: max(i for i, w in enumerate(todo) if w[0] == hh) for hh in range(2)}
    return [(*w, w[1] == (1, 1), i == ends[w[0]]) for i, w in enumerate(todo)]


def kernel(**inputs):
    import numpy as np
    import concourse.bacc as bacc
    from concourse.bass_utils import run_bass_kernel_spmd

    a = {k: np.asarray(t) for k, t in inputs.items()}
    two = lambda t: t.reshape(2, P, -1).transpose(1, 0, 2)
    col = lambda t: np.ascontiguousarray(t.reshape(-1, P).T)
    z0, z1, z2, z3 = (lambda n, i=i: a[f"L{i}_conv_{n}"] for i in range(4))

    taps = lambda w: w.transpose(1, 2, 3, 0).reshape(P, 4 * P)
    part = {
        "in_w": two(z0("in_w").T), "c1": z0("c1_w").T, "c2": taps(z0("c2_w")), "c3": taps(z0("c3_w")),
        "xb": np.concatenate([np.tile(z0(f"xw{s}")[R_DT:R_DT + NST].T, (1, DPG)) for s in (1, 2, 3)], 1),
        "xc": np.concatenate([np.tile(z0(f"xw{s}")[R_DT + NST:].T, (1, DPG)) for s in (1, 2, 3)], 1),
        "out": z0("out_w").T,
        "qkv1": two(z1("qkv_w").T), "proj1": two(z1("proj_w").T),
        "wo": two(z2("wo")[:, :, 0, 0].reshape(C, C // 4, 4).transpose(2, 1, 0).reshape(C, C)),
        "qkv3": two(z3("w_qkv")), "out3": two(z3("w_out")),
    }
    wpack = np.ascontiguousarray(np.concatenate([part[n].reshape(P, w) for n, w in WSEC], 1))

    def bn(n_dw, n_s, n_o):
        return np.concatenate([col(z2(n_dw).reshape(-1)), col(np.repeat(z2(n_s), C // 4)), col(z2(n_o))], 1)

    ws = z2("ws")[:, :, 0, 0]
    vec = {
        "in_b": col(z0("in_b")), "c1_b": col(z0("c1_b")), "c2_b": col(z0("c2_b")), "c3_b": col(z0("c3_b")),
        "out_b": col(z0("out_b")),
        "dtb": np.stack([z0(f"dtb{s}") for s in (1, 2, 3)], 1), "Dv": np.stack([z0(f"Dv{s}") for s in (1, 2, 3)], 1),
        "g": np.stack([z0(f"g{s}") for s in (1, 2, 3)], 1), "be": np.stack([z0(f"be{s}") for s in (1, 2, 3)], 1),
        "Al": np.concatenate([z0(f"Al{s}").reshape(SG, P).T for s in (1, 2, 3)], 1),
        "qkv_b1": col(z1("qkv_b")), "proj_b": col(z1("proj_b")),
        "bn_b": bn("bdw", "bs", "bo"), "bn_g": bn("gdw", "gs", "go"), "bn_be": bn("bedw", "bes", "beo"),
        "bn_m": bn("mdw", "ms", "mo"), "bn_v": bn("vdw", "vs", "vo"),
        "wdw": z2("wdw").reshape(2, P, 9).transpose(1, 0, 2),
        "ws": np.repeat(ws.T.reshape(2, 2, 4).transpose(1, 0, 2), C // 4, 0),
        "qkv_b3": col(z3("b_qkv")), "out3_b": col(z3("b_out")), "gamma1": col(z3("gamma1")),
        "beta1": col(z3("beta1")), "gamma2": col(z3("gamma2")), "beta2": col(z3("beta2")),
    }
    vpack = np.ascontiguousarray(np.concatenate([vec[n].reshape(P, w) for n, w in VSEC], 1))
    w8 = np.ascontiguousarray(np.stack([np.stack([z0(f"xw{s}")[:R_DT], z0(f"dtw{s}").T], 1) for s in (1, 2, 3)], 1))

    arrays = {"x": np.ascontiguousarray(a["x"].reshape(B, C, L)), "wpack": wpack, "vpack": vpack, "w8": w8}
    nc = bacc.Bacc("TRN2", target_bir_lowering=False, num_devices=1)
    args = [nc.dram_tensor(n, t.shape, F32, kind="ExternalInput").ap() for n, t in arrays.items()]
    out = nc.dram_tensor("out", (B, C, L), F32, kind="ExternalOutput").ap()
    build(nc, *args, out)
    r = run_bass_kernel_spmd(nc, [arrays], core_ids=[0])
    return r.results[0]["out"].reshape(B, C, HH, WW)
```
